# Optimizing a Trainium2 kernel written in Bass

```python
import numpy as np
import jax
import jax.numpy as jnp

def _softmax(x, axis=-1):
    return jax.nn.softmax(x, axis=axis)

def _gelu(x):
    return jax.nn.gelu(x, approximate=True)

def _silu(x):
    return jax.nn.silu(x)

def _sigmoid(x):
    return jax.nn.sigmoid(x)

def _layernorm(x, axis=-1, eps=1e-05):
    m = jnp.mean(x, axis=axis, keepdims=True)
    v = jnp.var(x, axis=axis, keepdims=True)
    return (x - m) / jnp.sqrt(v + eps)

def _scatter_add(tgt, idx, src, axis=0):
    return tgt.at[idx].add(src)

def _segment_sum(src, seg, n):
    return jax.ops.segment_sum(src, seg, n)
kernel_name = 'mk_macaron_d2_jaxref_r8_be6ae6'

def setup_inputs(seed: int=0):
    np.random.seed(seed)
    _w = jnp.asarray

    def _L0_attn_setup():
        import jax, jax.numpy as jnp
        import numpy as np
        KEY_DIM = 128
        SCALE = KEY_DIM ** (-0.5)
        key = jax.random.key(seed)
        k1, k2, k3, k4 = jax.random.split(key, 4)
        B, S, E = (4, 256, 128)
        x = jax.random.normal(k1, (B, S, E), dtype=jnp.float32)
        WQ = jax.random.normal(k2, (KEY_DIM, E), dtype=jnp.float32) * E ** (-0.5)
        WK = jax.random.normal(k3, (KEY_DIM, E), dtype=jnp.float32) * E ** (-0.5)
        WV = jax.random.normal(k4, (KEY_DIM, E), dtype=jnp.float32) * E ** (-0.5)
        return {'x': x, 'WQ': WQ, 'WK': WK, 'WV': WV}
    _L0_attn_in = _L0_attn_setup()

    def _L0_ffn_setup():
        import jax, jax.numpy as jnp
        import numpy as np
        E = 8
        K = 2
        CF = 1.2
        D = 128
        F = 512
        B, S = (4, 128)
        key = jax.random.key(seed)
        ks = jax.random.split(key, 4)

        def init(k, shape, fan_in):
            return jax.random.normal(k, shape, jnp.float32) * (1.0 / np.sqrt(fan_in))
        return {'x': jax.random.normal(ks[0], (B, S, D), jnp.float32), 'Wg': init(ks[1], (D, E), D), 'bg': jnp.zeros((E,), jnp.float32), 'W1': init(ks[2], (E, D, F), D), 'b1': jnp.zeros((E, F), jnp.float32), 'W2': init(ks[3], (E, F, D), F), 'b2': jnp.zeros((E, D), jnp.float32)}
    _L0_ffn_in = _L0_ffn_setup()

    def _L1_attn_setup():
        import jax, jax.numpy as jnp
        import numpy as np
        DT_RANK = 64
        D_STATE = 16

        def _dwconv_silu(x, w, b, dil):
            k = w.shape[-1]
            out = jax.lax.conv_general_dilated(x, w[:, None, :], window_strides=(1,), padding=[(dil * (k - 1), 0)], rhs_dilation=(dil,), dimension_numbers=('NCH', 'OIH', 'NCH'), feature_group_count=x.shape[1])
            return jax.nn.silu(out + b[None, :, None])
        key = jax.random.key(seed)
        ks = jax.random.split(key, 12)
        b, l, d_model, d_inner = (4, 256, 128, 256)
        s = lambda fan: 1.0 / np.sqrt(fan)
        inp = {'hidden_states': jax.random.normal(ks[0], (b, l, d_model), jnp.float32), 'W_in': jax.random.normal(ks[1], (2 * d_inner, d_model), jnp.float32) * s(d_model), 'conv_w1': jax.random.normal(ks[2], (d_inner, 4), jnp.float32) * 0.5, 'conv_b1': jax.random.normal(ks[3], (d_inner,), jnp.float32) * 0.1, 'conv_w2': jax.random.normal(ks[4], (d_inner, 4), jnp.float32) * 0.5, 'conv_b2': jax.random.normal(ks[5], (d_inner,), jnp.float32) * 0.1, 'conv_gates': jnp.ones((2,), jnp.float32), 'W_x': jax.random.normal(ks[6], (DT_RANK + 2 * D_STATE, d_inner), jnp.float32) * s(d_inner), 'W_dt': jax.random.normal(ks[7], (d_inner, DT_RANK), jnp.float32) * s(DT_RANK), 'b_dt': jax.random.normal(ks[8], (d_inner,), jnp.float32) - 4.0, 'A_log': jnp.log(1.0 + 15.0 * jax.random.uniform(ks[9], (d_inner, D_STATE), jnp.float32)), 'D_param': jnp.ones((d_inner,), jnp.float32), 'W_out': jax.random.normal(ks[10], (d_model, d_inner), jnp.float32) * s(d_inner)}
        return inp
    _L1_attn_in = _L1_attn_setup()

    def _L1_ffn_setup():
        import jax, jax.numpy as jnp
        import numpy as np
        B, L, D, H, E, TOP_K = (4, 256, 128, 512, 8, 2)
        LN_EPS = 1e-05
        key = jax.random.key(seed)
        ks = jax.random.split(key, 8)
        x = jax.random.normal(ks[0], (B, L, D), dtype=jnp.float32)
        gate_w = jax.random.normal(ks[1], (D, E), dtype=jnp.float32) / np.sqrt(D)
        w1 = jax.random.normal(ks[2], (E, D, H), dtype=jnp.float32) / np.sqrt(D)
        b1 = jnp.zeros((E, H), dtype=jnp.float32)
        w2 = jax.random.normal(ks[3], (E, H, D), dtype=jnp.float32) / np.sqrt(H)
        b2 = jnp.zeros((E, D), dtype=jnp.float32)
        gamma = jnp.ones((D,), dtype=jnp.float32)
        beta = jnp.zeros((D,), dtype=jnp.float32)
        return {'x': x, 'gate_w': gate_w, 'w1': w1, 'b1': b1, 'w2': w2, 'b2': b2, 'gamma': gamma, 'beta': beta}
    _L1_ffn_in = _L1_ffn_setup()
    _d = {'L0_attn_x': _L0_attn_in['x'], 'L0_attn_WQ': _L0_attn_in['WQ'], 'L0_attn_WK': _L0_attn_in['WK'], 'L0_attn_WV': _L0_attn_in['WV'], 'L0_ffn_Wg': _L0_ffn_in['Wg'], 'L0_ffn_bg': _L0_ffn_in['bg'], 'L0_ffn_W1': _L0_ffn_in['W1'], 'L0_ffn_b1': _L0_ffn_in['b1'], 'L0_ffn_W2': _L0_ffn_in['W2'], 'L0_ffn_b2': _L0_ffn_in['b2'], 'L1_attn_W_in': _L1_attn_in['W_in'], 'L1_attn_conv_w1': _L1_attn_in['conv_w1'], 'L1_attn_conv_b1': _L1_attn_in['conv_b1'], 'L1_attn_conv_w2': _L1_attn_in['conv_w2'], 'L1_attn_conv_b2': _L1_attn_in['conv_b2'], 'L1_attn_conv_gates': _L1_attn_in['conv_gates'], 'L1_attn_W_x': _L1_attn_in['W_x'], 'L1_attn_W_dt': _L1_attn_in['W_dt'], 'L1_attn_b_dt': _L1_attn_in['b_dt'], 'L1_attn_A_log': _L1_attn_in['A_log'], 'L1_attn_D_param': _L1_attn_in['D_param'], 'L1_attn_W_out': _L1_attn_in['W_out'], 'L1_ffn_gate_w': _L1_ffn_in['gate_w'], 'L1_ffn_w1': _L1_ffn_in['w1'], 'L1_ffn_b1': _L1_ffn_in['b1'], 'L1_ffn_w2': _L1_ffn_in['w2'], 'L1_ffn_b2': _L1_ffn_in['b2'], 'L1_ffn_gamma': _L1_ffn_in['gamma'], 'L1_ffn_beta': _L1_ffn_in['beta']}
    _x0 = _d['L0_attn_x']
    _d['L0_attn_x'] = jax.random.normal(jax.random.fold_in(jax.random.key(seed), 1), (16, 512, 128), dtype=_x0.dtype)
    del _x0
    return _d

def reference(L0_attn_x, L0_attn_WQ, L0_attn_WK, L0_attn_WV, L0_ffn_Wg, L0_ffn_bg, L0_ffn_W1, L0_ffn_b1, L0_ffn_W2, L0_ffn_b2, L1_attn_W_in, L1_attn_conv_w1, L1_attn_conv_b1, L1_attn_conv_w2, L1_attn_conv_b2, L1_attn_conv_gates, L1_attn_W_x, L1_attn_W_dt, L1_attn_b_dt, L1_attn_A_log, L1_attn_D_param, L1_attn_W_out, L1_ffn_gate_w, L1_ffn_w1, L1_ffn_b1, L1_ffn_w2, L1_ffn_b2, L1_ffn_gamma, L1_ffn_beta):

    def _L0_attn_ref(x, WQ, WK, WV):
        import jax, jax.numpy as jnp
        import numpy as np
        KEY_DIM = 128
        SCALE = KEY_DIM ** (-0.5)
        q = jnp.einsum('bse,ke->bsk', x, WQ)
        k = jnp.einsum('bse,ke->bsk', x, WK)
        v = jnp.einsum('bse,ve->bsv', x, WV)
        scores = jnp.einsum('bsk,btk->bst', q, k) * SCALE
        masked = jnp.where(jnp.tril(scores) == 0, -jnp.inf, scores)
        attn = jax.nn.softmax(masked, axis=-1)
        return jnp.einsum('bst,btv->bsv', attn, v)

    def _L0_ffn_ref(x, Wg, bg, W1, b1, W2, b2):
        import jax, jax.numpy as jnp
        import numpy as np
        E = 8
        K = 2
        CF = 1.2
        D = 128
        F = 512
        B, S = (4, 128)
        Bx, Sx, Dx = x.shape
        T = Bx * Sx
        xt = x.reshape(T, Dx)
        logits = xt @ Wg + bg
        probs = jax.nn.softmax(logits, axis=-1)
        gate_vals, exp_idx = jax.lax.top_k(probs, K)
        gate_vals = gate_vals / jnp.sum(gate_vals, axis=-1, keepdims=True)
        capacity = int(np.ceil(CF * T * K / E))
        eidx = exp_idx.T.reshape(-1)
        gv = gate_vals.T.reshape(-1)
        oh = jax.nn.one_hot(eidx, E, dtype=jnp.int32)
        pos = jnp.sum((jnp.cumsum(oh, axis=0) - oh) * oh, axis=-1)
        keep = pos < capacity
        pos_c = jnp.where(keep, pos, capacity)
        xk = jnp.tile(xt, (K, 1))
        buf = jnp.zeros((E, capacity + 1, Dx), x.dtype)
        buf = buf.at[eidx, pos_c].add(jnp.where(keep[:, None], xk, 0.0))
        buf = buf[:, :capacity]
        h = jax.nn.gelu(jnp.einsum('ecd,edf->ecf', buf, W1) + b1[:, None, :], approximate=True)
        ye = jnp.einsum('ecf,efd->ecd', h, W2) + b2[:, None, :]
        ye = jnp.concatenate([ye, jnp.zeros((E, 1, Dx), ye.dtype)], axis=1)
        gathered = ye[eidx, pos_c] * (gv * keep.astype(gv.dtype))[:, None]
        out = jnp.sum(gathered.reshape(K, T, Dx), axis=0)
        return out.reshape(Bx, Sx, Dx)

    def _L1_attn_ref(hidden_states, W_in, conv_w1, conv_b1, conv_w2, conv_b2, conv_gates, W_x, W_dt, b_dt, A_log, D_param, W_out):
        import jax, jax.numpy as jnp
        import numpy as np
        DT_RANK = 64
        D_STATE = 16

        def _dwconv_silu(x, w, b, dil):
            k = w.shape[-1]
            out = jax.lax.conv_general_dilated(x, w[:, None, :], window_strides=(1,), padding=[(dil * (k - 1), 0)], rhs_dilation=(dil,), dimension_numbers=('NCH', 'OIH', 'NCH'), feature_group_count=x.shape[1])
            return jax.nn.silu(out + b[None, :, None])
        b, l, d_model = hidden_states.shape
        d_inner = W_in.shape[0] // 2
        xz = jnp.einsum('bld,ed->bel', hidden_states, W_in)
        x, z = (xz[:, :d_inner], xz[:, d_inner:])
        x1 = _dwconv_silu(x, conv_w1, conv_b1, 1)
        x2 = _dwconv_silu(x, conv_w2, conv_b2, 2)
        gate = jax.nn.softmax(conv_gates)
        xc = gate[0] * x1 + gate[1] * x2
        xT = jnp.swapaxes(xc, 1, 2)
        x_dbl = jnp.einsum('bld,ed->ble', xT, W_x)
        dt_low = x_dbl[..., :DT_RANK]
        B = x_dbl[..., DT_RANK:DT_RANK + D_STATE]
        C = x_dbl[..., DT_RANK + D_STATE:]
        dt = jnp.einsum('blr,dr->bld', dt_low, W_dt)
        delta = jax.nn.softplus(dt + b_dt)
        A = -jnp.exp(A_log)

        def step(h, inp):
            dlt_t, B_t, C_t, x_t = inp
            dA = jnp.exp(dlt_t[:, :, None] * A)
            h = h * dA + dlt_t[:, :, None] * B_t[:, None, :] * x_t[:, :, None]
            y_t = jnp.einsum('bdn,bn->bd', h, C_t)
            return (h, y_t)
        h0 = jnp.zeros((b, d_inner, D_STATE), xT.dtype)
        seq = (jnp.swapaxes(delta, 0, 1), jnp.swapaxes(B, 0, 1), jnp.swapaxes(C, 0, 1), jnp.swapaxes(xT, 0, 1))
        _, ys = jax.lax.scan(step, h0, seq)
        y = jnp.swapaxes(ys, 0, 1)
        y = y + D_param * xT
        y = y * jax.nn.silu(jnp.swapaxes(z, 1, 2))
        return jnp.einsum('bld,od->blo', y, W_out)

    def _L1_ffn_ref(x, gate_w, w1, b1, w2, b2, gamma, beta):
        import jax, jax.numpy as jnp
        import numpy as np
        B, L, D, H, E, TOP_K = (4, 256, 128, 512, 8, 2)
        LN_EPS = 1e-05
        residual = x
        mu = jnp.mean(x, axis=-1, keepdims=True)
        var = jnp.mean(jnp.square(x - mu), axis=-1, keepdims=True)
        xn = (x - mu) * jax.lax.rsqrt(var + LN_EPS) * gamma + beta
        probs = jax.nn.softmax(jnp.einsum('bld,de->ble', xn, gate_w), axis=-1)
        w, idx = jax.lax.top_k(probs, TOP_K)
        w = w / jnp.sum(w, axis=-1, keepdims=True)
        cw = jnp.sum(w[..., None] * jax.nn.one_hot(idx, E, dtype=x.dtype), axis=2)
        h = jax.nn.gelu(jnp.einsum('bld,edh->eblh', xn, w1) + b1[:, None, None, :], approximate=False)
        out_e = jnp.einsum('eblh,ehd->ebld', h, w2) + b2[:, None, None, :]
        output = jnp.einsum('ble,ebld->bld', cw, out_e)
        return output + residual
    x = L0_attn_x
    x = x + 0.5 * _L0_ffn_ref(_layernorm(x, axis=-1), L0_ffn_Wg, L0_ffn_bg, L0_ffn_W1, L0_ffn_b1, L0_ffn_W2, L0_ffn_b2)
    x = x + _L0_attn_ref(_layernorm(x, axis=-1), L0_attn_WQ, L0_attn_WK, L0_attn_WV)
    x = x + 0.5 * _L0_ffn_ref(_layernorm(x, axis=-1), L0_ffn_Wg, L0_ffn_bg, L0_ffn_W1, L0_ffn_b1, L0_ffn_W2, L0_ffn_b2)
    x = x + 0.5 * _L1_ffn_ref(_layernorm(x, axis=-1), L1_ffn_gate_w, L1_ffn_w1, L1_ffn_b1, L1_ffn_w2, L1_ffn_b2, L1_ffn_gamma, L1_ffn_beta)
    x = x + _L1_attn_ref(_layernorm(x, axis=-1), L1_attn_W_in, L1_attn_conv_w1, L1_attn_conv_b1, L1_attn_conv_w2, L1_attn_conv_b2, L1_attn_conv_gates, L1_attn_W_x, L1_attn_W_dt, L1_attn_b_dt, L1_attn_A_log, L1_attn_D_param, L1_attn_W_out)
    x = x + 0.5 * _L1_ffn_ref(_layernorm(x, axis=-1), L1_ffn_gate_w, L1_ffn_w1, L1_ffn_b1, L1_ffn_w2, L1_ffn_b2, L1_ffn_gamma, L1_ffn_beta)
    return x

_drawn_inputs = setup_inputs


def setup_inputs(seed=0):
    import zlib

    import numpy as np

    out = dict(_drawn_inputs(seed))
    spreads = {'L0_ffn_bg': (0.0, 0.1),
     'L0_ffn_b1': (0.0, 0.1),
     'L0_ffn_b2': (0.0, 0.1),
     'L1_attn_conv_gates': (1.0, 0.6),
     'L1_attn_D_param': (1.0, 0.2),
     'L1_ffn_b1': (0.0, 0.3),
     'L1_ffn_b2': (0.0, 0.1),
     'L1_ffn_gamma': (1.0, 0.2),
     'L1_ffn_beta': (0.0, 0.1)}
    factors = {'L1_attn_conv_b1': 4.523,
     'L1_attn_conv_b2': 4.39,
     'L1_attn_W_x': 3.485,
     'L1_attn_W_dt': 8.0,
     'L1_attn_b_dt': 6.131,
     'L1_attn_A_log': 6.323}
    for name, (base, spread) in spreads.items():
        noise = np.random.default_rng([zlib.crc32(name.encode()), seed]).standard_normal(out[name].shape)
        drawn = base * np.exp(spread * noise) if base else spread * noise
        out[name] = jnp.asarray(drawn.astype(out[name].dtype))
    for name, factor in factors.items():
        out[name] = (out[name] * factor).astype(out[name].dtype)
    return out
```

```python
import concourse.bass as bass
from concourse import mybir
from contextlib import ExitStack

F32 = mybir.dt.float32
BF16 = mybir.dt.bfloat16
I32 = mybir.dt.int32
U32 = mybir.dt.uint32
ALU = mybir.AluOpType
ACT = mybir.ActivationFunctionType
AX = mybir.AxisListType

P = 128
BATCH, SEQ, D = 16, 512, 128
TOKENS = BATCH * SEQ
TILES = TOKENS // P
SEQ_TILES = SEQ // P
GROUPS = TILES // 4
EXPERTS, TOPK, HIDDEN = 8, 2, 512
FT = HIDDEN // P
BLOCK = 512
CAPACITY = -(-12 * TOKENS * TOPK // (10 * EXPERTS))
NBLK = TOKENS * TOPK // BLOCK + EXPERTS
REGION = 2 * TOKENS + BLOCK
DUMP = EXPERTS * REGION
TRASH = NBLK * BLOCK
SIGN = EXPERTS
BASE = SIGN + TOPK * EXPERTS
MIDDLE = BASE + TOPK * EXPERTS
EIGHT = MIDDLE + EXPERTS
NUMBER = EIGHT + EXPERTS
SMALL = NUMBER + NBLK
PACK = HIDDEN + FT * D + FT + 1
EPS = 1e-5
NEG = -1e30
SCALE = D ** -0.5
INNER, STATES, RANK, TAPS = 256, 16, 64, 4
DT = INNER // P
PAD = 2 * (TAPS - 1)
DVE_STATES = (5, 13)


class Chain:

    def __init__(self, eng, sem):
        self.eng, self.sem, self.n, self.base = eng, sem, 0, None

    def turn(self, i, per, turns):
        self.base, self.start, self.per, self.turns = i * per, self.n, per, turns

    def leave(self):
        assert self.n - self.start == self.per, (self.n - self.start, self.per)
        self.n = self.start + self.per * self.turns
        self.base = None

    def __call__(self, ins):
        ins.then_inc(self.sem, 1)
        self.n += 1
        self.eng.wait_ge(self.sem, self.n if self.base is None else self.base + self.n)


class Core:
    pass


class Stage:

    def __init__(self, nc, name):
        self.nc, self.name, self.ctx, self.sems = nc, name, ExitStack(), []

    def sem(self, n):
        self.sems.append(self.nc.alloc_semaphore(f"{self.name}_{n}"))
        return self.sems[-1]

    def sb(self, n, shape, dtype=F32):
        return self.ctx.enter_context(self.nc.sbuf_tensor(f"{self.name}_{n}", shape, dtype))

    def pb(self, n, shape, dtype=F32):
        return self.ctx.enter_context(self.nc.psum_tensor(f"{self.name}_{n}", shape, dtype))

    def block(self):
        return self.ctx.enter_context(self.nc.Block())

    def __enter__(self):
        return self

    def __exit__(self, *error):
        self.ctx.__exit__(*error)
        if error[0] is None:
            self.nc.clear_and_free_semaphores(self.sems)
            self.nc.all_engine_barrier()


def rows_of(x, t, n=1):
    v = x[:, bass.ds(t, n), :]
    return v.rearrange("p a d -> p (a d)") if n == 1 else v


def sequences(eng, body, chain=None, links=0):
    turns = (BATCH - 4) // 2
    for s in range(3):
        body(s, s % 2, s // 2, s == 0, False)
    with eng.Fori(0, turns) as i:
        if chain is not None:
            chain.turn(i, links, turns)
        body(i * 2 + 3, 1, i + 1, False, False)
        body(i * 2 + 4, 0, i + 2, False, False)
        if chain is not None:
            chain.leave()
    body(BATCH - 1, 1, BATCH // 2 - 1, False, True)


class Norm:

    def __init__(self, st, k, name, double=False):
        self.k, self.w = k, 2 if double else 1
        self.asked, self.logged, self.rooted, self.begun = (st.sem(f"{name}_{n}") for n in ("asked", "logged", "rooted", "begun"))
        self.stats = st.sb(f"{name}_stats", [P, 4, 6])
        self.mean, self.odd, self.var = (st.sb(f"{name}_{n}", [P, 4]) for n in ("mean", "odd", "var"))
        self.shifted, self.root, self.newton, self.rstd = (st.sb(f"{name}_{n}", [P, self.w, 4]) for n in ("shifted", "root", "newton", "rstd"))

    def dve_stats(self, nc, chain, s):
        chain.eng.sem_inc(self.begun, 1)
        st, m, o, v = self.stats, self.mean, self.odd, self.var
        for j in range(4):
            last = nc.vector.bn_stats(st[:, j, :], rows_of(self.k.X, s * 4 + j))
        chain(last)
        nc.vector.tensor_tensor(m[:, :], st[:, :, 1], st[:, :, 4], ALU.add)
        nc.vector.tensor_tensor(v[:, :], st[:, :, 2], st[:, :, 5], ALU.add)
        chain(nc.vector.tensor_tensor(o[:, :], st[:, :, 1], st[:, :, 4], ALU.subtract))
        nc.vector.tensor_scalar(m[:, :], m[:, :], 0.5, None, ALU.mult)
        chain(nc.vector.scalar_tensor_tensor(out=o[:, :], in0=o[:, :], scalar=0.25, in1=o[:, :], op0=ALU.mult, op1=ALU.mult))
        chain(nc.vector.scalar_tensor_tensor(out=v[:, :], in0=v[:, :], scalar=1.0 / D, in1=o[:, :], op0=ALU.mult, op1=ALU.add))
        last = nc.vector.tensor_scalar(self.shifted[:, 0, :], v[:, :], EPS, None, ALU.add)
        if self.w == 2:
            last = nc.vector.tensor_scalar(self.shifted[:, 1, :], v[:, :], 1.0 + EPS, EPS * EPS, ALU.mult, ALU.add)
        last.then_inc(self.asked, 1)

    def act_root(self, nc, act, s):
        act.wait_ge(self.asked, s + 1)
        nc.scalar.activation(self.root[:, :, :], self.shifted[:, :, :], ACT.Ln).then_inc(self.logged, 1)
        act.wait_ge(self.logged, s + 1)
        nc.scalar.activation(self.root[:, :, :], self.root[:, :, :], ACT.Exp, scale=-0.5).then_inc(self.rooted, 1)

    def dve_finish(self, nc, dve, chain, s):
        dve.wait_ge(self.rooted, s + 1)
        chain(nc.vector.tensor_tensor(self.newton[:, :, :], self.root[:, :, :], self.root[:, :, :], ALU.mult))
        chain(nc.vector.tensor_tensor(self.newton[:, :, :], self.newton[:, :, :], self.shifted[:, :, :], ALU.mult))
        chain(nc.vector.tensor_scalar(self.newton[:, :, :], self.newton[:, :, :], -0.5, 1.5, ALU.mult, ALU.add))
        chain(nc.vector.tensor_tensor(self.rstd[:, :, :], self.root[:, :, :], self.newton[:, :, :], ALU.mult))

    def dve_apply(self, nc, out, s):
        for j in range(4):
            last = nc.vector.tensor_scalar(out[:, j, :], rows_of(self.k.X, s * 4 + j), self.mean[:, j:j + 1],
                                           self.rstd[:, self.w - 1, j:j + 1], ALU.subtract, ALU.mult)
        return last


class Router:

    def __init__(self, st, k, first, psT, psL, psP):
        self.k, self.first, self.psT, self.psL, self.psP = k, first, psT, psL, psP
        self.norm = Norm(st, k, "r", double=not first)
        self.normed, self.flipped, self.turned, self.scored, self.centred = map(st.sem, ("r_normed", "r_flipped", "r_turned", "r_scored", "r_centred"))
        self.exped, self.chosen, self.placed, self.rowed, self.taken = map(st.sem, ("r_exped", "r_chosen", "r_placed", "r_rowed", "r_taken"))
        self.scattered = [st.sem(f"r_scattered{i}") for i in range(16)]
        self.zeroed, self.tabled = st.sem("r_zeroed"), st.sem("r_tabled")
        self.xn = st.sb("r_xn", [P, 2, 4, D])
        self.xnT = st.sb("r_xnT", [P, BLOCK])
        self.L, self.prob, self.work = (st.sb(f"r_{n}", [P, 4, EXPERTS]) for n in ("L", "prob", "work"))
        self.top, self.inv = st.sb("r_top", [P, 4]), st.sb("r_inv", [P, 4])
        self.pv = st.sb("r_pv", [P, 2, 4])
        self.hot_bf = st.sb("r_hot_bf", [P, 4, TOPK * EXPERTS], BF16)
        self.pos = st.sb("r_pos", [P, 4, TOPK * EXPERTS])
        self.run = st.sb("r_run", [P, TOPK * EXPERTS])
        self.row = st.sb("r_row", [P, 4, TOPK])
        self.idx = st.sb("r_idx", [P, 2, 4 * TOPK], I32)

    def four(self, s):
        return bass.ds(s * 4, 4)

    def dve_1(self, nc, dve, chain, s, b, turn):
        k, n = self.k, self.norm
        n.dve_finish(nc, dve, chain, s)
        if not (isinstance(turn, int) and turn == 0):
            for i in range(8):
                dve.wait_ge(self.scattered[8 * b + i], turn * 16)
        last = n.dve_apply(nc, self.xn[:, b, :, :], s)
        if not self.first:
            xn = self.xn[:, b, :, :]
            chain(last)
            chain(nc.vector.tensor_tensor(xn, xn, k.gamma[:, :].rearrange("p (a d) -> p a d", a=1).to_broadcast([P, 4, D]), ALU.mult))
            last = nc.vector.tensor_tensor(xn, xn, k.beta[:, :].rearrange("p (a d) -> p a d", a=1).to_broadcast([P, 4, D]), ALU.add)
        last.then_inc(self.normed, 1)
        if not self.first:
            chain(nc.vector.scalar_tensor_tensor(out=n.mean[:, :], in0=n.mean[:, :], scalar=-0.5, in1=n.rstd[:, 0, :], op0=ALU.mult, op1=ALU.mult))
            chain(nc.vector.tensor_scalar(n.rstd[:, 0, :], n.rstd[:, 0, :], 0.5, 1.0, ALU.mult, ALU.add))
            for j in range(4):
                x = rows_of(k.X, s * 4 + j)
                last = nc.vector.tensor_scalar(x, x, n.rstd[:, 0, j:j + 1], n.mean[:, j:j + 1], ALU.mult, ALU.add)
            chain(last)

    def pe_1(self, nc, pe, s, b):
        psT, psL = self.psT(b), self.psL(b)
        pe.wait_ge(self.normed, s + 1)
        for j in range(4):
            last = nc.tensor.transpose(psT[:, j * P:(j + 1) * P], self.xn[:, b, j, :], self.k.ident[:, :])
        last.then_inc(self.flipped, 1)
        pe.wait_ge(self.turned, s + 1)
        for j in range(4):
            last = nc.tensor.matmul(psL[:, j * EXPERTS:(j + 1) * EXPERTS], self.xnT[:, j * P:(j + 1) * P], self.k.gate_w[:, 0 if self.first else 1, :], start=True, stop=True)
        last.then_inc(self.scored, 1)

    def act_1(self, nc, act, s, b):
        act.wait_ge(self.flipped, s + 1)
        nc.scalar.activation(self.xnT[:, :], self.psT(b), ACT.Copy).then_inc(self.turned, 1)

    def wide(self, v):
        return v.rearrange("p (t a) -> p t a", a=1).to_broadcast([P, 4, EXPERTS])

    def dve_2a(self, nc, dve, chain, s, b):
        L, psL = self.L, self.psL(b)[:, 0:4 * EXPERTS].rearrange("p (t e) -> p t e", t=4)
        dve.wait_ge(self.scored, s + 1)
        if self.first:
            chain(nc.vector.tensor_tensor(L[:, :, :], psL, self.k.bg[:, :].rearrange("p (a e) -> p a e", a=1).to_broadcast([P, 4, EXPERTS]), ALU.add))
        else:
            chain(nc.vector.tensor_copy(L[:, :, :], psL))
        chain(nc.vector.tensor_reduce(self.top[:, :], L[:, :, :], AX.X, ALU.max))
        nc.vector.tensor_tensor(L[:, :, :], L[:, :, :], self.wide(self.top[:, :]), ALU.subtract).then_inc(self.centred, 1)

    def act_2(self, nc, act, s):
        act.wait_ge(self.centred, s + 1)
        nc.scalar.activation(self.prob[:, :, :], self.L[:, :, :], ACT.Exp).then_inc(self.exped, 1)

    def dve_2b(self, nc, dve, chain, s, b):
        k, prob, work = self.k, self.prob, self.work
        hot = k.hot[:, self.four(s), :]
        rank = k.small[:, 0:EXPERTS].rearrange("p (a e) -> p a e", a=1).to_broadcast([P, 4, EXPERTS])
        dve.wait_ge(self.exped, s + 1)
        for c in range(TOPK):
            h = hot[:, :, c * EXPERTS:(c + 1) * EXPERTS]
            chain(nc.vector.tensor_reduce(self.pv[:, c, :], prob[:, :, :], AX.X, ALU.max))
            chain(nc.vector.tensor_tensor(work[:, :, :], prob[:, :, :], self.wide(self.pv[:, c, :]), ALU.is_equal))
            chain(nc.vector.tensor_tensor(work[:, :, :], work[:, :, :], rank, ALU.mult))
            chain(nc.vector.tensor_reduce(self.top[:, :], work[:, :, :], AX.X, ALU.max))
            chain(nc.vector.tensor_tensor(h, work[:, :, :], self.wide(self.top[:, :]), ALU.is_equal))
            if c == 0:
                chain(nc.vector.scalar_tensor_tensor(out=prob[:, :, :], in0=h, scalar=-4.0, in1=prob[:, :, :], op0=ALU.mult, op1=ALU.add))
        nc.vector.tensor_scalar(self.hot_bf[:, :, :], hot, 1.0, None, ALU.mult).then_inc(self.chosen, 1)
        chain(nc.vector.tensor_tensor(self.inv[:, :], self.pv[:, 0, :], self.pv[:, 1, :], ALU.add))
        chain(nc.vector.reciprocal(self.inv[:, :], self.inv[:, :]))
        for c in range(TOPK):
            nc.vector.scalar_tensor_tensor(out=k.gate[:, c, self.four(s)], in0=self.pv[:, c, :], scalar=0.5, in1=self.inv[:, :], op0=ALU.mult, op1=ALU.mult)

    def pe_2(self, nc, pe, s, b):
        psP, W = self.psP(b), TOPK * EXPERTS
        pe.wait_ge(self.chosen, s + 1)
        for j in range(5):
            for i in range(j):
                last = nc.tensor.matmul(psP[:, j * W:(j + 1) * W], self.k.ones[:, :], self.hot_bf[:, i, :], start=(i == 0), stop=(j == 4 and i == 3))
            if j < 4:
                last = nc.tensor.matmul(psP[:, j * W:(j + 1) * W], self.k.before[:, :], self.hot_bf[:, j, :], start=(j == 0), stop=True)
        last.then_inc(self.placed, 1)

    def dve_2c(self, nc, dve, chain, s, b):
        k, W = self.k, TOPK * EXPERTS
        psP, pos = self.psP(b), self.pos
        all4 = lambda v: v.rearrange("p (a c) -> p a c", a=1).to_broadcast([P, 4, W])
        dve.wait_ge(self.placed, s + 1)
        chain(nc.vector.tensor_tensor(pos[:, :, :], psP[:, 0:4 * W].rearrange("p (t c) -> p t c", t=4), all4(self.run[:, :]), ALU.add))
        nc.vector.tensor_tensor(self.run[:, :], psP[:, 4 * W:5 * W], self.run[:, :], ALU.add)
        chain(nc.vector.tensor_tensor(pos[:, :, :], pos[:, :, :], all4(k.small[:, SIGN:SIGN + W]), ALU.mult))
        chain(nc.vector.tensor_tensor(pos[:, :, :], pos[:, :, :], all4(k.small[:, BASE:BASE + W]), ALU.add))
        chain(nc.vector.tensor_tensor(pos[:, :, :], pos[:, :, :], k.hot[:, self.four(s), :], ALU.mult))
        chain(nc.vector.tensor_reduce(self.row[:, :, :], pos[:, :, :].rearrange("p t (c e) -> p t c e", c=TOPK), AX.X, ALU.add))
        nc.vector.tensor_scalar(k.row[:, self.four(s), :], self.row[:, :, :], 1.0, None, ALU.mult)
        nc.vector.tensor_copy(self.idx[:, b, :], self.row[:, :, :].rearrange("p t c -> p (t c)")).then_inc(self.rowed, 1)

    def links(self):
        one = 4 + (0 if self.first else 5)
        return one, 2, 11 + 2, 5

    def pool_start(self, pool):
        self.last_row = pool.to_reg(DUMP - 1)

    def pool(self, pool, s, b):
        pool.wait_ge(self.rowed, s + 1)
        pool.sem_inc(self.taken, 1)
        for i in range(8):
            pool.indirect_dma_start(out=self.k.xslots[:, :], out_offset=bass.IndirectOffsetOnAxis(ap=self.idx[:, b, i:i + 1].bitcast(U32), axis=0),
                                    in_=self.xn[:, b, i // 2, :], in_offset=None, bounds_check=self.last_row, oob_is_err=False).then_inc(self.scattered[8 * b + i], 16)

    def dve_tables(self, nc, dve, chain, st):
        k, E = self.k, EXPERTS
        names = "n1 start length nblk end before ones".split()
        n1, start, length, nblk, end, before, ones = (st.sb(f"r_{n}", [P, E]) for n in names)
        count_i = st.sb("r_count_i", [P, E], I32)
        owner, late = (st.sb(f"r_{n}", [P, NBLK, E]) for n in ("owner", "late"))
        of_block, row_f = st.sb("r_of_block", [P, NBLK]), st.sb("r_row_f", [P, NBLK])
        middle = k.small[:, MIDDLE:MIDDLE + E]
        per_block = lambda v: v.rearrange("p (a e) -> p a e", a=1).to_broadcast([P, NBLK, E])
        number = k.small[:, NUMBER:NUMBER + NBLK]
        numbers = number.rearrange("p (n a) -> p n a", a=1).to_broadcast([P, NBLK, E])
        first_n, second_n = self.run[:, 0:E], self.run[:, E:2 * E]
        limit, shift = st.sb("r_limit", [P, TOPK, E]), st.sb("r_shift", [P, E])
        mine, per_token, keep = st.sb("r_mine", [P, TILES, E]), st.sb("r_per_token", [P, TILES]), st.sb("r_keep", [P, TILES])
        chain(nc.vector.memset(ones[:, :], 1.0))
        chain(nc.vector.tensor_tensor(length[:, :], first_n, second_n, ALU.add))
        if self.first:
            chain(nc.vector.tensor_scalar(n1[:, :], first_n, float(CAPACITY), None, ALU.min))
            chain(nc.vector.tensor_scalar(length[:, :], length[:, :], float(CAPACITY), None, ALU.min))
            chain(nc.vector.tensor_scalar(limit[:, 0, :], middle, float(-CAPACITY), None, ALU.add))
            chain(nc.vector.tensor_tensor(limit[:, 1, :], middle, first_n, ALU.subtract))
            chain(nc.vector.tensor_scalar(limit[:, 1, :], limit[:, 1, :], float(CAPACITY), None, ALU.add))
        else:
            chain(nc.vector.tensor_copy(n1[:, :], first_n))
        chain(nc.vector.tensor_tensor(start[:, :], middle, n1[:, :], ALU.subtract))
        chain(nc.vector.tensor_tensor(nblk[:, :], start[:, :], length[:, :], ALU.add))
        chain(nc.vector.tensor_copy(k.pad_row[:, :], nblk[:, :]))
        chain(nc.vector.tensor_scalar(length[:, :], length[:, :], float(BLOCK - 1), None, ALU.add))
        chain(nc.vector.tensor_copy(count_i[:, :], length[:, :]))
        chain(nc.vector.tensor_scalar(count_i[:, :], count_i[:, :], BLOCK.bit_length() - 1, None, ALU.arith_shift_right))
        chain(nc.vector.tensor_copy(nblk[:, :], count_i[:, :]))
        chain(nc.vector.tensor_tensor_scan(end[:, :], ones[:, :], nblk[:, :], 0.0, ALU.mult, ALU.add))
        chain(nc.vector.tensor_tensor(before[:, :], end[:, :], nblk[:, :], ALU.subtract))
        chain(nc.vector.scalar_tensor_tensor(out=shift[:, :], in0=before[:, :], scalar=float(BLOCK), in1=start[:, :], op0=ALU.mult, op1=ALU.subtract))
        per_tile = lambda v: v.rearrange("p (a e) -> p a e", a=1).to_broadcast([P, TILES, E])
        for c in range(TOPK):
            hot, row = k.hot[:, :, c * E:(c + 1) * E], k.row[:, :, c]
            if self.first:
                chain(nc.vector.tensor_tensor(mine[:, :, :], hot, per_tile(limit[:, c, :]), ALU.mult))
                chain(nc.vector.tensor_reduce(per_token[:, :], mine[:, :, :], AX.X, ALU.add))
                chain(nc.vector.tensor_tensor(keep[:, :], row, per_token[:, :], ALU.is_lt if c else ALU.is_ge))
            chain(nc.vector.tensor_tensor(mine[:, :, :], hot, per_tile(shift[:, :]), ALU.mult))
            chain(nc.vector.tensor_reduce(per_token[:, :], mine[:, :, :], AX.X, ALU.add))
            chain(nc.vector.tensor_tensor(row, row, per_token[:, :], ALU.add))
            if self.first:
                chain(nc.vector.tensor_scalar(row, row, float(-TRASH), None, ALU.add))
                chain(nc.vector.tensor_tensor(row, row, keep[:, :], ALU.mult))
                chain(nc.vector.tensor_scalar(row, row, float(TRASH), None, ALU.add))
        chain(nc.vector.tensor_copy(k.idx[:, 0:TILES, :], k.row[:, :, :]))
        chain(nc.vector.tensor_tensor(owner[:, :, :], per_block(before[:, :]), numbers, ALU.is_le))
        chain(nc.vector.tensor_tensor(late[:, :, :], per_block(end[:, :]), numbers, ALU.is_gt))
        chain(nc.vector.tensor_tensor(owner[:, :, :], owner[:, :, :], late[:, :, :], ALU.mult))
        chain(nc.vector.tensor_reduce(of_block[:, :], owner[:, :, :], AX.X, ALU.add))
        chain(nc.vector.tensor_scalar(before[:, :], before[:, :], float(-BLOCK), float(-DUMP), ALU.mult, ALU.add))
        chain(nc.vector.tensor_tensor(start[:, :], start[:, :], before[:, :], ALU.add))
        chain(nc.vector.tensor_tensor(late[:, :, :], owner[:, :, :], per_block(start[:, :]), ALU.mult))
        chain(nc.vector.tensor_reduce(row_f[:, :], late[:, :, :], AX.X, ALU.add))
        chain(nc.vector.tensor_tensor(of_block[:, :], of_block[:, :], number, ALU.mult))
        chain(nc.vector.tensor_scalar(of_block[:, :], of_block[:, :], float(BLOCK), float(DUMP), ALU.mult, ALU.add))
        chain(nc.vector.tensor_tensor(row_f[:, :], row_f[:, :], of_block[:, :], ALU.add))
        chain(nc.vector.tensor_copy(k.block_row[:, :], row_f[:, :]))
        chain(nc.vector.tensor_tensor(late[:, :, :], owner[:, :, :], per_block(k.small[:, EIGHT:EIGHT + E]), ALU.mult))
        chain(nc.vector.tensor_reduce(of_block[:, :], late[:, :, :], AX.X, ALU.add))
        nc.vector.tensor_copy(k.owner[:, :], of_block[:, :]).then_inc(self.tabled, 1)

    def sp_pads(self, nc, sp, zeros, cleared):
        sp.wait_ge(self.tabled, 1)
        sp.wait_ge(cleared, 1)
        for s in range(16):
            sp.wait_ge(self.scattered[s], BATCH // 2 * 16)
        for e in range(EXPERTS):
            r = sp.value_load(self.k.pad_row[0:1, e:e + 1], min_val=0, max_val=DUMP - BLOCK)
            sp.dma_start(self.k.xslots[bass.ds(r, BLOCK), :].rearrange("(p r) d -> p (r d)", p=P), zeros[:, :]).then_inc(self.zeroed, 16)
        sp.wait_ge(self.zeroed, EXPERTS * 16)


class Gather:

    def __init__(self, st, k):
        self.k = k
        self.gathered = [st.sem(f"g_gathered{i}") for i in range(16)]
        self.idx_ready, self.taken = st.sem("g_idx_ready"), st.sem("g_taken")
        self.rows = st.sb("g_rows", [P, 2, 8, D])
        self.idx = st.sb("g_idx", [P, 2, 8], I32)

    def dve_ask(self, nc, s, b):
        nc.vector.tensor_scalar(self.idx[:, b, :], self.k.idx[:, bass.ds(s * 4, 4), :].rearrange("p t c -> p (t c)"), 1.0, None, ALU.mult).then_inc(self.idx_ready, 1)

    def dve(self, nc, dve, chain, s, b, turn):
        for c in range(TOPK):
            for j in range(4):
                x = rows_of(self.k.X, s * 4 + j)
                dve.wait_ge(self.gathered[8 * b + 2 * j + c], turn * 16 + 16)
                last = nc.vector.scalar_tensor_tensor(out=x, in0=self.rows[:, b, 2 * j + c, :], scalar=self.k.gate[:, c, bass.ds(s * 4 + j, 1)],
                                                      in1=x, op0=ALU.mult, op1=ALU.add)
            chain(last)
        self.dve_ask(nc, s + 2, b)

    def pool_start(self, pool):
        self.last_row = pool.to_reg(TRASH)

    def pool(self, pool, s, b):
        pool.wait_ge(self.idx_ready, s + 1)
        pool.sem_inc(self.taken, 1)
        for i in range(8):
            pool.indirect_dma_start(out=self.rows[:, b, i, :], out_offset=None, in_=self.k.yslots[:, :],
                                    in_offset=bass.IndirectOffsetOnAxis(ap=self.idx[:, b, i:i + 1].bitcast(U32), axis=0),
                                    bounds_check=self.last_row, oob_is_err=False).then_inc(self.gathered[8 * b + i], 16)


def plain_stage(nc, k, name, gather, route, out=None):
    routing = route is not None
    with Stage(nc, name) as st:
        G = Gather(st, k) if gather else None
        linked, cleared, added = st.sem("linked"), st.sem("cleared"), st.sem("added")
        if routing:
            psT, psL, psP = st.pb("psT", [P, BLOCK]), st.pb("psL", [P, 2, BLOCK]), st.pb("psP", [P, BLOCK])
            R = Router(st, k, route, lambda b: psT[:, :], lambda b: psL[:, b, :], lambda b: psP[:, :])
            zeros = st.sb("zeros", [P, BLOCK])
        saved = st.sem("saved")
        block = st.block()

        def order(eng, head, tail, chain=None, links=0):
            head(0, 0, 0)
            sequences(eng, lambda s, b, turn, first, last: ((None if last else head(s + 1, 1 - b, turn + b)), tail(s, b)), chain, links)

        @block.vector
        def _(dve):
            chain = Chain(dve, linked)
            if routing:
                nc.vector.memset(zeros[:, :], 0.0).then_inc(cleared, 1)
                chain(nc.vector.memset(R.run[:, :], 0.0))
            if gather:
                for b in range(2):
                    G.dve_ask(nc, b, b)

            def head(s, b, turn):
                if gather:
                    G.dve(nc, dve, chain, s, b, turn)
                    if not routing:
                        dve.sem_inc(added, 1)
                if routing:
                    R.norm.dve_stats(nc, chain, s)
                    R.dve_1(nc, dve, chain, s, b, turn)

            def tail(s, b):
                if routing:
                    R.dve_2a(nc, dve, chain, s, b)
                    R.dve_2b(nc, dve, chain, s, b)
                    R.dve_2c(nc, dve, chain, s, b)

            links = (2 if gather else 0) + (sum(R.links()) + 4 if routing else 0)
            order(dve, head, tail, chain, 2 * links)
            if routing:
                R.dve_tables(nc, dve, chain, st)

        if routing:
            @block.scalar
            def _(act):
                act.preload_act_table_set("natural_log_exp_and_others")
                order(act, lambda s, b, turn: (R.norm.act_root(nc, act, s), R.act_1(nc, act, s, b)), lambda s, b: R.act_2(nc, act, s))

            @block.tensor
            def _(pe):
                order(pe, lambda s, b, turn: R.pe_1(nc, pe, s, b), lambda s, b: R.pe_2(nc, pe, s, b))

        @block.gpsimd
        def _(pool):
            if routing:
                R.pool_start(pool)
            if gather:
                G.pool_start(pool)
            order(pool, lambda s, b, turn: G.pool(pool, s, b) if gather else None, lambda s, b: R.pool(pool, s, b) if routing else None)

        @block.sync
        def _(sp):
            if routing:
                R.sp_pads(nc, sp, zeros, cleared)
            if out is not None:
                with sp.Fori(0, BATCH) as s:
                    sp.wait_ge(added, s + 1)
                    sp.dma_start(out[bass.ds(s * SEQ, SEQ), :].rearrange("(t p) d -> p t d", p=P), k.X[:, bass.ds(s * 4, 4), :]).then_inc(saved, 16)
                sp.wait_ge(saved, BATCH * 16)


def load_stage(nc, k, x, consts, l0_bg, gate_w, gamma, beta):
    with Stage(nc, "load") as st:
        loaded, zeroed, cleared = map(st.sem, ("loaded", "zeroed", "cleared"))
        zeros = st.sb("zeros", [P, BLOCK])
        raw = st.sb("raw", [P, 35 * P])
        block = st.block()

        @block.sync
        def _(sp):
            wide = lambda v: v.rearrange("(a e) -> a e", a=1)
            for dst, src in ((raw[:, :], consts[:, P:36 * P]), (k.ident[:, :], consts[:, 0:P]), (k.small[:, :], consts[:, 36 * P:]),
                             (k.bg[:, :], wide(l0_bg).to_broadcast([P, EXPERTS])), (k.gamma[:, :], wide(gamma).to_broadcast([P, D])),
                             (k.beta[:, :], wide(beta).to_broadcast([P, D])), (k.gate_w[:, 0, :], gate_w[0]), (k.gate_w[:, 1, :], gate_w[1]),
                             (k.X[:, :, :], x.rearrange("(t p) d -> p t d", p=P))):
                sp.dma_start(dst, src).then_inc(loaded, 16)
            sp.wait_ge(loaded, 9 * 16)

        @block.scalar
        def _(act):
            act.wait_ge(cleared, 1)
            act.dma_start(k.xslots[DUMP:DUMP + BLOCK, :].rearrange("(p r) d -> p (r d)", p=P), zeros[:, :]).then_inc(zeroed, 16)
            act.dma_start(k.yslots[TRASH:TRASH + 1, :], zeros[0:1, 0:D]).then_inc(zeroed, 16)
            act.wait_ge(zeroed, 32)

        @block.vector
        def _(dve):
            nc.vector.memset(k.ones[:, :], 1.0)
            nc.vector.memset(k.idx[:, TILES:, :], TRASH)
            nc.vector.memset(zeros[:, :], 0.0).then_inc(cleared, 1)
            dve.wait_ge(loaded, 9 * 16)
            nc.vector.tensor_copy(k.before[:, :], raw[:, 0:P])
            nc.vector.tensor_copy(k.causal[:, :], raw[:, P:2 * P])
            nc.vector.tensor_copy(k.ident_bf[:, :], raw[:, 2 * P:3 * P])
            nc.vector.tensor_copy(k.pick[:, :, :].rearrange("p n m -> p (n m)"), raw[0:96, 3 * P:])


def blocks_stage(nc, k, name, pack, gelu):
    with Stage(nc, name) as st:
        sem, sb, pb = st.sem, st.sb, st.pb
        w_ready = [sem(f"w_ready{i}") for i in range(2)]
        x_ready = [sem(f"x_ready{i}") for i in range(2)]
        stored = [sem(f"stored{i}") for i in range(2)]
        x_flipped, xT_ready, h_summed, h_ready, y_summed, yT_ready, y_flipped, y_ready = map(
            sem, ("x_flipped", "xT_ready", "h_summed", "h_ready", "y_summed", "yT_ready", "y_flipped", "y_ready"))
        W = sb("W", [P, 2, PACK])
        xs = sb("xs", [P, 2, 4, D])
        xT = sb("xT", [P, 2, BLOCK])
        H = sb("H", [P, 2, FT, BLOCK])
        yT = sb("yT", [P, 2, BLOCK])
        yr = sb("yr", [P, 2, 4, D])
        psX = pb("psX", [P, 4, P])
        psH = pb("psH", [P, FT, BLOCK])
        psY = pb("psY", [P, BLOCK])
        psR = pb("psR", [P, 4, P])
        block = st.block()

        TURNS = NBLK // 2

        def turns(eng, one):
            one(0, 0, 0, True, False)
            one(1, 1, 0, False, False)
            with eng.Fori(1, TURNS - 1) as j2:
                for b in range(2):
                    one(j2 * 2 + b, b, j2, False, False)
            one(NBLK - 2, 0, TURNS - 1, False, False)
            one(NBLK - 1, 1, TURNS - 1, False, True)

        @block.sync
        def _(sp):
            def load(j, b, waits):
                if waits:
                    sp.wait_ge(yT_ready, j - 1)
                r = sp.value_load(k.block_row[0:1, bass.ds(j, 1)], min_val=0, max_val=DUMP)
                e = sp.value_load(k.owner[0:1, bass.ds(j, 1)], min_val=0, max_val=EXPERTS - 1)
                sp.dma_start(W[:, b, :], pack[bass.ds(e, 1), :, :].rearrange("a p n -> (a p) n")).then_inc(w_ready[b], 16)
                sp.dma_start(xs[:, b, :, :], k.xslots[bass.ds(r, BLOCK), :].rearrange("(p s) d -> p s d", p=P)).then_inc(x_ready[b], 16)

            def store(j, b):
                sp.wait_ge(y_ready, j + 1)
                sp.dma_start(k.yslots[bass.ds(j * BLOCK, BLOCK), :].rearrange("(p s) d -> p s d", p=P), yr[:, b, :, :]).then_inc(stored[b], 16)

            for b in range(2):
                load(b, b, False)
            with sp.Fori(1, TURNS) as j2:
                for b in range(2):
                    load(j2 * 2 + b, b, True)
                    store(j2 * 2 + b - 2, b)
            for b in range(2):
                store(NBLK - 2 + b, b)
                sp.wait_ge(stored[b], TURNS * 16)

        @block.tensor
        def _(pe):
            def flip_in(b, turn):
                pe.wait_ge(x_ready[b], turn * 16 + 16)
                for s in range(4):
                    last = nc.tensor.transpose(psX[:, s, :], xs[:, b, s, :], k.ident[:, :])
                last.then_inc(x_flipped, 1)

            def flip_out(count, b):
                pe.wait_ge(yT_ready, count)
                for s in range(4):
                    last = nc.tensor.transpose(psR[:, s, :], yT[:, b, s * P:(s + 1) * P], k.ident[:, :])
                last.then_inc(y_flipped, 1)

            def one(j, b, j2, first_block, last_block):
                pe.wait_ge(w_ready[b], j2 * 16 + 16)
                pe.wait_ge(xT_ready, j + 1)
                for f in range(FT):
                    nc.tensor.matmul(psH[:, f, :], W[:, b, f * P:(f + 1) * P], xT[:, b, :], start=True, stop=True).then_inc(h_summed, 1)
                if not first_block:
                    flip_out(j, 1 - b)
                if not last_block:
                    flip_in(1 - b, j2 + b)
                for f in range(FT):
                    pe.wait_ge(h_ready, j * FT + f + 1)
                    last = nc.tensor.matmul(psY[:, :], W[:, b, HIDDEN + f * D:HIDDEN + (f + 1) * D], H[:, b, f, :], start=(f == 0), stop=(f == FT - 1))
                last.then_inc(y_summed, 1)

            flip_in(0, 0)
            turns(pe, one)
            flip_out(NBLK, 1)

        @block.scalar
        def _(act):
            with act.Fori(0, TURNS) as j2:
                for b in range(2):
                    for f in range(FT):
                        act.wait_ge(h_summed, (j2 * 2 + b) * FT + f + 1)
                        nc.scalar.activation(H[:, b, f, :], psH[:, f, :], gelu, bias=W[:, b, HIDDEN + FT * D + f:HIDDEN + FT * D + f + 1]).then_inc(h_ready, 1)

        @block.vector
        def _(dve):
            def turn_in(j, b):
                dve.wait_ge(x_flipped, j + 1)
                nc.vector.tensor_copy(xT[:, b, :], psX[:, :, :].rearrange("p a d -> p (a d)")).then_inc(xT_ready, 1)

            def rows_out(count, b, stores):
                dve.wait_ge(y_flipped, count)
                if stores is not None:
                    dve.wait_ge(stored[b], stores)
                nc.vector.tensor_copy(yr[:, b, :, :], psR[:, :, :]).then_inc(y_ready, 1)

            def one(j, b, j2, first_block, last_block):
                if not first_block:
                    early = isinstance(j2, int) and j2 == 0
                    rows_out(j, 1 - b, None if early else (j2 - 1 + b) * 16 if not (isinstance(j2, int) and j2 + b < 2) else None)
                if not last_block:
                    turn_in(j + 1, 1 - b)
                dve.wait_ge(y_summed, j + 1)
                nc.vector.tensor_scalar(yT[:, b, :], psY[:, :], W[:, b, PACK - 1:PACK], None, ALU.add).then_inc(yT_ready, 1)

            turn_in(0, 0)
            one(0, 0, 0, True, False)
            one(1, 1, 0, False, False)
            one(2, 0, 1, False, False)
            one(3, 1, 1, False, False)
            with dve.Fori(2, TURNS - 1) as j2:
                for b in range(2):
                    one(j2 * 2 + b, b, j2, False, False)
            one(NBLK - 2, 0, TURNS - 1, False, False)
            one(NBLK - 1, 1, TURNS - 1, False, True)
            rows_out(NBLK, 1, (TURNS - 1) * 16)


def attention_stage(nc, k, wqkv):
    with Stage(nc, "att") as st:
        sem, sb, pb = st.sem, st.sb, st.pb
        w_ready, linked, normed, flipped, turned, q_summed, k_summed, v_summed, qk_ready, v_ready = map(
            sem, ("w_ready", "linked", "normed", "flipped", "turned", "q_summed", "k_summed", "v_summed", "qk_ready", "v_ready"))
        scored, topped, exped, p_flipped, p_turned, summed, added, holed, cleared = map(
            sem, ("scored", "topped", "exped", "p_flipped", "p_turned", "summed", "added", "holed", "cleared"))
        W = sb("W", [P, 3, P])
        xn = sb("xn", [P, 4, D])
        xnT = sb("xnT", [P, SEQ])
        QT, KT = sb("QT", [P, SEQ]), sb("KT", [P, SEQ])
        V = sb("V", [P, 4, D])
        hole, S, E, PT = (sb(n, [P, 2, SEQ]) for n in ("hole", "S", "E", "PT"))
        top, ntop, total, inv = (sb(n, [P, 2]) for n in ("top", "ntop", "total", "inv"))
        zeros = sb("zeros", [P, BLOCK])
        psT = pb("psT", [P, SEQ])
        psQ, psK = pb("psQ", [P, SEQ]), pb("psK", [P, SEQ])
        psS = pb("psS", [P, 2, SEQ])
        psE = pb("psE", [P, SEQ])
        psO = pb("psO", [P, D])
        psR = pb("psR", [P, SEQ])
        G = Gather(st, k)
        N = Norm(st, k, "n")
        R = Router(st, k, True, lambda b: psT[:, :], lambda b: psR[:, 0:4 * EXPERTS], lambda b: psR[:, 256:])
        block = st.block()
        ST = SEQ_TILES

        @block.sync
        def _(sp):
            sp.dma_start(W[:, :, :], wqkv).then_inc(w_ready, 16)
            R.sp_pads(nc, sp, zeros, cleared)

        @block.gpsimd
        def _(pool):
            R.pool_start(pool)
            G.pool_start(pool)
            G.pool(pool, 0, 0)

            def body(s, b, turn, first, last):
                if not last:
                    G.pool(pool, s + 1, 1 - b)
                if not first:
                    R.pool(pool, s - 1, 1 - b)
            sequences(pool, body)
            R.pool(pool, BATCH - 1, 1)

        @block.tensor
        def _(pe):
            pe.wait_ge(w_ready, 16)

            def body(s, b, turn, first, last):
                pe.wait_ge(normed, s + 1)
                for j in range(ST):
                    ins = nc.tensor.transpose(psT[:, j * P:(j + 1) * P], xn[:, j, :], k.ident[:, :])
                ins.then_inc(flipped, 1)
                pe.wait_ge(turned, s + 1)
                nc.tensor.matmul(psQ[:, :], W[:, 0, :], xnT[:, :], start=True, stop=True).then_inc(q_summed, 1)
                nc.tensor.matmul(psK[:, :], W[:, 1, :], xnT[:, :], start=True, stop=True).then_inc(k_summed, 1)
                for j in range(ST):
                    ins = nc.tensor.matmul(psT[:, j * P:(j + 1) * P], xnT[:, j * P:(j + 1) * P], W[:, 2, :], start=True, stop=True)
                ins.then_inc(v_summed, 1)

                def scores(i):
                    n = (i + 1) * P
                    if i > 0:
                        nc.tensor.matmul(psS[:, i % 2, 0:i * P], QT[:, i * P:n], KT[:, 0:i * P], start=True, stop=True)
                    nc.tensor.matmul(psS[:, i % 2, i * P:n], QT[:, i * P:n], KT[:, i * P:n], start=True, stop=False)
                    nc.tensor.matmul(psS[:, i % 2, i * P:n], k.ident_bf[:, :], k.causal[:, :], start=False, stop=True).then_inc(scored, 1)

                pe.wait_ge(qk_ready, s * 2 + 2)
                scores(0)
                for i in range(ST):
                    if i + 1 < ST:
                        scores(i + 1)
                    pe.wait_ge(exped, s * ST + i + 1)
                    for j in range(i + 1):
                        ins = nc.tensor.transpose(psE[:, j * P:(j + 1) * P], E[:, i % 2, j * P:(j + 1) * P], k.ident[:, :])
                    ins.then_inc(p_flipped, 1)
                    pe.wait_ge(p_turned, s * ST + i + 1)
                    if i == 0:
                        pe.wait_ge(v_ready, s + 1)
                    if not (i == 0 and first):
                        pe.wait_ge(added, s * ST + i)
                    for j in range(i + 1):
                        ins = nc.tensor.matmul(psO[:, :], PT[:, i % 2, j * P:(j + 1) * P], V[:, j, :], start=(j == 0), stop=(j == i))
                    ins.then_inc(summed, 1)
                    if i == 0 and not first:
                        R.pe_1(nc, pe, s - 1, 1 - b)
                    if i == 2 and not first:
                        R.pe_2(nc, pe, s - 1, 1 - b)
            sequences(pe, body)
            R.pe_1(nc, pe, BATCH - 1, 1)
            R.pe_2(nc, pe, BATCH - 1, 1)

        @block.scalar
        def _(act):
            act.preload_act_table_set("natural_log_exp_and_others")
            N.act_root(nc, act, 0)

            def body(s, b, turn, first, last):
                act.wait_ge(flipped, s + 1)
                nc.scalar.activation(xnT[:, :], psT[:, :], ACT.Copy).then_inc(turned, 1)
                act.wait_ge(k_summed, s + 1)
                nc.scalar.activation(KT[:, :], psK[:, :], ACT.Copy).then_inc(qk_ready, 1)
                act.wait_ge(v_summed, s + 1)
                nc.scalar.activation(V[:, :, :], psT[:, :].rearrange("p (a d) -> p a d", a=4), ACT.Copy).then_inc(v_ready, 1)
                if not first:
                    R.norm.act_root(nc, act, s - 1)
                for i in range(ST):
                    n = (i + 1) * P
                    act.wait_ge(topped, s * ST + i + 1)
                    nc.scalar.activation(E[:, i % 2, 0:n], S[:, i % 2, 0:n], ACT.Exp, bias=ntop[:, i % 2:i % 2 + 1], scale=SCALE,
                                         accum_out=total[:, i % 2:i % 2 + 1]).then_inc(exped, 1)
                    act.wait_ge(p_flipped, s * ST + i + 1)
                    nc.scalar.activation(PT[:, i % 2, 0:n], psE[:, 0:n], ACT.Copy).then_inc(p_turned, 1)
                    if i == 0 and not first:
                        R.act_1(nc, act, s - 1, 1 - b)
                    if i == 1 and not first:
                        R.act_2(nc, act, s - 1)
                    if i == 2 and not last:
                        N.act_root(nc, act, s + 1)
            sequences(act, body)
            R.norm.act_root(nc, act, BATCH - 1)
            R.act_1(nc, act, BATCH - 1, 1)
            R.act_2(nc, act, BATCH - 1)

        @block.vector
        def _(dve):
            chain = Chain(dve, linked)
            nc.vector.memset(zeros[:, :], 0.0).then_inc(cleared, 1)
            chain(nc.vector.memset(R.run[:, :], 0.0))
            for b in range(2):
                G.dve_ask(nc, b, b)
            G.dve(nc, dve, chain, 0, 0, 0)
            N.dve_stats(nc, chain, 0)
            N.dve_finish(nc, dve, chain, 0)
            N.dve_apply(nc, xn, 0).then_inc(normed, 1)

            def body(s, b, turn, first, last):
                def mask(i):
                    n, h = (i + 1) * P, i % 2
                    dve.wait_ge(scored, s * ST + i + 1)
                    chain(nc.vector.tensor_scalar(hole[:, h, 0:n], psS[:, h, 0:n], 0.0, NEG, ALU.is_equal, ALU.mult))
                    dve.sem_inc(holed, 1)
                    chain(nc.vector.tensor_tensor_reduce(out=S[:, h, 0:n], in0=psS[:, h, 0:n], in1=hole[:, h, 0:n], scale=1.0, scalar=3.0 * NEG,
                                                         op0=ALU.add, op1=ALU.max, accum_out=top[:, h:h + 1]))
                    nc.vector.tensor_scalar(ntop[:, h:h + 1], top[:, h:h + 1], -SCALE, None, ALU.mult).then_inc(topped, 1)

                def finish(i):
                    t, h = s * ST + i, i % 2
                    dve.wait_ge(exped, s * ST + i + 1)
                    chain(nc.vector.reciprocal(inv[:, h:h + 1], total[:, h:h + 1]))
                    dve.wait_ge(summed, s * ST + i + 1)
                    nc.vector.scalar_tensor_tensor(out=rows_of(k.X, t), in0=psO[:, :], scalar=inv[:, h:h + 1], in1=rows_of(k.X, t),
                                                   op0=ALU.mult, op1=ALU.add).then_inc(added, 1)

                dve.wait_ge(q_summed, s + 1)
                nc.vector.tensor_copy(QT[:, :], psQ[:, :]).then_inc(qk_ready, 1)
                if not first:
                    dve.wait_ge(added, s * ST)
                    R.norm.dve_stats(nc, chain, s - 1)
                mask(0)
                if not first:
                    R.dve_1(nc, dve, chain, s - 1, 1 - b, turn - 1 + b)
                mask(1)
                finish(0)
                if not first:
                    R.dve_2a(nc, dve, chain, s - 1, 1 - b)
                mask(2)
                finish(1)
                if not last:
                    G.dve(nc, dve, chain, s + 1, 1 - b, turn + b)
                    N.dve_stats(nc, chain, s + 1)
                if not first:
                    R.dve_2b(nc, dve, chain, s - 1, 1 - b)
                mask(3)
                finish(2)
                if not last:
                    N.dve_finish(nc, dve, chain, s + 1)
                    N.dve_apply(nc, xn, s + 1).then_inc(normed, 1)
                if not first:
                    R.dve_2c(nc, dve, chain, s - 1, 1 - b)
                finish(3)
            sequences(dve, body, chain, 2 * (3 * ST + 2 + 4 + 4 + 4 + sum(R.links())))
            s, b = BATCH - 1, 1
            dve.wait_ge(added, BATCH * ST)
            R.norm.dve_stats(nc, chain, s)
            R.dve_1(nc, dve, chain, s, b, s // 2)
            R.dve_2a(nc, dve, chain, s, b)
            R.dve_2b(nc, dve, chain, s, b)
            R.dve_2c(nc, dve, chain, s, b)
            R.dve_tables(nc, dve, chain, st)


def scan_stage(nc, k, w):
    with Stage(nc, "ssm") as st:
        sem, sb, pb = st.sem, st.sb, st.pb
        Win = sb("Win", [P, 2 * INNER])
        Wtap = sb("Wtap", [P, 2, TAPS, INNER])
        Wx = sb("Wx", [P, DT, RANK + 3 * 32])
        Wdt = sb("Wdt", [RANK, INNER])
        Wout = sb("Wout", [P, DT, D])
        col = sb("col", [P, DT, 4 + STATES])
        gates, gmax = sb("gates", [P, 2]), sb("gmax", [P, 1])
        A = sb("A", [P, DT, STATES])
        xn = sb("xn", [P, 4, D])
        hT = sb("hT", [P, PAD + SEQ])
        pre = sb("pre", [P, 2 * DT, SEQ])
        zs, xc, delta, ux = (sb(n, [P, 2, DT, SEQ]) for n in ("zs", "xc", "delta", "ux"))
        low = sb("low", [RANK, SEQ])
        bc = sb("bc", [96, SEQ])
        bc3 = sb("bc3", [96, 2, SEQ], BF16)
        v, absv, soft, rest = (sb(n, [P, DT, SEQ]) for n in ("v", "absv", "soft", "rest"))
        RA, RB, RH, RC, RP = 4, 2, 4, 2, 2
        dA, dBx, H, HC = (sb(n, [P, r, DT, SEQ]) for n, r in (("dA", RA), ("dBx", RB), ("H", RH), ("HC", RP)))
        Cs = sb("Cs", [P, RC, 1, SEQ])
        zeros = dBx[:, 0, 0, :]
        tap = H[:, 0:2, :, :].rearrange("p a b t -> p (a b t)").rearrange("p (c t e) -> p c t e", c=2, t=TAPS)
        psA, psB = pb("psA", [P, 2, SEQ]), pb("psB", [P, 2, SEQ])
        psC, psR, psY = pb("psC", [P, SEQ]), pb("psR", [P, SEQ]), pb("psY", [P, DT, SEQ])
        G, N = Gather(st, k), Norm(st, k, "n")
        R = Router(st, k, False, lambda b: psR[:, :], lambda b: psR[:, 0:4 * EXPERTS], lambda b: psR[:, 256:])
        (loaded, linked, loose, exp_ready, setup, normed, flipped, turned, fronted, emptied, silu_done, mixed, projected, cut, low_ready, dt_summed, v_ready,
         abs_ready, u_ready, l_ready, delta_ready, ux_ready) = map(sem, "loaded linked loose exp_ready setup normed flipped turned fronted emptied silu_done mixed projected cut low_ready dt_summed v_ready abs_ready u_ready l_ready delta_ready ux_ready".split())
        dA_ready, B_ready, C_ready, Cs_ready, dBx_done, h_ready, hc_ready, y_summed, y_emptied, y_ready, out_summed, added, cleared, z_done = map(
            sem, "dA_ready B_ready C_ready Cs_ready dBx_done h_ready hc_ready y_summed y_emptied y_ready out_summed added cleared z_done".split())
        block = st.block()
        ST, NB = SEQ_TILES, STATES
        on_dve = lambda n: n in DVE_STATES

        def run(eng, main, between, chain=None, links=0):
            def body(s, b, turn, first, last):
                for n in range(NB):
                    main(s, b, n, first)
                    between(s, b, turn, n, first, last)
            sequences(eng, body, chain, links)

        @block.sync
        def _(sp):
            for dst, src in ((Win[:, :], w["in"]), (tap, w["taps"].to_broadcast([P, 2, TAPS, INNER])), (Wx[:, :, 0:RANK + 32], w["x"]),
                             (Wdt[:, :], w["dt"]), (Wout[:, :, :], w["out"]), (col[:, :, :], w["col"]),
                             (gates[:, :], w["gates"].rearrange("(a e) -> a e", a=1).to_broadcast([P, 2]))):
                sp.dma_start(dst, src).then_inc(loaded, 16)
            sp.wait_ge(loaded, 7 * 16)
            R.sp_pads(nc, sp, zeros, cleared)

        @block.tensor
        def _(pe):
            def flip(s):
                pe.wait_ge(normed, s + 1)
                for j in range(ST):
                    last = nc.tensor.transpose(psA[:, 1, j * P:(j + 1) * P], xn[:, j, :], k.ident[:, :])
                last.then_inc(flipped, 1)

            def conv(s, g):
                c, dt = g // 2, g % 2
                if g == 0:
                    pe.wait_ge(turned, s + 1)
                elif g < 2 * DT:
                    pe.wait_ge(emptied, s * 6 + g)
                else:
                    pe.wait_ge(v_ready, s + 1)
                o = psA[:, g % 2, :]
                if g < 2 * DT:
                    for t in range(TAPS):
                        back = (TAPS - 1 - t) * (c + 1)
                        last = nc.tensor.matmul(o, Wtap[:, c, t, dt * P:(dt + 1) * P], hT[:, PAD - back:PAD - back + SEQ], start=(t == 0), stop=(t == TAPS - 1))
                else:
                    last = nc.tensor.matmul(o, Win[:, INNER + dt * P:INNER + (dt + 1) * P], hT[:, PAD:PAD + SEQ], start=True, stop=True)
                last.then_inc(fronted, 1)

            def project(s, b):
                pe.wait_ge(emptied, s * 6 + 4)
                pe.wait_ge(mixed, s + 1)
                for dt in range(DT):
                    nc.tensor.matmul(psA[0:RANK, 0, :], Wx[:, dt, 0:RANK], xc[:, b, dt, :], start=(dt == 0), stop=(dt == DT - 1))
                for dt in range(DT):
                    last = nc.tensor.matmul(psA[0:96, 1, :], Wx[:, dt, RANK:RANK + 96], xc[:, b, dt, :], start=(dt == 0), stop=(dt == DT - 1))
                last.then_inc(projected, 1)

            def steps(s):
                pe.wait_ge(low_ready, s + 1)
                pe.wait_ge(cut, s + 1)
                for dt in range(DT):
                    last = nc.tensor.matmul(psA[:, dt, :], Wdt[:, dt * P:(dt + 1) * P], low[:, :], start=True, stop=True)
                last.then_inc(dt_summed, 1)

            def out(s):
                pe.wait_ge(y_ready, s + 1)
                for j in range(ST):
                    for dt in range(DT):
                        last = nc.tensor.matmul(psA[:, 0, j * P:(j + 1) * P], v[:, dt, j * P:(j + 1) * P], Wout[:, dt, :], start=(dt == 0), stop=(dt == DT - 1))
                last.then_inc(out_summed, 1)

            def spread_B(s, b, n, waits=True):
                if waits:
                    pe.wait_ge(dBx_done, s * NB + n - 1)
                nc.tensor.matmul(psB[:, n % 2, :], k.pick[:, n, :], bc3[:, b, :], start=True, stop=True).then_inc(B_ready, 1)

            def spread_C(s, b, n, waits=True):
                if waits:
                    pe.wait_ge(Cs_ready, s * NB + n)
                nc.tensor.matmul(psC[:, :], k.pick[:, STATES + n, :], bc3[:, b, :], start=True, stop=True).then_inc(C_ready, 1)

            def main(s, b, n, first):
                if n == 0:
                    spread_C(s, b, 0, not first)
                    for i in range(2):
                        spread_B(s, b, i, not first)
                if n + 1 < NB:
                    spread_C(s, b, n + 1)
                pe.wait_ge(hc_ready, s * NB + n + 1)
                if n == 0 and not first:
                    pe.wait_ge(y_emptied, s)
                for dt in range(DT):
                    last = nc.tensor.matmul(psY[:, dt, :], k.ident[:, :], HC[:, n % RP, dt, :], start=(n == 0), stop=(n == NB - 1))
                last.then_inc(y_summed, 1)
                if n + 2 < NB:
                    spread_B(s, b, n + 2)

            def between(s, b, turn, n, first, last):
                if not first:
                    if n == 2:
                        out(s - 1)
                    if n == 7:
                        R.pe_1(nc, pe, s - 1, 1 - b)
                    if n == 12:
                        R.pe_2(nc, pe, s - 1, 1 - b)
                if not last:
                    if n == 3:
                        flip(s + 1)
                        if not first:
                            pe.wait_ge(added, s)
                    if 3 <= n < 7:
                        conv(s + 1, n - 3)
                    if n == 8:
                        project(s + 1, 1 - b)
                    if n == 10:
                        steps(s + 1)
                    if n == 13:
                        conv(s + 1, 4)
                        conv(s + 1, 5)

            pe.wait_ge(setup, 1)
            flip(0)
            for g in range(4):
                conv(0, g)
            project(0, 0)
            steps(0)
            conv(0, 4)
            conv(0, 5)
            pe.wait_ge(ux_ready, 1)
            run(pe, main, between)
            out(BATCH - 1)
            R.pe_1(nc, pe, BATCH - 1, 1)
            R.pe_2(nc, pe, BATCH - 1, 1)

        @block.scalar
        def _(act):
            def to_hT(s):
                act.wait_ge(flipped, s + 1)
                nc.scalar.activation(hT[:, PAD:], psA[:, 1, :], ACT.Copy).then_inc(turned, 1)

            def empty(s, b, g):
                c, dt = g // 2, g % 2
                act.wait_ge(fronted, s * 6 + g + 1)
                if g < 4:
                    nc.scalar.activation(pre[:, g, :], psA[:, g % 2, :], ACT.Identity, bias=col[:, dt, c:c + 1]).then_inc(emptied, 1)
                else:
                    nc.scalar.activation(zs[:, b, dt, :], psA[:, g % 2, :], ACT.Copy).then_inc(emptied, 1)

            def silu(s):
                act.wait_ge(emptied, s * 6 + 4)
                nc.scalar.activation(pre[:, :, :], pre[:, :, :], ACT.Silu).then_inc(silu_done, 1)

            def silu_z(s, b):
                act.wait_ge(emptied, s * 6 + 6)
                nc.scalar.activation(zs[:, b, :, :], zs[:, b, :, :], ACT.Silu).then_inc(z_done, 1)

            def to_low(s):
                act.wait_ge(projected, s + 1)
                nc.scalar.activation(low[:, :], psA[0:RANK, 0, :], ACT.Copy).then_inc(low_ready, 1)

            def soften(s):
                act.wait_ge(dt_summed, s + 1)
                for dt in range(DT):
                    last = nc.scalar.activation(v[:, dt, :], psA[:, dt, :], ACT.Identity, bias=col[:, dt, 2:3])
                last.then_inc(v_ready, 1)
                act.wait_ge(v_ready, s + 1)
                nc.scalar.activation(absv[:, :, :], v[:, :, :], ACT.Abs).then_inc(abs_ready, 1)
                act.wait_ge(abs_ready, s + 1)
                nc.scalar.activation(soft[:, :, :], absv[:, :, :], ACT.Exp, scale=-1.0).then_inc(u_ready, 1)
                act.wait_ge(u_ready, s + 1)
                nc.scalar.activation(absv[:, :, :], soft[:, :, :], ACT.Ln, bias=1.0).then_inc(l_ready, 1)

            def main(s, b, n, first):
                if n == 0:
                    act.wait_ge(delta_ready, s + 1)
                if n >= RA or not first:
                    act.wait_ge(h_ready, s * NB + n - RA + 1)
                for dt in range(DT):
                    last = nc.scalar.activation(dA[:, n % RA, dt, 1:], delta[:, b, dt, 1:], ACT.Exp, scale=A[:, dt, n:n + 1])
                last.then_inc(dA_ready, 1)
                if n >= RC or not first:
                    act.wait_ge(hc_ready, s * NB + n - RC + 1)
                act.wait_ge(C_ready, s * NB + n + 1)
                nc.scalar.activation(Cs[:, n % RC, 0, :], psC[:, :], ACT.Copy).then_inc(Cs_ready, 1)

            def between(s, b, turn, n, first, last):
                if not first:
                    if n == 5:
                        R.norm.act_root(nc, act, s - 1)
                    if n == 8:
                        R.act_1(nc, act, s - 1, 1 - b)
                    if n == 10:
                        R.act_2(nc, act, s - 1)
                if not last:
                    if n == 1:
                        N.act_root(nc, act, s + 1)
                    if n == 3:
                        to_hT(s + 1)
                    if 4 <= n < 8:
                        empty(s + 1, 1 - b, n - 4)
                    if n == 7:
                        silu(s + 1)
                    if n == 9:
                        to_low(s + 1)
                    if n == 11:
                        soften(s + 1)
                    if n == 14:
                        empty(s + 1, 1 - b, 4)
                        empty(s + 1, 1 - b, 5)
                        silu_z(s + 1, 1 - b)

            act.wait_ge(loaded, 7 * 16)
            nc.scalar.activation(A[:, :, :], col[:, :, 4:], ACT.Exp).then_inc(exp_ready, 1)
            act.wait_ge(loose, 2)
            nc.scalar.activation(gates[:, :], gates[:, :], ACT.Exp).then_inc(exp_ready, 1)
            act.wait_ge(setup, 1)
            N.act_root(nc, act, 0)
            to_hT(0)
            for g in range(4):
                empty(0, 0, g)
            silu(0)
            to_low(0)
            soften(0)
            empty(0, 0, 4)
            empty(0, 0, 5)
            silu_z(0, 0)
            act.preload_act_table_set("natural_log_exp_and_others")
            run(act, main, between)
            R.norm.act_root(nc, act, BATCH - 1)
            R.act_1(nc, act, BATCH - 1, 1)
            R.act_2(nc, act, BATCH - 1)

        def product(eng, s, n, first):
            eng.wait_ge(h_ready, s * NB + n + 1)
            eng.wait_ge(Cs_ready, s * NB + n + 1)
            if n >= 1 or not first:
                eng.wait_ge(hc_ready, s * NB + n)
            if n >= RP or not first:
                eng.wait_ge(y_summed, s * NB + n - RP + 1)
            eng.tensor_tensor(HC[:, n % RP, :, :], H[:, n % RH, :, :], Cs[:, n % RC, :, :].to_broadcast([P, DT, SEQ]), ALU.mult).then_inc(hc_ready, 1)

        @block.gpsimd
        def _(pool):
            def main(s, b, n, first):
                if not on_dve(n):
                    product(nc.gpsimd, s, n, first)

            def between(s, b, turn, n, first, last):
                if n == 6 and not last:
                    G.pool(pool, s + 2, b)
                if n == NB - 1 and not first:
                    R.pool(pool, s - 1, 1 - b)

            R.pool_start(pool)
            G.pool_start(pool)
            G.pool(pool, 0, 0)
            G.pool(pool, 1, 1)
            run(pool, main, between)
            R.pool(pool, BATCH - 1, 1)
            for i in range(8):
                pool.wait_ge(G.gathered[i], (BATCH // 2 + 1) * 16)

        @block.vector
        def _(dve):
            chain = Chain(dve, linked)

            def stats(s, b, turn):
                G.dve(nc, dve, chain, s, b, turn)
                N.dve_stats(nc, chain, s)

            def normalize(s):
                N.dve_finish(nc, dve, chain, s)
                N.dve_apply(nc, xn, s).then_inc(normed, 1)

            def mix(s, b):
                dve.wait_ge(silu_done, s + 1)
                chain(nc.vector.tensor_scalar(xc[:, b, :, :], pre[:, 0:2, :], gates[:, 0:1], None, ALU.mult))
                nc.vector.scalar_tensor_tensor(out=xc[:, b, :, :], in0=pre[:, 2:4, :], scalar=gates[:, 1:2], in1=xc[:, b, :, :],
                                               op0=ALU.mult, op1=ALU.add).then_inc(mixed, 1)

            def cut_rows(s, b):
                dve.wait_ge(projected, s + 1)
                c3 = bc3[:, b, :]
                chain(nc.vector.tensor_copy(c3, psA[0:96, 1, :]))
                chain(nc.vector.tensor_tensor(bc[0:64, :], psA[0:64, 1, :], bc3[0:64, b, :], ALU.subtract))
                chain(nc.vector.tensor_copy(bc3[0:64, b, :], bc[0:64, :]))
                chain(nc.vector.tensor_tensor(bc[0:32, :], bc[0:32, :], bc3[0:32, b, :], ALU.subtract))
                nc.vector.tensor_copy(bc3[0:32, b, :], bc[0:32, :]).then_inc(cut, 1)

            def step_sizes(s, b):
                dve.wait_ge(u_ready, s + 1)
                nc.vector.tensor_scalar(v[:, :, :], v[:, :, :], 0.0, None, ALU.max)
                chain(nc.vector.tensor_scalar(rest[:, :, :], soft[:, :, :], 1.0, None, ALU.add))
                chain(nc.vector.tensor_scalar(rest[:, :, :], rest[:, :, :], -1.0, None, ALU.add))
                chain(nc.vector.tensor_tensor(rest[:, :, :], soft[:, :, :], rest[:, :, :], ALU.subtract))
                dve.wait_ge(l_ready, s + 1)
                chain(nc.vector.tensor_tensor(rest[:, :, :], rest[:, :, :], absv[:, :, :], ALU.add))
                nc.vector.tensor_tensor(delta[:, b, :, :], rest[:, :, :], v[:, :, :], ALU.add).then_inc(delta_ready, 1)
                dve.wait_ge(delta_ready, s + 1)
                nc.vector.tensor_tensor(ux[:, b, :, :], delta[:, b, :, :], xc[:, b, :, :], ALU.mult).then_inc(ux_ready, 1)

            def gated(s, b):
                dve.wait_ge(y_summed, s * NB + NB)
                for dt in range(DT):
                    last = nc.vector.scalar_tensor_tensor(out=v[:, dt, :], in0=xc[:, b, dt, :], scalar=col[:, dt, 3:4], in1=psY[:, dt, :], op0=ALU.mult, op1=ALU.add)
                last.then_inc(y_emptied, 1)
                dve.wait_ge(y_emptied, s + 1)
                dve.wait_ge(z_done, s + 1)
                nc.vector.tensor_tensor(v[:, :, :], v[:, :, :], zs[:, b, :, :], ALU.mult).then_inc(y_ready, 1)

            def add(s):
                dve.wait_ge(out_summed, s + 1)
                four = k.X[:, bass.ds(s * ST, ST), :]
                nc.vector.tensor_tensor(four, four, psA[:, 0, :].rearrange("p (a d) -> p a d", a=ST), ALU.add).then_inc(added, 1)

            def main(s, b, n, first):
                if n == 0:
                    dve.wait_ge(ux_ready, s + 1)
                dve.wait_ge(B_ready, s * NB + n + 1)
                nc.vector.tensor_tensor(dBx[:, n % RB, :, :], ux[:, b, :, :], psB[:, n % 2:n % 2 + 1, :].to_broadcast([P, DT, SEQ]), ALU.mult).then_inc(dBx_done, 1)
                dve.wait_ge(dBx_done, s * NB + n + 1)
                dve.wait_ge(dA_ready, s * NB + n + 1)
                if n >= RH or not first:
                    dve.wait_ge(hc_ready, s * NB + n - RH + 1)
                flat = lambda v, r: v[:, n % r, :, :].rearrange("p a t -> p (a t)")
                nc.vector.tensor_tensor_scan(flat(H, RH), flat(dA, RA), flat(dBx, RB), 0.0, ALU.mult, ALU.add).then_inc(h_ready, 1)
                if on_dve(n):
                    product(nc.vector, s, n, first)

            def between(s, b, turn, n, first, last):
                if not first:
                    if n == 1:
                        gated(s - 1, 1 - b)
                    if n == 3:
                        add(s - 1)
                    if n == 4:
                        dve.wait_ge(added, s)
                        R.norm.dve_stats(nc, chain, s - 1)
                    if n == 6:
                        R.dve_1(nc, dve, chain, s - 1, 1 - b, turn - 1 + b)
                    if n == 9:
                        R.dve_2a(nc, dve, chain, s - 1, 1 - b)
                    if n == 11:
                        R.dve_2b(nc, dve, chain, s - 1, 1 - b)
                    if n == 14:
                        R.dve_2c(nc, dve, chain, s - 1, 1 - b)
                if not last:
                    if n == 0:
                        stats(s + 1, 1 - b, turn + b)
                    if n == 2:
                        normalize(s + 1)
                    if n == 8:
                        mix(s + 1, 1 - b)
                    if n == 9:
                        cut_rows(s + 1, 1 - b)
                    if n == 12:
                        step_sizes(s + 1, 1 - b)

            dve.wait_ge(loaded, 7 * 16)
            nc.vector.tensor_reduce(gmax[:, :], gates[:, :], AX.X, ALU.max).then_inc(loose, 1)
            dve.wait_ge(loose, 1)
            nc.vector.tensor_scalar(gates[:, :], gates[:, :], gmax[:, :], None, ALU.subtract).then_inc(loose, 1)
            dve.wait_ge(exp_ready, 2)
            chain(nc.vector.tensor_reduce(gmax[:, :], gates[:, :], AX.X, ALU.add))
            chain(nc.vector.reciprocal(gmax[:, :], gmax[:, :]))
            chain(nc.vector.tensor_scalar(gates[:, :], gates[:, :], gmax[:, :], None, ALU.mult))
            nc.vector.tensor_scalar(A[:, :, :], A[:, :, :], -1.0, None, ALU.mult)
            for r in range(1, 3):
                chain(nc.vector.tensor_copy(Wx[:, :, RANK + 32 * r:RANK + 32 * r + 32], Wx[:, :, RANK:RANK + 32]))
            for c in range(2):
                for t in range(TAPS):
                    chain(nc.vector.tensor_tensor(Wtap[:, c, t, :], Win[:, 0:INNER], tap[:, c, t, :], ALU.mult))
            nc.vector.memset(hT[:, 0:PAD], 0.0)
            for r in range(RA):
                nc.vector.memset(dA[:, r, :, 0:1], 0.0)
            nc.vector.memset(R.run[:, :], 0.0).then_inc(setup, 1)
            dve.wait_ge(setup, 1)
            for b in range(2):
                G.dve_ask(nc, b, b)
            stats(0, 0, 0)
            normalize(0)
            mix(0, 0)
            cut_rows(0, 0)
            step_sizes(0, 0)
            links = (2 + 4) + 4 + 4 + sum(R.links()) + 1 + 4 + 4
            run(dve, main, between, chain, 2 * links)
            s, b = BATCH - 1, 1
            gated(s, b)
            add(s)
            dve.wait_ge(added, BATCH)
            nc.vector.memset(zeros, 0.0).then_inc(cleared, 1)
            R.norm.dve_stats(nc, chain, s)
            R.dve_1(nc, dve, chain, s, b, s // 2)
            R.dve_2a(nc, dve, chain, s, b)
            R.dve_2b(nc, dve, chain, s, b)
            R.dve_2c(nc, dve, chain, s, b)
            R.dve_tables(nc, dve, chain, st)


def macaron_kernel(nc, x, consts, l0_pack, l1_pack, wqkv, l0_bg, l0_wg, l1_wg, gamma, beta, w_in, taps, w_x, w_dt, w_out, col, conv_gates, out):
    k = Core()
    with ExitStack() as ctx:
        sb = lambda n, s, t=F32: ctx.enter_context(nc.sbuf_tensor(n, s, t))
        k.X = sb("X", [P, TILES, D])
        k.ident = sb("ident", [P, P])
        k.ident_bf = sb("ident_bf", [P, P], BF16)
        k.before = sb("before", [P, P], BF16)
        k.causal = sb("causal", [P, P], BF16)
        k.ones = sb("ones", [P, P], BF16)
        k.pick = sb("pick", [96, 2 * STATES, P], BF16)
        k.small = sb("small", [P, SMALL])
        k.bg = sb("bg", [P, EXPERTS])
        k.gate_w = sb("gate_w", [P, 2, EXPERTS])
        k.gamma, k.beta = sb("gamma", [P, D]), sb("beta", [P, D])
        k.gate = sb("gate", [P, TOPK, TILES])
        k.hot = sb("hot", [P, TILES, TOPK * EXPERTS])
        k.row = sb("row", [P, TILES, TOPK])
        k.idx = sb("idx", [P, TILES + 2 * SEQ_TILES, TOPK], I32)
        k.pad_row = sb("pad_row", [P, EXPERTS], I32)
        k.block_row = sb("block_row", [P, NBLK], I32)
        k.owner = sb("owner", [P, NBLK], I32)
        k.xslots = nc.dram_tensor("xslots", [DUMP + BLOCK, D], F32, kind="Internal").ap()
        k.yslots = nc.dram_tensor("yslots", [TRASH + 1, D], F32, kind="Internal").ap()

        load_stage(nc, k, x, consts, l0_bg, (l0_wg, l1_wg), gamma, beta)
        plain_stage(nc, k, "to_a", False, True)
        blocks_stage(nc, k, "a", l0_pack, ACT.Gelu_apprx_tanh)
        attention_stage(nc, k, wqkv)
        blocks_stage(nc, k, "b", l0_pack, ACT.Gelu_apprx_tanh)
        plain_stage(nc, k, "to_c", True, False)
        blocks_stage(nc, k, "c", l1_pack, ACT.Gelu)
        scan_stage(nc, k, {"in": w_in, "taps": taps, "x": w_x, "dt": w_dt, "out": w_out, "col": col, "gates": conv_gates})
        blocks_stage(nc, k, "d", l1_pack, ACT.Gelu)
        plain_stage(nc, k, "end", True, None, out)


def kernel(**inputs):
    import numpy as np
    import concourse.bacc as bacc
    from concourse.bass_utils import run_bass_kernel_spmd as run

    a = {n: np.asarray(v) for n, v in inputs.items()}

    def pack(w1, b1, w2, b2):
        return np.concatenate([w1, w2.reshape(EXPERTS, FT, P, D).transpose(0, 2, 1, 3).reshape(EXPERTS, P, FT * D),
                               b1.reshape(EXPERTS, FT, P).transpose(0, 2, 1), b2.reshape(EXPERTS, D, 1)], axis=2)

    r, c = np.arange(P)[:, None], np.arange(P)[None, :]
    consts = np.zeros((P, 36 * P + SMALL), np.float32)
    consts[:, 0:P] = r == c
    consts[:, P:2 * P] = r < c
    consts[:, 2 * P:3 * P] = np.where(c > r, NEG, 0.0)
    consts[:, 3 * P:4 * P] = r == c
    for n in range(32):
        consts[:96, (4 + n) * P:(5 + n) * P] = (np.arange(96) % 32 == n)[:, None]
    e = np.arange(EXPERTS)
    middle = e * REGION + TOKENS
    consts[:, 36 * P:] = np.concatenate([EXPERTS - e, np.repeat([-1, 1], EXPERTS), middle - 1, middle, middle, e, np.arange(NBLK)])
    two = lambda v: v.reshape(DT, P, -1).transpose(1, 0, 2)
    rows = lambda n: a[f"L1_attn_{n}"].reshape(INNER, -1)
    arrays = {
        "x": a["L0_attn_x"].reshape(TOKENS, D),
        "consts": consts,
        "l0_pack": pack(a["L0_ffn_W1"], a["L0_ffn_b1"], a["L0_ffn_W2"], a["L0_ffn_b2"]),
        "l1_pack": pack(a["L1_ffn_w1"], a["L1_ffn_b1"], a["L1_ffn_w2"], a["L1_ffn_b2"]),
        "wqkv": np.stack([a["L0_attn_WQ"].T, a["L0_attn_WK"].T, a["L0_attn_WV"].T], axis=1),
        "l0_bg": a["L0_ffn_bg"], "l0_wg": a["L0_ffn_Wg"], "l1_wg": a["L1_ffn_gate_w"],
        "gamma": a["L1_ffn_gamma"], "beta": a["L1_ffn_beta"],
        "w_in": a["L1_attn_W_in"].T,
        "taps": np.stack([a["L1_attn_conv_w1"].T, a["L1_attn_conv_w2"].T])[None],
        "w_x": two(a["L1_attn_W_x"].T), "w_dt": a["L1_attn_W_dt"].T, "w_out": two(a["L1_attn_W_out"].T),
        "col": two(np.concatenate([rows("conv_b1"), rows("conv_b2"), rows("b_dt"), rows("D_param"), rows("A_log")], axis=1)),
        "conv_gates": a["L1_attn_conv_gates"],
    }
    nc = bacc.Bacc("TRN2", target_bir_lowering=False, num_devices=1)
    given, args = {}, []
    for name, v in arrays.items():
        v = np.ascontiguousarray(v)
        given[f"in_{name}"] = v
        args.append(nc.dram_tensor(f"in_{name}", v.shape, mybir.dt.from_np(v.dtype), kind="ExternalInput").ap())
    args.append(nc.dram_tensor("out", (TOKENS, D), F32, kind="ExternalOutput").ap())
    macaron_kernel(nc, *args)
    return run(nc, [given], core_ids=[0]).results[0]["out"].reshape(BATCH, SEQ, D)
```

```python
import concourse.bass as bass
from concourse import mybir
from contextlib import ExitStack

F32 = mybir.dt.float32
BF16 = mybir.dt.bfloat16
I32 = mybir.dt.int32
U32 = mybir.dt.uint32
ALU = mybir.AluOpType
ACT = mybir.ActivationFunctionType
AX = mybir.AxisListType

P = 128
BATCH, SEQ, D = 16, 512, 128
TOKENS = BATCH * SEQ
TILES = TOKENS // P
SEQ_TILES = SEQ // P
GROUPS = TILES // 4
EXPERTS, TOPK, HIDDEN = 8, 2, 512
FT = HIDDEN // P
BLOCK = 512
CAPACITY = -(-12 * TOKENS * TOPK // (10 * EXPERTS))
NBLK = TOKENS * TOPK // BLOCK + EXPERTS
REGION = 2 * TOKENS + BLOCK
DUMP = EXPERTS * REGION
TRASH = NBLK * BLOCK
SIGN = EXPERTS
BASE = SIGN + TOPK * EXPERTS
MIDDLE = BASE + TOPK * EXPERTS
EIGHT = MIDDLE + EXPERTS
NUMBER = EIGHT + EXPERTS
SMALL = NUMBER + NBLK
PACK = HIDDEN + FT * D + FT
EPS = 1e-5
NEG = -1e30
SCALE = D ** -0.5
INNER, STATES, RANK, TAPS = 256, 16, 64, 4
DT = INNER // P
PAD = 2 * (TAPS - 1)


class Chain:

    def __init__(self, eng, sem):
        self.eng, self.sem, self.n, self.base = eng, sem, 0, None

    def turn(self, i, per, turns):
        self.base, self.start, self.per, self.turns = i * per, self.n, per, turns

    def leave(self):
        assert self.n - self.start == self.per, (self.n - self.start, self.per)
        self.n = self.start + self.per * self.turns
        self.base = None

    def __call__(self, ins):
        ins.then_inc(self.sem, 1)
        self.n += 1
        self.eng.wait_ge(self.sem, self.n if self.base is None else self.base + self.n)


class Core:
    pass


class Stage:

    def __init__(self, nc, name):
        self.nc, self.name, self.ctx, self.sems = nc, name, ExitStack(), []

    def sem(self, n):
        self.sems.append(self.nc.alloc_semaphore(f"{self.name}_{n}"))
        return self.sems[-1]

    def sb(self, n, shape, dtype=F32):
        return self.ctx.enter_context(self.nc.sbuf_tensor(f"{self.name}_{n}", shape, dtype))

    def pb(self, n, shape, dtype=F32):
        return self.ctx.enter_context(self.nc.psum_tensor(f"{self.name}_{n}", shape, dtype))

    def block(self):
        return self.ctx.enter_context(self.nc.Block())

    def __enter__(self):
        return self

    def __exit__(self, *error):
        self.ctx.__exit__(*error)
        if error[0] is None:
            self.nc.clear_and_free_semaphores(self.sems)
            self.nc.all_engine_barrier()


def rows_of(x, t, n=1):
    v = x[:, bass.ds(t, n), :]
    return v.rearrange("p a d -> p (a d)") if n == 1 else v


def sequences(eng, body, chain=None, links=0):
    turns = (BATCH - 4) // 2
    for s in range(3):
        body(s, s % 2, s // 2, s == 0, False)
    with eng.Fori(0, turns) as i:
        if chain is not None:
            chain.turn(i, links, turns)
        body(i * 2 + 3, 1, i + 1, False, False)
        body(i * 2 + 4, 0, i + 2, False, False)
        if chain is not None:
            chain.leave()
    body(BATCH - 1, 1, BATCH // 2 - 1, False, True)


class Norm:

    def __init__(self, st, k, name, double=False):
        self.k, self.w = k, 2 if double else 1
        self.asked, self.logged, self.rooted, self.begun = (st.sem(f"{name}_{n}") for n in ("asked", "logged", "rooted", "begun"))
        self.stats = st.sb(f"{name}_stats", [P, 4, 6])
        self.mean, self.odd, self.var = (st.sb(f"{name}_{n}", [P, 4]) for n in ("mean", "odd", "var"))
        self.shifted, self.root, self.newton, self.rstd = (st.sb(f"{name}_{n}", [P, self.w, 4]) for n in ("shifted", "root", "newton", "rstd"))

    def dve_stats(self, nc, chain, s):
        chain.eng.sem_inc(self.begun, 1)
        st, m, o, v = self.stats, self.mean, self.odd, self.var
        for j in range(4):
            last = nc.vector.bn_stats(st[:, j, :], rows_of(self.k.X, s * 4 + j))
        chain(last)
        nc.vector.tensor_tensor(m[:, :], st[:, :, 1], st[:, :, 4], ALU.add)
        nc.vector.tensor_tensor(v[:, :], st[:, :, 2], st[:, :, 5], ALU.add)
        chain(nc.vector.tensor_tensor(o[:, :], st[:, :, 1], st[:, :, 4], ALU.subtract))
        nc.vector.tensor_scalar(m[:, :], m[:, :], 0.5, None, ALU.mult)
        chain(nc.vector.scalar_tensor_tensor(out=o[:, :], in0=o[:, :], scalar=0.25, in1=o[:, :], op0=ALU.mult, op1=ALU.mult))
        chain(nc.vector.scalar_tensor_tensor(out=v[:, :], in0=v[:, :], scalar=1.0 / D, in1=o[:, :], op0=ALU.mult, op1=ALU.add))
        last = nc.vector.tensor_scalar(self.shifted[:, 0, :], v[:, :], EPS, None, ALU.add)
        if self.w == 2:
            last = nc.vector.tensor_scalar(self.shifted[:, 1, :], v[:, :], 1.0 + EPS, EPS * EPS, ALU.mult, ALU.add)
        last.then_inc(self.asked, 1)

    def act_root(self, nc, act, s):
        act.wait_ge(self.asked, s + 1)
        nc.scalar.activation(self.root[:, :, :], self.shifted[:, :, :], ACT.Ln).then_inc(self.logged, 1)
        act.wait_ge(self.logged, s + 1)
        nc.scalar.activation(self.root[:, :, :], self.root[:, :, :], ACT.Exp, scale=-0.5).then_inc(self.rooted, 1)

    def dve_finish(self, nc, dve, chain, s):
        dve.wait_ge(self.rooted, s + 1)
        chain(nc.vector.tensor_tensor(self.newton[:, :, :], self.root[:, :, :], self.root[:, :, :], ALU.mult))
        chain(nc.vector.tensor_tensor(self.newton[:, :, :], self.newton[:, :, :], self.shifted[:, :, :], ALU.mult))
        chain(nc.vector.tensor_scalar(self.newton[:, :, :], self.newton[:, :, :], -0.5, 1.5, ALU.mult, ALU.add))
        chain(nc.vector.tensor_tensor(self.rstd[:, :, :], self.root[:, :, :], self.newton[:, :, :], ALU.mult))

    def dve_apply(self, nc, out, s):
        for j in range(4):
            last = nc.vector.tensor_scalar(out[:, j, :], rows_of(self.k.X, s * 4 + j), self.mean[:, j:j + 1],
                                           self.rstd[:, self.w - 1, j:j + 1], ALU.subtract, ALU.mult)
        return last


class Router:

    def __init__(self, st, k, first, psT, psL, psP):
        self.k, self.first, self.psT, self.psL, self.psP = k, first, psT, psL, psP
        self.norm = Norm(st, k, "r", double=not first)
        self.normed, self.flipped, self.turned, self.scored, self.centred = map(st.sem, ("r_normed", "r_flipped", "r_turned", "r_scored", "r_centred"))
        self.exped, self.chosen, self.placed, self.rowed, self.taken = map(st.sem, ("r_exped", "r_chosen", "r_placed", "r_rowed", "r_taken"))
        self.scattered = [st.sem(f"r_scattered{i}") for i in range(16)]
        self.zeroed, self.tabled = st.sem("r_zeroed"), st.sem("r_tabled")
        self.xn = st.sb("r_xn", [P, 2, 4, D])
        self.xnT = st.sb("r_xnT", [P, BLOCK])
        self.L, self.prob, self.work = (st.sb(f"r_{n}", [P, 4, EXPERTS]) for n in ("L", "prob", "work"))
        self.top, self.inv = st.sb("r_top", [P, 4]), st.sb("r_inv", [P, 4])
        self.pv = st.sb("r_pv", [P, 2, 4])
        self.hot_bf = st.sb("r_hot_bf", [P, 4, TOPK * EXPERTS], BF16)
        self.pos = st.sb("r_pos", [P, 4, TOPK * EXPERTS])
        self.run = st.sb("r_run", [P, TOPK * EXPERTS])
        self.row = st.sb("r_row", [P, 4, TOPK])
        self.idx = st.sb("r_idx", [P, 2, 4 * TOPK], I32)

    def four(self, s):
        return bass.ds(s * 4, 4)

    def dve_1(self, nc, dve, chain, s, b, turn):
        k, n = self.k, self.norm
        n.dve_finish(nc, dve, chain, s)
        if not (isinstance(turn, int) and turn == 0):
            for i in range(8):
                dve.wait_ge(self.scattered[8 * b + i], turn * 16)
        last = n.dve_apply(nc, self.xn[:, b, :, :], s)
        if not self.first:
            xn = self.xn[:, b, :, :]
            chain(last)
            chain(nc.vector.tensor_tensor(xn, xn, k.gamma[:, :].rearrange("p (a d) -> p a d", a=1).to_broadcast([P, 4, D]), ALU.mult))
            last = nc.vector.tensor_tensor(xn, xn, k.beta[:, :].rearrange("p (a d) -> p a d", a=1).to_broadcast([P, 4, D]), ALU.add)
        last.then_inc(self.normed, 1)
        if not self.first:
            chain(nc.vector.scalar_tensor_tensor(out=n.mean[:, :], in0=n.mean[:, :], scalar=-0.5, in1=n.rstd[:, 0, :], op0=ALU.mult, op1=ALU.mult))
            chain(nc.vector.tensor_scalar(n.rstd[:, 0, :], n.rstd[:, 0, :], 0.5, 1.0, ALU.mult, ALU.add))
            for j in range(4):
                x = rows_of(k.X, s * 4 + j)
                last = nc.vector.tensor_scalar(x, x, n.rstd[:, 0, j:j + 1], n.mean[:, j:j + 1], ALU.mult, ALU.add)
            chain(last)

    def pe_1(self, nc, pe, s, b):
        self.pe_1a(nc, pe, s, b)
        self.pe_1b(nc, pe, s, b)

    def pe_1a(self, nc, pe, s, b):
        psT = self.psT(b)
        pe.wait_ge(self.normed, s + 1)
        for j in range(4):
            last = nc.tensor.transpose(psT[:, j * P:(j + 1) * P], self.xn[:, b, j, :], self.k.ident[:, :])
        last.then_inc(self.flipped, 1)

    def pe_1b(self, nc, pe, s, b):
        psL = self.psL(b)
        pe.wait_ge(self.turned, s + 1)
        for j in range(4):
            last = nc.tensor.matmul(psL[:, j * EXPERTS:(j + 1) * EXPERTS], self.xnT[:, j * P:(j + 1) * P], self.k.gate_w[:, 0 if self.first else 1, :], start=True, stop=True)
        last.then_inc(self.scored, 1)

    def act_1(self, nc, act, s, b):
        act.wait_ge(self.flipped, s + 1)
        nc.scalar.activation(self.xnT[:, :], self.psT(b), ACT.Copy).then_inc(self.turned, 1)

    def wide(self, v):
        return v.rearrange("p (t a) -> p t a", a=1).to_broadcast([P, 4, EXPERTS])

    def dve_2a(self, nc, dve, chain, s, b):
        L, psL = self.L, self.psL(b)[:, 0:4 * EXPERTS].rearrange("p (t e) -> p t e", t=4)
        dve.wait_ge(self.scored, s + 1)
        if self.first:
            chain(nc.vector.tensor_tensor(L[:, :, :], psL, self.k.bg[:, :].rearrange("p (a e) -> p a e", a=1).to_broadcast([P, 4, EXPERTS]), ALU.add))
        else:
            chain(nc.vector.tensor_copy(L[:, :, :], psL))
        chain(nc.vector.tensor_reduce(self.top[:, :], L[:, :, :], AX.X, ALU.max))
        nc.vector.tensor_tensor(L[:, :, :], L[:, :, :], self.wide(self.top[:, :]), ALU.subtract).then_inc(self.centred, 1)

    def act_2(self, nc, act, s):
        act.wait_ge(self.centred, s + 1)
        nc.scalar.activation(self.prob[:, :, :], self.L[:, :, :], ACT.Exp).then_inc(self.exped, 1)

    def dve_2b(self, nc, dve, chain, s, b):
        k, prob, work = self.k, self.prob, self.work
        hot = k.hot[:, self.four(s), :]
        rank = k.small[:, 0:EXPERTS].rearrange("p (a e) -> p a e", a=1).to_broadcast([P, 4, EXPERTS])
        dve.wait_ge(self.exped, s + 1)
        for c in range(TOPK):
            h = hot[:, :, c * EXPERTS:(c + 1) * EXPERTS]
            chain(nc.vector.tensor_reduce(self.pv[:, c, :], prob[:, :, :], AX.X, ALU.max))
            chain(nc.vector.tensor_tensor(work[:, :, :], prob[:, :, :], self.wide(self.pv[:, c, :]), ALU.is_equal))
            chain(nc.vector.tensor_tensor(work[:, :, :], work[:, :, :], rank, ALU.mult))
            chain(nc.vector.tensor_reduce(self.top[:, :], work[:, :, :], AX.X, ALU.max))
            chain(nc.vector.tensor_tensor(h, work[:, :, :], self.wide(self.top[:, :]), ALU.is_equal))
            if c == 0:
                chain(nc.vector.scalar_tensor_tensor(out=prob[:, :, :], in0=h, scalar=-4.0, in1=prob[:, :, :], op0=ALU.mult, op1=ALU.add))
        nc.vector.tensor_scalar(self.hot_bf[:, :, :], hot, 1.0, None, ALU.mult).then_inc(self.chosen, 1)
        chain(nc.vector.tensor_tensor(self.inv[:, :], self.pv[:, 0, :], self.pv[:, 1, :], ALU.add))
        chain(nc.vector.reciprocal(self.inv[:, :], self.inv[:, :]))
        for c in range(TOPK):
            nc.vector.scalar_tensor_tensor(out=k.gate[:, c, self.four(s)], in0=self.pv[:, c, :], scalar=0.5, in1=self.inv[:, :], op0=ALU.mult, op1=ALU.mult)

    def pe_2(self, nc, pe, s, b):
        psP, W = self.psP(b), TOPK * EXPERTS
        pe.wait_ge(self.chosen, s + 1)
        for j in range(5):
            for i in range(j):
                last = nc.tensor.matmul(psP[:, j * W:(j + 1) * W], self.k.ones[:, :], self.hot_bf[:, i, :], start=(i == 0), stop=(j == 4 and i == 3))
            if j < 4:
                last = nc.tensor.matmul(psP[:, j * W:(j + 1) * W], self.k.before[:, :], self.hot_bf[:, j, :], start=(j == 0), stop=True)
        last.then_inc(self.placed, 1)

    def dve_2c(self, nc, dve, chain, s, b):
        k, W = self.k, TOPK * EXPERTS
        psP, pos = self.psP(b), self.pos
        all4 = lambda v: v.rearrange("p (a c) -> p a c", a=1).to_broadcast([P, 4, W])
        dve.wait_ge(self.placed, s + 1)
        chain(nc.vector.tensor_tensor(pos[:, :, :], psP[:, 0:4 * W].rearrange("p (t c) -> p t c", t=4), all4(self.run[:, :]), ALU.add))
        nc.vector.tensor_tensor(self.run[:, :], psP[:, 4 * W:5 * W], self.run[:, :], ALU.add)
        chain(nc.vector.tensor_tensor(pos[:, :, :], pos[:, :, :], all4(k.small[:, SIGN:SIGN + W]), ALU.mult))
        chain(nc.vector.tensor_tensor(pos[:, :, :], pos[:, :, :], all4(k.small[:, BASE:BASE + W]), ALU.add))
        chain(nc.vector.tensor_tensor(pos[:, :, :], pos[:, :, :], k.hot[:, self.four(s), :], ALU.mult))
        chain(nc.vector.tensor_reduce(self.row[:, :, :], pos[:, :, :].rearrange("p t (c e) -> p t c e", c=TOPK), AX.X, ALU.add))
        nc.vector.tensor_scalar(k.row[:, self.four(s), :], self.row[:, :, :], 1.0, None, ALU.mult)
        nc.vector.tensor_copy(self.idx[:, b, :], self.row[:, :, :].rearrange("p t c -> p (t c)")).then_inc(self.rowed, 1)

    def links(self):
        one = 4 + (0 if self.first else 5)
        return one, 2, 11 + 2, 5

    def pool_start(self, pool):
        self.last_row = pool.to_reg(DUMP - 1)

    def pool(self, pool, s, b):
        for i in range(8):
            self.pool_one(pool, s, b, i)

    def pool_one(self, pool, s, b, i):
        if i == 0:
            pool.wait_ge(self.rowed, s + 1)
            pool.sem_inc(self.taken, 1)
        pool.indirect_dma_start(out=self.k.xslots[:, :], out_offset=bass.IndirectOffsetOnAxis(ap=self.idx[:, b, i:i + 1].bitcast(U32), axis=0),
                                in_=self.xn[:, b, i // 2, :], in_offset=None, bounds_check=self.last_row, oob_is_err=False).then_inc(self.scattered[8 * b + i], 16)

    def dve_tables(self, nc, dve, chain, st):
        k, E = self.k, EXPERTS
        names = "n1 start length nblk end before ones".split()
        n1, start, length, nblk, end, before, ones = (st.sb(f"r_{n}", [P, E]) for n in names)
        count_i = st.sb("r_count_i", [P, E], I32)
        owner, late = (st.sb(f"r_{n}", [P, NBLK, E]) for n in ("owner", "late"))
        of_block, row_f = st.sb("r_of_block", [P, NBLK]), st.sb("r_row_f", [P, NBLK])
        middle = k.small[:, MIDDLE:MIDDLE + E]
        per_block = lambda v: v.rearrange("p (a e) -> p a e", a=1).to_broadcast([P, NBLK, E])
        number = k.small[:, NUMBER:NUMBER + NBLK]
        numbers = number.rearrange("p (n a) -> p n a", a=1).to_broadcast([P, NBLK, E])
        first_n, second_n = self.run[:, 0:E], self.run[:, E:2 * E]
        limit, shift = st.sb("r_limit", [P, TOPK, E]), st.sb("r_shift", [P, E])
        mine, per_token, keep = st.sb("r_mine", [P, TILES, E]), st.sb("r_per_token", [P, TILES]), st.sb("r_keep", [P, TILES])
        chain(nc.vector.memset(ones[:, :], 1.0))
        chain(nc.vector.tensor_tensor(length[:, :], first_n, second_n, ALU.add))
        if self.first:
            chain(nc.vector.tensor_scalar(n1[:, :], first_n, float(CAPACITY), None, ALU.min))
            chain(nc.vector.tensor_scalar(length[:, :], length[:, :], float(CAPACITY), None, ALU.min))
            chain(nc.vector.tensor_scalar(limit[:, 0, :], middle, float(-CAPACITY), None, ALU.add))
            chain(nc.vector.tensor_tensor(limit[:, 1, :], middle, first_n, ALU.subtract))
            chain(nc.vector.tensor_scalar(limit[:, 1, :], limit[:, 1, :], float(CAPACITY), None, ALU.add))
        else:
            chain(nc.vector.tensor_copy(n1[:, :], first_n))
        chain(nc.vector.tensor_tensor(start[:, :], middle, n1[:, :], ALU.subtract))
        chain(nc.vector.tensor_tensor(nblk[:, :], start[:, :], length[:, :], ALU.add))
        chain(nc.vector.tensor_copy(k.pad_row[:, :], nblk[:, :]))
        chain(nc.vector.tensor_scalar(length[:, :], length[:, :], float(BLOCK - 1), None, ALU.add))
        chain(nc.vector.tensor_copy(count_i[:, :], length[:, :]))
        chain(nc.vector.tensor_scalar(count_i[:, :], count_i[:, :], BLOCK.bit_length() - 1, None, ALU.arith_shift_right))
        chain(nc.vector.tensor_copy(nblk[:, :], count_i[:, :]))
        chain(nc.vector.tensor_tensor_scan(end[:, :], ones[:, :], nblk[:, :], 0.0, ALU.mult, ALU.add))
        chain(nc.vector.tensor_tensor(before[:, :], end[:, :], nblk[:, :], ALU.subtract))
        chain(nc.vector.scalar_tensor_tensor(out=shift[:, :], in0=before[:, :], scalar=float(BLOCK), in1=start[:, :], op0=ALU.mult, op1=ALU.subtract))
        per_tile = lambda v: v.rearrange("p (a e) -> p a e", a=1).to_broadcast([P, TILES, E])
        for c in range(TOPK):
            hot, row = k.hot[:, :, c * E:(c + 1) * E], k.row[:, :, c]
            if self.first:
                chain(nc.vector.tensor_tensor(mine[:, :, :], hot, per_tile(limit[:, c, :]), ALU.mult))
                chain(nc.vector.tensor_reduce(per_token[:, :], mine[:, :, :], AX.X, ALU.add))
                chain(nc.vector.tensor_tensor(keep[:, :], row, per_token[:, :], ALU.is_lt if c else ALU.is_ge))
            chain(nc.vector.tensor_tensor(mine[:, :, :], hot, per_tile(shift[:, :]), ALU.mult))
            chain(nc.vector.tensor_reduce(per_token[:, :], mine[:, :, :], AX.X, ALU.add))
            chain(nc.vector.tensor_tensor(row, row, per_token[:, :], ALU.add))
            if self.first:
                chain(nc.vector.tensor_scalar(row, row, float(-TRASH), None, ALU.add))
                chain(nc.vector.tensor_tensor(row, row, keep[:, :], ALU.mult))
                chain(nc.vector.tensor_scalar(row, row, float(TRASH), None, ALU.add))
        chain(nc.vector.tensor_copy(k.idx[:, 0:TILES, :], k.row[:, :, :]))
        chain(nc.vector.tensor_tensor(owner[:, :, :], per_block(before[:, :]), numbers, ALU.is_le))
        chain(nc.vector.tensor_tensor(late[:, :, :], per_block(end[:, :]), numbers, ALU.is_gt))
        chain(nc.vector.tensor_tensor(owner[:, :, :], owner[:, :, :], late[:, :, :], ALU.mult))
        chain(nc.vector.tensor_reduce(of_block[:, :], owner[:, :, :], AX.X, ALU.add))
        chain(nc.vector.tensor_scalar(before[:, :], before[:, :], float(-BLOCK), float(-DUMP), ALU.mult, ALU.add))
        chain(nc.vector.tensor_tensor(start[:, :], start[:, :], before[:, :], ALU.add))
        chain(nc.vector.tensor_tensor(late[:, :, :], owner[:, :, :], per_block(start[:, :]), ALU.mult))
        chain(nc.vector.tensor_reduce(row_f[:, :], late[:, :, :], AX.X, ALU.add))
        chain(nc.vector.tensor_tensor(of_block[:, :], of_block[:, :], number, ALU.mult))
        chain(nc.vector.tensor_scalar(of_block[:, :], of_block[:, :], float(BLOCK), float(DUMP), ALU.mult, ALU.add))
        chain(nc.vector.tensor_tensor(row_f[:, :], row_f[:, :], of_block[:, :], ALU.add))
        chain(nc.vector.tensor_copy(k.block_row[:, :], row_f[:, :]))
        chain(nc.vector.tensor_tensor(late[:, :, :], owner[:, :, :], per_block(k.small[:, EIGHT:EIGHT + E]), ALU.mult))
        chain(nc.vector.tensor_reduce(of_block[:, :], late[:, :, :], AX.X, ALU.add))
        nc.vector.tensor_copy(k.owner[:, :], of_block[:, :]).then_inc(self.tabled, 1)

    def sp_pads(self, nc, sp, zeros, cleared):
        sp.wait_ge(self.tabled, 1)
        sp.wait_ge(cleared, 1)
        for s in range(16):
            sp.wait_ge(self.scattered[s], BATCH // 2 * 16)
        for e in range(EXPERTS):
            r = sp.value_load(self.k.pad_row[0:1, e:e + 1], min_val=0, max_val=DUMP - BLOCK)
            sp.dma_start(self.k.xslots[bass.ds(r, BLOCK), :].rearrange("(p r) d -> p (r d)", p=P), zeros[:, :]).then_inc(self.zeroed, 16)
        sp.wait_ge(self.zeroed, EXPERTS * 16)


class Gather:

    def __init__(self, st, k):
        self.k = k
        self.gathered = [st.sem(f"g_gathered{i}") for i in range(16)]
        self.idx_ready, self.taken = st.sem("g_idx_ready"), st.sem("g_taken")
        self.rows = st.sb("g_rows", [P, 2, 8, D])
        self.idx = st.sb("g_idx", [P, 2, 8], I32)

    def dve_ask(self, nc, s, b):
        nc.vector.tensor_scalar(self.idx[:, b, :], self.k.idx[:, bass.ds(s * 4, 4), :].rearrange("p t c -> p (t c)"), 1.0, None, ALU.mult).then_inc(self.idx_ready, 1)

    def dve(self, nc, dve, chain, s, b, turn):
        for c in range(TOPK):
            for j in range(4):
                x = rows_of(self.k.X, s * 4 + j)
                dve.wait_ge(self.gathered[8 * b + 2 * j + c], turn * 16 + 16)
                last = nc.vector.scalar_tensor_tensor(out=x, in0=self.rows[:, b, 2 * j + c, :], scalar=self.k.gate[:, c, bass.ds(s * 4 + j, 1)],
                                                      in1=x, op0=ALU.mult, op1=ALU.add)
            chain(last)
        self.dve_ask(nc, s + 2, b)

    def pool_start(self, pool):
        self.last_row = pool.to_reg(TRASH)

    def pool(self, pool, s, b):
        for i in range(8):
            self.pool_one(pool, s, b, i)

    def pool_one(self, pool, s, b, i):
        if i == 0:
            pool.wait_ge(self.idx_ready, s + 1)
            pool.sem_inc(self.taken, 1)
        pool.indirect_dma_start(out=self.rows[:, b, i, :], out_offset=None, in_=self.k.yslots[:, :],
                                in_offset=bass.IndirectOffsetOnAxis(ap=self.idx[:, b, i:i + 1].bitcast(U32), axis=0),
                                bounds_check=self.last_row, oob_is_err=False).then_inc(self.gathered[8 * b + i], 16)


def plain_stage(nc, k, name, gather, route, out=None):
    routing = route is not None
    with Stage(nc, name) as st:
        G = Gather(st, k) if gather else None
        linked, cleared, added = st.sem("linked"), st.sem("cleared"), st.sem("added")
        if routing:
            psT, psL, psP = st.pb("psT", [P, BLOCK]), st.pb("psL", [P, 2, BLOCK]), st.pb("psP", [P, BLOCK])
            R = Router(st, k, route, lambda b: psT[:, :], lambda b: psL[:, b, :], lambda b: psP[:, :])
            zeros = st.sb("zeros", [P, BLOCK])
        saved = st.sem("saved")
        block = st.block()

        def order(eng, head, tail, chain=None, links=0):
            head(0, 0, 0)
            sequences(eng, lambda s, b, turn, first, last: ((None if last else head(s + 1, 1 - b, turn + b)), tail(s, b)), chain, links)

        @block.vector
        def _(dve):
            chain = Chain(dve, linked)
            if routing:
                nc.vector.memset(zeros[:, :], 0.0).then_inc(cleared, 1)
                chain(nc.vector.memset(R.run[:, :], 0.0))
            if gather:
                for b in range(2):
                    G.dve_ask(nc, b, b)

            def head(s, b, turn):
                if gather:
                    G.dve(nc, dve, chain, s, b, turn)
                    if not routing:
                        dve.sem_inc(added, 1)
                if routing:
                    R.norm.dve_stats(nc, chain, s)
                    R.dve_1(nc, dve, chain, s, b, turn)

            def tail(s, b):
                if routing:
                    R.dve_2a(nc, dve, chain, s, b)
                    R.dve_2b(nc, dve, chain, s, b)
                    R.dve_2c(nc, dve, chain, s, b)

            links = (2 if gather else 0) + (sum(R.links()) + 4 if routing else 0)
            order(dve, head, tail, chain, 2 * links)
            if routing:
                R.dve_tables(nc, dve, chain, st)

        if routing:
            @block.scalar
            def _(act):
                act.preload_act_table_set("natural_log_exp_and_others")
                order(act, lambda s, b, turn: (R.norm.act_root(nc, act, s), R.act_1(nc, act, s, b)), lambda s, b: R.act_2(nc, act, s))

            @block.tensor
            def _(pe):
                order(pe, lambda s, b, turn: R.pe_1(nc, pe, s, b), lambda s, b: R.pe_2(nc, pe, s, b))

        @block.gpsimd
        def _(pool):
            if routing:
                R.pool_start(pool)
            if gather:
                G.pool_start(pool)
                G.pool(pool, 0, 0)
                G.pool(pool, 1, 1)
            sequences(pool, lambda s, b, turn, first, last: (G.pool(pool, s + 2, b) if gather and not last else None, R.pool(pool, s, b) if routing else None))
            if gather:
                for i in range(8):
                    pool.wait_ge(G.gathered[i], (BATCH // 2 + 1) * 16)

        @block.sync
        def _(sp):
            if routing:
                R.sp_pads(nc, sp, zeros, cleared)
            if out is not None:
                with sp.Fori(0, BATCH) as s:
                    sp.wait_ge(added, s + 1)
                    sp.dma_start(out[bass.ds(s * SEQ, SEQ), :].rearrange("(t p) d -> p t d", p=P), k.X[:, bass.ds(s * 4, 4), :]).then_inc(saved, 16)
                sp.wait_ge(saved, BATCH * 16)


def load_stage(nc, k, x, consts, l0_bg, gate_w, gamma, beta):
    with Stage(nc, "load") as st:
        loaded, zeroed, cleared = map(st.sem, ("loaded", "zeroed", "cleared"))
        zeros = st.sb("zeros", [P, BLOCK])
        raw = st.sb("raw", [P, 35 * P])
        block = st.block()

        @block.sync
        def _(sp):
            wide = lambda v: v.rearrange("(a e) -> a e", a=1)
            for dst, src in ((raw[:, :], consts[:, P:36 * P]), (k.ident[:, :], consts[:, 0:P]), (k.small[:, :], consts[:, 36 * P:]),
                             (k.bg[:, :], wide(l0_bg).to_broadcast([P, EXPERTS])), (k.gamma[:, :], wide(gamma).to_broadcast([P, D])),
                             (k.beta[:, :], wide(beta).to_broadcast([P, D])), (k.gate_w[:, 0, :], gate_w[0]), (k.gate_w[:, 1, :], gate_w[1]),
                             (k.X[:, :, :], x.rearrange("(t p) d -> p t d", p=P))):
                sp.dma_start(dst, src).then_inc(loaded, 16)
            sp.wait_ge(loaded, 9 * 16)

        @block.scalar
        def _(act):
            act.wait_ge(cleared, 1)
            act.dma_start(k.xslots[DUMP:DUMP + BLOCK, :].rearrange("(p r) d -> p (r d)", p=P), zeros[:, :]).then_inc(zeroed, 16)
            act.dma_start(k.yslots[TRASH:TRASH + 1, :], zeros[0:1, 0:D]).then_inc(zeroed, 16)
            act.wait_ge(zeroed, 32)

        @block.vector
        def _(dve):
            nc.vector.memset(k.ones[:, :], 1.0)
            nc.vector.memset(k.idx[:, TILES:, :], TRASH)
            nc.vector.memset(zeros[:, :], 0.0).then_inc(cleared, 1)
            dve.wait_ge(loaded, 9 * 16)
            nc.vector.tensor_copy(k.before[:, :], raw[:, 0:P])
            nc.vector.tensor_copy(k.causal[:, :], raw[:, P:2 * P])
            nc.vector.tensor_copy(k.ident_bf[:, :], raw[:, 2 * P:3 * P])
            nc.vector.tensor_copy(k.pick[:, :, :].rearrange("p n m -> p (n m)"), raw[0:96, 3 * P:])


def blocks_stage(nc, k, name, pack, down_bias, gelu):
    with Stage(nc, name) as st:
        sem, sb, pb = st.sem, st.sb, st.pb
        w_ready = [sem(f"w_ready{i}") for i in range(2)]
        x_ready = [sem(f"x_ready{i}") for i in range(2)]
        stored = [sem(f"stored{i}") for i in range(2)]
        x_flipped, xT_ready, h_summed, h_ready, y_summed, y_ready = map(
            sem, ("x_flipped", "xT_ready", "h_summed", "h_ready", "y_summed", "y_ready"))
        W = sb("W", [P, 2, PACK])
        b2 = sb("b2", [P, 2, 1, D])
        xs = sb("xs", [P, 2, 4, D])
        xT = sb("xT", [P, 2, BLOCK])
        H = sb("H", [P, 2, FT, BLOCK])
        yr = sb("yr", [P, 2, 4, D])
        psX = pb("psX", [P, 4, P])
        psH = pb("psH", [P, FT, BLOCK])
        psY = pb("psY", [P, 2, 4, P])
        block = st.block()

        TURNS = NBLK // 2

        def turns(eng, one):
            one(0, 0, 0, True, False)
            one(1, 1, 0, False, False)
            with eng.Fori(1, TURNS - 1) as j2:
                for b in range(2):
                    one(j2 * 2 + b, b, j2, False, False)
            one(NBLK - 2, 0, TURNS - 1, False, False)
            one(NBLK - 1, 1, TURNS - 1, False, True)

        @block.sync
        def _(sp):
            def load(j, b, waits):
                r = sp.value_load(k.block_row[0:1, bass.ds(j, 1)], min_val=0, max_val=DUMP)
                e = sp.value_load(k.owner[0:1, bass.ds(j, 1)], min_val=0, max_val=EXPERTS - 1)
                if waits:
                    sp.wait_ge(x_flipped, j - 1)
                sp.dma_start(xs[:, b, :, :], k.xslots[bass.ds(r, BLOCK), :].rearrange("(p s) d -> p s d", p=P)).then_inc(x_ready[b], 16)
                if waits:
                    sp.wait_ge(y_ready, j - 1)
                sp.dma_start(W[:, b, :], pack[bass.ds(e, 1), :, :].rearrange("a p n -> (a p) n")).then_inc(w_ready[b], 16)
                sp.dma_start(b2[:, b, 0, :], down_bias[bass.ds(e, 1), :].to_broadcast([P, D])).then_inc(w_ready[b], 16)

            def store(j, b):
                sp.wait_ge(y_ready, j + 1)
                sp.dma_start(k.yslots[bass.ds(j * BLOCK, BLOCK), :].rearrange("(p s) d -> p s d", p=P), yr[:, b, :, :]).then_inc(stored[b], 16)

            for b in range(2):
                load(b, b, False)
            with sp.Fori(1, TURNS) as j2:
                for b in range(2):
                    load(j2 * 2 + b, b, True)
                    store(j2 * 2 + b - 2, b)
            for b in range(2):
                store(NBLK - 2 + b, b)
                sp.wait_ge(stored[b], TURNS * 16)

        @block.tensor
        def _(pe):
            def flip_in(j, b, turn):
                pe.wait_ge(x_ready[b], turn * 16 + 16)
                for s in range(4):
                    last = nc.tensor.transpose(psX[:, s, :], xs[:, b, s, :], k.ident[:, :])
                last.then_inc(x_flipped, 1)

            def one(j, b, j2, first_block, last_block):
                pe.wait_ge(w_ready[b], j2 * 32 + 32)
                pe.wait_ge(xT_ready, j + 1)
                for f in range(FT):
                    nc.tensor.matmul(psH[:, f, :], W[:, b, f * P:(f + 1) * P], xT[:, b, :], start=True, stop=True).then_inc(h_summed, 1)
                if not last_block:
                    flip_in(j + 1, 1 - b, j2 + b)
                if not (isinstance(j, int) and j < 2):
                    pe.wait_ge(y_ready, j - 1)
                pe.wait_ge(h_ready, j * FT + FT)
                for s in range(4):
                    for f in range(FT):
                        last = nc.tensor.matmul(psY[:, b, s, :], H[:, b, f, s * P:(s + 1) * P], W[:, b, HIDDEN + f * D:HIDDEN + (f + 1) * D], start=(f == 0), stop=(f == FT - 1))
                last.then_inc(y_summed, 1)

            flip_in(0, 0, 0)
            turns(pe, one)

        @block.scalar
        def _(act):
            with act.Fori(0, TURNS) as j2:
                for b in range(2):
                    for f in range(FT):
                        act.wait_ge(h_summed, (j2 * 2 + b) * FT + f + 1)
                        nc.scalar.activation(H[:, b, f, :], psH[:, f, :], gelu, bias=W[:, b, HIDDEN + FT * D + f:HIDDEN + FT * D + f + 1]).then_inc(h_ready, 1)

        @block.vector
        def _(dve):
            def turn_in(j, b):
                dve.wait_ge(x_flipped, j + 1)
                nc.vector.tensor_copy(xT[:, b, :], psX[:, :, :].rearrange("p a d -> p (a d)")).then_inc(xT_ready, 1)

            def one(j, b, j2, first_block, last_block):
                if not last_block:
                    turn_in(j + 1, 1 - b)
                dve.wait_ge(y_summed, j + 1)
                if not (isinstance(j2, int) and j2 == 0):
                    dve.wait_ge(stored[b], j2 * 16)
                nc.vector.tensor_tensor(yr[:, b, :, :], psY[:, b, :, :], b2[:, b, :, :].to_broadcast([P, 4, D]), ALU.add).then_inc(y_ready, 1)

            turn_in(0, 0)
            turns(dve, one)


def attention_stage(nc, k, wqkv):
    with Stage(nc, "att") as st:
        sem, sb, pb = st.sem, st.sb, st.pb
        w_ready, linked, normed, flipped, turned, q_summed, k_summed, v_summed, qk_ready, v_ready = map(
            sem, ("w_ready", "linked", "normed", "flipped", "turned", "q_summed", "k_summed", "v_summed", "qk_ready", "v_ready"))
        scored, topped, exped, p_flipped, p_turned, summed, added, holed, cleared = map(
            sem, ("scored", "topped", "exped", "p_flipped", "p_turned", "summed", "added", "holed", "cleared"))
        W = sb("W", [P, 3, P])
        xn = sb("xn", [P, 4, D])
        xnT = sb("xnT", [P, SEQ])
        QT, KT = sb("QT", [P, SEQ]), sb("KT", [P, SEQ])
        V = sb("V", [P, 4, D])
        hole, S, E, PT = (sb(n, [P, 2, SEQ]) for n in ("hole", "S", "E", "PT"))
        top, ntop, total, inv = (sb(n, [P, 2]) for n in ("top", "ntop", "total", "inv"))
        zeros = sb("zeros", [P, BLOCK])
        psT = pb("psT", [P, SEQ])
        psQ, psK = pb("psQ", [P, SEQ]), pb("psK", [P, SEQ])
        psS = pb("psS", [P, 2, SEQ])
        psE = pb("psE", [P, SEQ])
        psO = pb("psO", [P, D])
        psR = pb("psR", [P, SEQ])
        G = Gather(st, k)
        N = Norm(st, k, "n")
        R = Router(st, k, True, lambda b: psT[:, :], lambda b: psR[:, 0:4 * EXPERTS], lambda b: psR[:, 256:])
        block = st.block()
        ST = SEQ_TILES

        @block.sync
        def _(sp):
            sp.dma_start(W[:, :, :], wqkv).then_inc(w_ready, 16)
            R.sp_pads(nc, sp, zeros, cleared)

        @block.gpsimd
        def _(pool):
            R.pool_start(pool)
            G.pool_start(pool)
            G.pool(pool, 0, 0)
            G.pool(pool, 1, 1)

            def body(s, b, turn, first, last):
                if not last:
                    G.pool(pool, s + 2, b)
                if not first:
                    R.pool(pool, s - 1, 1 - b)
            sequences(pool, body)
            R.pool(pool, BATCH - 1, 1)
            for i in range(8):
                pool.wait_ge(G.gathered[i], (BATCH // 2 + 1) * 16)

        @block.tensor
        def _(pe):
            pe.wait_ge(w_ready, 16)

            def body(s, b, turn, first, last):
                pe.wait_ge(normed, s + 1)
                for j in range(ST):
                    ins = nc.tensor.transpose(psT[:, j * P:(j + 1) * P], xn[:, j, :], k.ident[:, :])
                ins.then_inc(flipped, 1)
                pe.wait_ge(turned, s + 1)
                nc.tensor.matmul(psQ[:, :], W[:, 0, :], xnT[:, :], start=True, stop=True).then_inc(q_summed, 1)
                nc.tensor.matmul(psK[:, :], W[:, 1, :], xnT[:, :], start=True, stop=True).then_inc(k_summed, 1)
                for j in range(ST):
                    ins = nc.tensor.matmul(psT[:, j * P:(j + 1) * P], xnT[:, j * P:(j + 1) * P], W[:, 2, :], start=True, stop=True)
                ins.then_inc(v_summed, 1)

                def scores(i):
                    n = (i + 1) * P
                    if i > 0:
                        nc.tensor.matmul(psS[:, i % 2, 0:i * P], QT[:, i * P:n], KT[:, 0:i * P], start=True, stop=True)
                    nc.tensor.matmul(psS[:, i % 2, i * P:n], QT[:, i * P:n], KT[:, i * P:n], start=True, stop=False)
                    nc.tensor.matmul(psS[:, i % 2, i * P:n], k.ident_bf[:, :], k.causal[:, :], start=False, stop=True).then_inc(scored, 1)

                pe.wait_ge(qk_ready, s * 2 + 2)
                scores(0)
                for i in range(ST):
                    if i + 1 < ST:
                        scores(i + 1)
                    pe.wait_ge(exped, s * ST + i + 1)
                    for j in range(i + 1):
                        ins = nc.tensor.transpose(psE[:, j * P:(j + 1) * P], E[:, i % 2, j * P:(j + 1) * P], k.ident[:, :])
                    ins.then_inc(p_flipped, 1)
                    pe.wait_ge(p_turned, s * ST + i + 1)
                    if i == 0:
                        pe.wait_ge(v_ready, s + 1)
                    if not (i == 0 and first):
                        pe.wait_ge(added, s * ST + i)
                    for j in range(i + 1):
                        ins = nc.tensor.matmul(psO[:, :], PT[:, i % 2, j * P:(j + 1) * P], V[:, j, :], start=(j == 0), stop=(j == i))
                    ins.then_inc(summed, 1)
                    if i == 0 and not first:
                        R.pe_1(nc, pe, s - 1, 1 - b)
                    if i == 2 and not first:
                        R.pe_2(nc, pe, s - 1, 1 - b)
            sequences(pe, body)
            R.pe_1(nc, pe, BATCH - 1, 1)
            R.pe_2(nc, pe, BATCH - 1, 1)

        @block.scalar
        def _(act):
            act.preload_act_table_set("natural_log_exp_and_others")
            N.act_root(nc, act, 0)

            def body(s, b, turn, first, last):
                act.wait_ge(flipped, s + 1)
                nc.scalar.activation(xnT[:, :], psT[:, :], ACT.Copy).then_inc(turned, 1)
                act.wait_ge(k_summed, s + 1)
                nc.scalar.activation(KT[:, :], psK[:, :], ACT.Copy).then_inc(qk_ready, 1)
                act.wait_ge(v_summed, s + 1)
                nc.scalar.activation(V[:, :, :], psT[:, :].rearrange("p (a d) -> p a d", a=4), ACT.Copy).then_inc(v_ready, 1)
                if not first:
                    R.norm.act_root(nc, act, s - 1)
                for i in range(ST):
                    n = (i + 1) * P
                    act.wait_ge(topped, s * ST + i + 1)
                    nc.scalar.activation(E[:, i % 2, 0:n], S[:, i % 2, 0:n], ACT.Exp, bias=ntop[:, i % 2:i % 2 + 1], scale=SCALE,
                                         accum_out=total[:, i % 2:i % 2 + 1]).then_inc(exped, 1)
                    act.wait_ge(p_flipped, s * ST + i + 1)
                    nc.scalar.activation(PT[:, i % 2, 0:n], psE[:, 0:n], ACT.Copy).then_inc(p_turned, 1)
                    if i == 0 and not first:
                        R.act_1(nc, act, s - 1, 1 - b)
                    if i == 1 and not first:
                        R.act_2(nc, act, s - 1)
                    if i == 2 and not last:
                        N.act_root(nc, act, s + 1)
            sequences(act, body)
            R.norm.act_root(nc, act, BATCH - 1)
            R.act_1(nc, act, BATCH - 1, 1)
            R.act_2(nc, act, BATCH - 1)

        @block.vector
        def _(dve):
            chain = Chain(dve, linked)
            nc.vector.memset(zeros[:, :], 0.0).then_inc(cleared, 1)
            chain(nc.vector.memset(R.run[:, :], 0.0))
            for b in range(2):
                G.dve_ask(nc, b, b)
            G.dve(nc, dve, chain, 0, 0, 0)
            N.dve_stats(nc, chain, 0)
            N.dve_finish(nc, dve, chain, 0)
            N.dve_apply(nc, xn, 0).then_inc(normed, 1)

            def body(s, b, turn, first, last):
                def mask(i):
                    n, h = (i + 1) * P, i % 2
                    dve.wait_ge(scored, s * ST + i + 1)
                    chain(nc.vector.tensor_scalar(hole[:, h, 0:n], psS[:, h, 0:n], 0.0, NEG, ALU.is_equal, ALU.mult))
                    dve.sem_inc(holed, 1)
                    chain(nc.vector.tensor_tensor_reduce(out=S[:, h, 0:n], in0=psS[:, h, 0:n], in1=hole[:, h, 0:n], scale=1.0, scalar=3.0 * NEG,
                                                         op0=ALU.add, op1=ALU.max, accum_out=top[:, h:h + 1]))
                    nc.vector.tensor_scalar(ntop[:, h:h + 1], top[:, h:h + 1], -SCALE, None, ALU.mult).then_inc(topped, 1)

                def finish(i):
                    t, h = s * ST + i, i % 2
                    dve.wait_ge(exped, s * ST + i + 1)
                    chain(nc.vector.reciprocal(inv[:, h:h + 1], total[:, h:h + 1]))
                    dve.wait_ge(summed, s * ST + i + 1)
                    nc.vector.scalar_tensor_tensor(out=rows_of(k.X, t), in0=psO[:, :], scalar=inv[:, h:h + 1], in1=rows_of(k.X, t),
                                                   op0=ALU.mult, op1=ALU.add).then_inc(added, 1)

                dve.wait_ge(q_summed, s + 1)
                nc.vector.tensor_copy(QT[:, :], psQ[:, :]).then_inc(qk_ready, 1)
                if not first:
                    dve.wait_ge(added, s * ST)
                    R.norm.dve_stats(nc, chain, s - 1)
                mask(0)
                if not first:
                    R.dve_1(nc, dve, chain, s - 1, 1 - b, turn - 1 + b)
                mask(1)
                finish(0)
                if not first:
                    R.dve_2a(nc, dve, chain, s - 1, 1 - b)
                mask(2)
                finish(1)
                if not last:
                    G.dve(nc, dve, chain, s + 1, 1 - b, turn + b)
                    N.dve_stats(nc, chain, s + 1)
                if not first:
                    R.dve_2b(nc, dve, chain, s - 1, 1 - b)
                mask(3)
                finish(2)
                if not last:
                    N.dve_finish(nc, dve, chain, s + 1)
                    N.dve_apply(nc, xn, s + 1).then_inc(normed, 1)
                if not first:
                    R.dve_2c(nc, dve, chain, s - 1, 1 - b)
                finish(3)
            sequences(dve, body, chain, 2 * (3 * ST + 2 + 4 + 4 + 4 + sum(R.links())))
            s, b = BATCH - 1, 1
            dve.wait_ge(added, BATCH * ST)
            R.norm.dve_stats(nc, chain, s)
            R.dve_1(nc, dve, chain, s, b, s // 2)
            R.dve_2a(nc, dve, chain, s, b)
            R.dve_2b(nc, dve, chain, s, b)
            R.dve_2c(nc, dve, chain, s, b)
            R.dve_tables(nc, dve, chain, st)


CONV_STEPS = {0: ((0, (0, 1, 2)),), 1: ((0, (3,)), (1, (0, 1))), 2: ((1, (2, 3)), (2, (0,))), 3: ((2, (1, 2, 3)),),
              4: ((3, (0, 1, 2)),), 5: ((3, (3,)), (4, (0,))), 6: ((5, (0,)),)}
EMPTY_STEPS = {1: (0,), 2: (1,), 3: (2,), 5: (3, 4), 7: (5,)}


def scan_stage(nc, k, w):
    with Stage(nc, "ssm") as st:
        sem, sb, pb = st.sem, st.sb, st.pb
        Win = sb("Win", [P, 2 * INNER])
        Wtap = sb("Wtap", [P, 2, TAPS, INNER])
        Wx = sb("Wx", [P, DT, RANK + 3 * 32])
        Wdt = sb("Wdt", [RANK, INNER])
        Wout = sb("Wout", [P, DT, D])
        col = sb("col", [P, DT, 4 + STATES])
        gates, gmax = sb("gates", [P, 2]), sb("gmax", [P, 1])
        A = sb("A", [P, DT, STATES])
        xn = sb("xn", [P, 4, D])
        hT = sb("hT", [P, PAD + SEQ])
        pre = sb("pre", [P, 2 * DT, SEQ])
        absv, soft = pre[:, 0:DT, :], pre[:, DT:, :]
        zs, xc, delta, ux = (sb(n, [P, 2, DT, SEQ]) for n in ("zs", "xc", "delta", "ux"))
        low = sb("low", [RANK, SEQ])
        bc = sb("bc", [96, SEQ])
        bc3 = sb("bc3", [96, 2, SEQ], BF16)
        v, rest = sb("v", [P, DT, SEQ]), sb("rest", [P, DT, SEQ])
        RA, RB, RH, RC, RP = 4, 2, 4, 4, 4
        dA, dBx, H, HC = (sb(n, [P, r, DT, SEQ]) for n, r in (("dA", RA), ("dBx", RB), ("H", RH), ("HC", RP)))
        Cs = sb("Cs", [P, RC, 1, SEQ])
        zeros = dBx[:, 0, 0, :]
        tap = H[:, 0:2, :, :].rearrange("p a b t -> p (a b t)").rearrange("p (c t e) -> p c t e", c=2, t=TAPS)
        psA, psB = pb("psA", [P, 2, SEQ]), pb("psB", [P, 2, SEQ])
        psC, psR, psY = pb("psC", [P, SEQ]), pb("psR", [P, SEQ]), pb("psY", [P, DT, SEQ])
        G, N = Gather(st, k), Norm(st, k, "n")
        R = Router(st, k, False, lambda b: psR[:, :], lambda b: psR[:, 0:4 * EXPERTS], lambda b: psR[:, 256:])
        (loaded, linked, loose, exp_ready, setup, normed, flipped, turned, fronted, emptied, silu_done, mixed, projected, cut, low_ready, dt_summed, v_ready,
         abs_ready, u_ready, l_ready, delta_ready, ux_ready) = map(sem, "loaded linked loose exp_ready setup normed flipped turned fronted emptied silu_done mixed projected cut low_ready dt_summed v_ready abs_ready u_ready l_ready delta_ready ux_ready".split())
        dA_ready, B_ready, C_ready, Cs_ready, dBx_done, h_ready, hc_ready, y_summed, y_emptied, y_ready, out_summed, added, cleared, z_done = map(
            sem, "dA_ready B_ready C_ready Cs_ready dBx_done h_ready hc_ready y_summed y_emptied y_ready out_summed added cleared z_done".split())
        block = st.block()
        ST, NB = SEQ_TILES, STATES
        positive = lambda count: not isinstance(count, int) or count > 0
        there = lambda s, d: not isinstance(s, int) or 0 <= s + d < BATCH

        def run(eng, main, between, chain=None, links=0):
            turns = (BATCH - 6) // 2

            def body(s, b, turn):
                for n in range(NB):
                    main(s, b, n)
                    between(s, b, turn, n)
            for s in range(3):
                body(s, s % 2, s // 2)
            with eng.Fori(0, turns) as i:
                if chain is not None:
                    chain.turn(i, links, turns)
                body(i * 2 + 3, 1, i + 1)
                body(i * 2 + 4, 0, i + 2)
                if chain is not None:
                    chain.leave()
            for s in range(BATCH - 3, BATCH):
                body(s, s % 2, s // 2)

        @block.sync
        def _(sp):
            for dst, src in ((Win[:, :], w["in"]), (tap, w["taps"].to_broadcast([P, 2, TAPS, INNER])), (Wx[:, :, 0:RANK + 32], w["x"]),
                             (Wdt[:, :], w["dt"]), (Wout[:, :, :], w["out"]), (col[:, :, :], w["col"]),
                             (gates[:, :], w["gates"].rearrange("(a e) -> a e", a=1).to_broadcast([P, 2]))):
                sp.dma_start(dst, src).then_inc(loaded, 16)
            sp.wait_ge(loaded, 7 * 16)
            R.sp_pads(nc, sp, zeros, cleared)

        @block.tensor
        def _(pe):
            def flip(s):
                pe.wait_ge(normed, s + 1)
                if positive(s):
                    pe.wait_ge(v_ready, s)
                for j in range(ST):
                    last = nc.tensor.transpose(psA[:, 1, j * P:(j + 1) * P], xn[:, j, :], k.ident[:, :])
                last.then_inc(flipped, 1)

            def conv(s, g, taps=range(TAPS)):
                c, dt = g // 2, g % 2
                o = psA[:, g % 2, :]
                if 0 in taps:
                    if g == 0:
                        pe.wait_ge(turned, s + 1)
                    if g >= 2:
                        pe.wait_ge(emptied, s * 6 + g - 1)
                if g < 2 * DT:
                    for t in taps:
                        back = (TAPS - 1 - t) * (c + 1)
                        last = nc.tensor.matmul(o, Wtap[:, c, t, dt * P:(dt + 1) * P], hT[:, PAD - back:PAD - back + SEQ], start=(t == 0), stop=(t == TAPS - 1))
                    done = TAPS - 1 in taps
                else:
                    last = nc.tensor.matmul(o, Win[:, INNER + dt * P:INNER + (dt + 1) * P], hT[:, PAD:PAD + SEQ], start=True, stop=True)
                    done = True
                if done:
                    last.then_inc(fronted, 1)

            def project(s, b):
                pe.wait_ge(emptied, s * 6 + 6)
                pe.wait_ge(mixed, s + 1)
                for dt in range(DT):
                    nc.tensor.matmul(psA[0:RANK, 0, :], Wx[:, dt, 0:RANK], xc[:, b, dt, :], start=(dt == 0), stop=(dt == DT - 1))
                for dt in range(DT):
                    last = nc.tensor.matmul(psA[0:96, 1, :], Wx[:, dt, RANK:RANK + 96], xc[:, b, dt, :], start=(dt == 0), stop=(dt == DT - 1))
                last.then_inc(projected, 1)

            def steps(s):
                pe.wait_ge(low_ready, s + 1)
                pe.wait_ge(cut, s + 1)
                for dt in range(DT):
                    last = nc.tensor.matmul(psA[:, dt, :], Wdt[:, dt * P:(dt + 1) * P], low[:, :], start=True, stop=True)
                last.then_inc(dt_summed, 1)

            def out(s):
                pe.wait_ge(y_ready, s + 1)
                for j in range(ST):
                    for dt in range(DT):
                        last = nc.tensor.matmul(psR[:, j * P:(j + 1) * P], v[:, dt, j * P:(j + 1) * P], Wout[:, dt, :], start=(dt == 0), stop=(dt == DT - 1))
                last.then_inc(out_summed, 1)

            def spread_B(s, b, n):
                if positive(s * NB + n - 1):
                    pe.wait_ge(dBx_done, s * NB + n - 1)
                nc.tensor.matmul(psB[:, n % 2, :], k.pick[:, n, :], bc3[:, b, :], start=True, stop=True).then_inc(B_ready, 1)

            def spread_C(s, b, n):
                if positive(s * NB + n):
                    pe.wait_ge(Cs_ready, s * NB + n)
                nc.tensor.matmul(psC[:, :], k.pick[:, STATES + n, :], bc3[:, b, :], start=True, stop=True).then_inc(C_ready, 1)

            def total(s, n):
                pe.wait_ge(hc_ready, s * NB + n + 1)
                if n == 0 and positive(s):
                    pe.wait_ge(y_emptied, s)
                for dt in range(DT):
                    last = nc.tensor.matmul(psY[:, dt, :], k.ident[:, :], HC[:, n % RP, dt, :], start=(n == 0), stop=(n == NB - 1))
                last.then_inc(y_summed, 1)

            def main(s, b, n):
                if n + 2 < NB:
                    spread_B(s, b, n + 2)
                elif there(s, 1):
                    spread_B(s + 1, 1 - b, n + 2 - NB)
                if n >= 2:
                    total(s, n - 2)
                elif there(s, -1):
                    total(s - 1, n - 2 + NB)
                if n + 1 < NB:
                    spread_C(s, b, n + 1)
                elif there(s, 1):
                    spread_C(s + 1, 1 - b, 0)

            def between(s, b, turn, n):
                if there(s, -1):
                    if n == 2:
                        out(s - 1)
                    if n == 6:
                        R.pe_1a(nc, pe, s - 1, 1 - b)
                    if n == 8:
                        R.pe_1b(nc, pe, s - 1, 1 - b)
                    if n == 13:
                        R.pe_2(nc, pe, s - 1, 1 - b)
                if there(s, 1):
                    for g, taps in CONV_STEPS.get(n, ()):
                        conv(s + 1, g, taps)
                    if n == 9:
                        project(s + 1, 1 - b)
                    if n == 11:
                        steps(s + 1)
                if there(s, 2) and n == 14:
                    flip(s + 2)

            pe.wait_ge(setup, 1)
            flip(0)
            for g in range(6):
                conv(0, g)
            project(0, 0)
            steps(0)
            flip(1)
            spread_B(0, 0, 0)
            spread_B(0, 0, 1)
            spread_C(0, 0, 0)
            run(pe, main, between)
            for n in range(NB - 2, NB):
                total(BATCH - 1, n)
            out(BATCH - 1)
            R.pe_1a(nc, pe, BATCH - 1, 1)
            R.pe_1b(nc, pe, BATCH - 1, 1)
            R.pe_2(nc, pe, BATCH - 1, 1)

        @block.scalar
        def _(act):
            def to_hT(s):
                act.wait_ge(flipped, s + 1)
                nc.scalar.activation(hT[:, PAD:], psA[:, 1, :], ACT.Copy).then_inc(turned, 1)

            def empty(s, b, g):
                c, dt = g // 2, g % 2
                act.wait_ge(fronted, s * 6 + g + 1)
                if g < 4:
                    nc.scalar.activation(pre[:, g, :], psA[:, g % 2, :], ACT.Identity, bias=col[:, dt, c:c + 1]).then_inc(emptied, 1)
                else:
                    nc.scalar.activation(zs[:, b, dt, :], psA[:, g % 2, :], ACT.Copy).then_inc(emptied, 1)

            def silu(s, b):
                act.wait_ge(emptied, s * 6 + 6)
                nc.scalar.activation(pre[:, :, :], pre[:, :, :], ACT.Silu).then_inc(silu_done, 1)
                nc.scalar.activation(zs[:, b, :, :], zs[:, b, :, :], ACT.Silu).then_inc(z_done, 1)

            def to_low(s):
                act.wait_ge(projected, s + 1)
                nc.scalar.activation(low[:, :], psA[0:RANK, 0, :], ACT.Copy).then_inc(low_ready, 1)

            def soften(s):
                act.wait_ge(dt_summed, s + 1)
                for dt in range(DT):
                    last = nc.scalar.activation(absv[:, dt, :], psA[:, dt, :], ACT.Abs, bias=col[:, dt, 2:3])
                last.then_inc(abs_ready, 1)
                for dt in range(DT):
                    last = nc.scalar.activation(v[:, dt, :], psA[:, dt, :], ACT.Relu, bias=col[:, dt, 2:3])
                last.then_inc(v_ready, 1)
                act.wait_ge(abs_ready, s + 1)
                nc.scalar.activation(soft, absv, ACT.Exp, scale=-1.0).then_inc(u_ready, 1)
                act.wait_ge(u_ready, s + 1)
                nc.scalar.activation(absv, soft, ACT.Ln, bias=1.0).then_inc(l_ready, 1)

            def decay(s, b, n):
                if n == 0:
                    act.wait_ge(delta_ready, s + 1)
                if positive(s * NB + n - RA + 1):
                    act.wait_ge(h_ready, s * NB + n - RA + 1)
                for dt in range(DT):
                    last = nc.scalar.activation(dA[:, n % RA, dt, 1:], delta[:, b, dt, 1:], ACT.Exp, scale=A[:, dt, n:n + 1])
                last.then_inc(dA_ready, 1)

            def main(s, b, n):
                act.wait_ge(C_ready, s * NB + n + 1)
                if positive(s * NB + n - RC + 1):
                    act.wait_ge(hc_ready, s * NB + n - RC + 1)
                nc.scalar.activation(Cs[:, n % RC, 0, :], psC[:, :], ACT.Copy).then_inc(Cs_ready, 1)
                if n + 1 < NB:
                    decay(s, b, n + 1)
                elif there(s, 1):
                    decay(s + 1, 1 - b, 0)

            def between(s, b, turn, n):
                if there(s, -1):
                    if n == 4:
                        R.norm.act_root(nc, act, s - 1)
                    if n == 7:
                        R.act_1(nc, act, s - 1, 1 - b)
                    if n == 10:
                        R.act_2(nc, act, s - 1)
                if there(s, 1):
                    for g in EMPTY_STEPS.get(n, ()):
                        empty(s + 1, 1 - b, g)
                    if n == 7:
                        silu(s + 1, 1 - b)
                    if n == 10:
                        to_low(s + 1)
                    if n == 12:
                        soften(s + 1)
                if there(s, 2):
                    if n == 9:
                        N.act_root(nc, act, s + 2)
                    if n == 15:
                        to_hT(s + 2)

            act.wait_ge(loaded, 7 * 16)
            nc.scalar.activation(A[:, :, :], col[:, :, 4:], ACT.Exp).then_inc(exp_ready, 1)
            act.wait_ge(loose, 2)
            nc.scalar.activation(gates[:, :], gates[:, :], ACT.Exp).then_inc(exp_ready, 1)
            act.wait_ge(setup, 1)
            N.act_root(nc, act, 0)
            to_hT(0)
            for g in range(6):
                empty(0, 0, g)
            silu(0, 0)
            to_low(0)
            soften(0)
            N.act_root(nc, act, 1)
            to_hT(1)
            decay(0, 0, 0)
            run(act, main, between)
            R.norm.act_root(nc, act, BATCH - 1)
            R.act_1(nc, act, BATCH - 1, 1)
            R.act_2(nc, act, BATCH - 1)

        @block.gpsimd
        def _(pool):
            def main(s, b, n):
                pool.wait_ge(h_ready, s * NB + n + 1)
                pool.wait_ge(Cs_ready, s * NB + n + 1)
                if positive(s * NB + n - RP + 1):
                    pool.wait_ge(y_summed, s * NB + n - RP + 1)
                nc.gpsimd.tensor_tensor(HC[:, n % RP, :, :], H[:, n % RH, :, :], Cs[:, n % RC, :, :].to_broadcast([P, DT, SEQ]), ALU.mult).then_inc(hc_ready, 1)

            def between(s, b, turn, n):
                if n < 8 and there(s, -2):
                    R.pool_one(pool, s - 2, b, n)
                if n >= 8 and there(s, 3):
                    G.pool_one(pool, s + 3, 1 - b, n - 8)

            R.pool_start(pool)
            G.pool_start(pool)
            for s in range(3):
                G.pool(pool, s, s % 2)
            run(pool, main, between)
            R.pool(pool, BATCH - 2, 0)
            R.pool(pool, BATCH - 1, 1)

        @block.vector
        def _(dve):
            chain = Chain(dve, linked)

            def stats(s, b, turn):
                G.dve(nc, dve, chain, s, b, turn)
                N.dve_stats(nc, chain, s)

            def normalize(s):
                N.dve_finish(nc, dve, chain, s)
                N.dve_apply(nc, xn, s).then_inc(normed, 1)

            def mix(s, b):
                dve.wait_ge(silu_done, s + 1)
                chain(nc.vector.tensor_scalar(xc[:, b, :, :], pre[:, 0:2, :], gates[:, 0:1], None, ALU.mult))
                nc.vector.scalar_tensor_tensor(out=xc[:, b, :, :], in0=pre[:, 2:4, :], scalar=gates[:, 1:2], in1=xc[:, b, :, :],
                                               op0=ALU.mult, op1=ALU.add).then_inc(mixed, 1)

            def cut_rows(s, b):
                dve.wait_ge(projected, s + 1)
                c3 = bc3[:, b, :]
                chain(nc.vector.tensor_copy(c3, psA[0:96, 1, :]))
                chain(nc.vector.tensor_tensor(bc[0:64, :], psA[0:64, 1, :], bc3[0:64, b, :], ALU.subtract))
                chain(nc.vector.tensor_copy(bc3[0:64, b, :], bc[0:64, :]))
                chain(nc.vector.tensor_tensor(bc[0:32, :], bc[0:32, :], bc3[0:32, b, :], ALU.subtract))
                nc.vector.tensor_copy(bc3[0:32, b, :], bc[0:32, :]).then_inc(cut, 1)

            def step_sizes_1(s, b):
                dve.wait_ge(u_ready, s + 1)
                chain(nc.vector.tensor_scalar(rest[:, :, :], soft, 1.0, None, ALU.add))
                chain(nc.vector.scalar_tensor_tensor(out=rest[:, :, :], in0=rest[:, :, :], scalar=-1.0, in1=soft, op0=ALU.add, op1=ALU.subtract))

            def step_sizes_2(s, b):
                dve.wait_ge(l_ready, s + 1)
                chain(nc.vector.tensor_tensor(rest[:, :, :], absv, rest[:, :, :], ALU.subtract))
                nc.vector.tensor_tensor(delta[:, b, :, :], rest[:, :, :], v[:, :, :], ALU.add).then_inc(delta_ready, 1)
                dve.wait_ge(delta_ready, s + 1)
                nc.vector.tensor_tensor(ux[:, b, :, :], delta[:, b, :, :], xc[:, b, :, :], ALU.mult).then_inc(ux_ready, 1)

            def gated(s, b):
                dve.wait_ge(y_summed, s * NB + NB)
                for dt in range(DT):
                    last = nc.vector.scalar_tensor_tensor(out=v[:, dt, :], in0=xc[:, b, dt, :], scalar=col[:, dt, 3:4], in1=psY[:, dt, :], op0=ALU.mult, op1=ALU.add)
                last.then_inc(y_emptied, 1)
                dve.wait_ge(y_emptied, s + 1)
                dve.wait_ge(z_done, s + 1)
                nc.vector.tensor_tensor(v[:, :, :], v[:, :, :], zs[:, b, :, :], ALU.mult).then_inc(y_ready, 1)

            def add(s):
                dve.wait_ge(out_summed, s + 1)
                four = k.X[:, bass.ds(s * ST, ST), :]
                nc.vector.tensor_tensor(four, four, psR[:, :].rearrange("p (a d) -> p a d", a=ST), ALU.add).then_inc(added, 1)

            def main(s, b, n):
                if n == 0:
                    dve.wait_ge(ux_ready, s + 1)
                dve.wait_ge(B_ready, s * NB + n + 1)
                nc.vector.tensor_tensor(dBx[:, n % RB, :, :], ux[:, b, :, :], psB[:, n % 2:n % 2 + 1, :].to_broadcast([P, DT, SEQ]), ALU.mult).then_inc(dBx_done, 1)
                dve.wait_ge(dBx_done, s * NB + n + 1)
                dve.wait_ge(dA_ready, s * NB + n + 1)
                if positive(s * NB + n - RH + 1):
                    dve.wait_ge(hc_ready, s * NB + n - RH + 1)
                flat = lambda v, r: v[:, n % r, :, :].rearrange("p a t -> p (a t)")
                nc.vector.tensor_tensor_scan(flat(H, RH), flat(dA, RA), flat(dBx, RB), 0.0, ALU.mult, ALU.add).then_inc(h_ready, 1)

            def between(s, b, turn, n):
                if there(s, -1):
                    if n == 1:
                        gated(s - 1, 1 - b)
                    if n == 3:
                        add(s - 1)
                        dve.wait_ge(added, s)
                        R.norm.dve_stats(nc, chain, s - 1)
                    if n == 5:
                        R.dve_1(nc, dve, chain, s - 1, 1 - b, turn - 1 + b)
                    if n == 9:
                        R.dve_2a(nc, dve, chain, s - 1, 1 - b)
                    if n == 12:
                        R.dve_2b(nc, dve, chain, s - 1, 1 - b)
                    if n == 15:
                        R.dve_2c(nc, dve, chain, s - 1, 1 - b)
                if there(s, 1):
                    if n == 8:
                        mix(s + 1, 1 - b)
                    if n == 10:
                        cut_rows(s + 1, 1 - b)
                    if n == 13:
                        step_sizes_1(s + 1, 1 - b)
                    if n == 14:
                        step_sizes_2(s + 1, 1 - b)
                if there(s, 2):
                    if n == 7:
                        stats(s + 2, b, turn + 1)
                    if n == 11:
                        normalize(s + 2)

            dve.wait_ge(loaded, 7 * 16)
            nc.vector.tensor_reduce(gmax[:, :], gates[:, :], AX.X, ALU.max).then_inc(loose, 1)
            dve.wait_ge(loose, 1)
            nc.vector.tensor_scalar(gates[:, :], gates[:, :], gmax[:, :], None, ALU.subtract).then_inc(loose, 1)
            dve.wait_ge(exp_ready, 2)
            chain(nc.vector.tensor_reduce(gmax[:, :], gates[:, :], AX.X, ALU.add))
            chain(nc.vector.reciprocal(gmax[:, :], gmax[:, :]))
            chain(nc.vector.tensor_scalar(gates[:, :], gates[:, :], gmax[:, :], None, ALU.mult))
            nc.vector.tensor_scalar(A[:, :, :], A[:, :, :], -1.0, None, ALU.mult)
            for r in range(1, 3):
                chain(nc.vector.tensor_copy(Wx[:, :, RANK + 32 * r:RANK + 32 * r + 32], Wx[:, :, RANK:RANK + 32]))
            for c in range(2):
                for t in range(TAPS):
                    chain(nc.vector.tensor_tensor(Wtap[:, c, t, :], Win[:, 0:INNER], tap[:, c, t, :], ALU.mult))
            nc.vector.memset(hT[:, 0:PAD], 0.0)
            for r in range(RA):
                nc.vector.memset(dA[:, r, :, 0:1], 0.0)
            nc.vector.memset(R.run[:, :], 0.0).then_inc(setup, 1)
            dve.wait_ge(setup, 1)
            for b in range(2):
                G.dve_ask(nc, b, b)
            stats(0, 0, 0)
            normalize(0)
            mix(0, 0)
            cut_rows(0, 0)
            step_sizes_1(0, 0)
            step_sizes_2(0, 0)
            stats(1, 1, 0)
            normalize(1)
            links = (2 + 4) + 4 + 4 + sum(R.links()) + 1 + 4 + 3
            run(dve, main, between, chain, 2 * links)
            s, b = BATCH - 1, 1
            gated(s, b)
            add(s)
            dve.wait_ge(added, BATCH)
            nc.vector.memset(zeros, 0.0).then_inc(cleared, 1)
            R.norm.dve_stats(nc, chain, s)
            R.dve_1(nc, dve, chain, s, b, s // 2)
            R.dve_2a(nc, dve, chain, s, b)
            R.dve_2b(nc, dve, chain, s, b)
            R.dve_2c(nc, dve, chain, s, b)
            R.dve_tables(nc, dve, chain, st)


def macaron_kernel(nc, x, consts, l0_pack, l1_pack, l0_b2, l1_b2, wqkv, l0_bg, l0_wg, l1_wg, gamma, beta, w_in, taps, w_x, w_dt, w_out, col, conv_gates, out):
    k = Core()
    with ExitStack() as ctx:
        sb = lambda n, s, t=F32: ctx.enter_context(nc.sbuf_tensor(n, s, t))
        k.X = sb("X", [P, TILES, D])
        k.ident = sb("ident", [P, P])
        k.ident_bf = sb("ident_bf", [P, P], BF16)
        k.before = sb("before", [P, P], BF16)
        k.causal = sb("causal", [P, P], BF16)
        k.ones = sb("ones", [P, P], BF16)
        k.pick = sb("pick", [96, 2 * STATES, P], BF16)
        k.small = sb("small", [P, SMALL])
        k.bg = sb("bg", [P, EXPERTS])
        k.gate_w = sb("gate_w", [P, 2, EXPERTS])
        k.gamma, k.beta = sb("gamma", [P, D]), sb("beta", [P, D])
        k.gate = sb("gate", [P, TOPK, TILES])
        k.hot = sb("hot", [P, TILES, TOPK * EXPERTS])
        k.row = sb("row", [P, TILES, TOPK])
        k.idx = sb("idx", [P, TILES + 2 * SEQ_TILES, TOPK], I32)
        k.pad_row = sb("pad_row", [P, EXPERTS], I32)
        k.block_row = sb("block_row", [P, NBLK], I32)
        k.owner = sb("owner", [P, NBLK], I32)
        k.xslots = nc.dram_tensor("xslots", [DUMP + BLOCK, D], F32, kind="Internal").ap()
        k.yslots = nc.dram_tensor("yslots", [TRASH + 1, D], F32, kind="Internal").ap()

        load_stage(nc, k, x, consts, l0_bg, (l0_wg, l1_wg), gamma, beta)
        plain_stage(nc, k, "to_a", False, True)
        blocks_stage(nc, k, "a", l0_pack, l0_b2, ACT.Gelu_apprx_tanh)
        attention_stage(nc, k, wqkv)
        blocks_stage(nc, k, "b", l0_pack, l0_b2, ACT.Gelu_apprx_tanh)
        plain_stage(nc, k, "to_c", True, False)
        blocks_stage(nc, k, "c", l1_pack, l1_b2, ACT.Gelu)
        scan_stage(nc, k, {"in": w_in, "taps": taps, "x": w_x, "dt": w_dt, "out": w_out, "col": col, "gates": conv_gates})
        blocks_stage(nc, k, "d", l1_pack, l1_b2, ACT.Gelu)
        plain_stage(nc, k, "end", True, None, out)


def kernel(**inputs):
    import numpy as np
    import concourse.bacc as bacc
    from concourse.bass_utils import run_bass_kernel_spmd as run

    a = {n: np.asarray(v) for n, v in inputs.items()}

    def pack(w1, b1, w2):
        return np.concatenate([w1, w2.reshape(EXPERTS, FT, P, D).transpose(0, 2, 1, 3).reshape(EXPERTS, P, FT * D),
                               b1.reshape(EXPERTS, FT, P).transpose(0, 2, 1)], axis=2)

    r, c = np.arange(P)[:, None], np.arange(P)[None, :]
    consts = np.zeros((P, 36 * P + SMALL), np.float32)
    consts[:, 0:P] = r == c
    consts[:, P:2 * P] = r < c
    consts[:, 2 * P:3 * P] = np.where(c > r, NEG, 0.0)
    consts[:, 3 * P:4 * P] = r == c
    for n in range(32):
        consts[:96, (4 + n) * P:(5 + n) * P] = (np.arange(96) % 32 == n)[:, None]
    e = np.arange(EXPERTS)
    middle = e * REGION + TOKENS
    consts[:, 36 * P:] = np.concatenate([EXPERTS - e, np.repeat([-1, 1], EXPERTS), middle - 1, middle, middle, e, np.arange(NBLK)])
    two = lambda v: v.reshape(DT, P, -1).transpose(1, 0, 2)
    rows = lambda n: a[f"L1_attn_{n}"].reshape(INNER, -1)
    arrays = {
        "x": a["L0_attn_x"].reshape(TOKENS, D),
        "consts": consts,
        "l0_pack": pack(a["L0_ffn_W1"], a["L0_ffn_b1"], a["L0_ffn_W2"]),
        "l1_pack": pack(a["L1_ffn_w1"], a["L1_ffn_b1"], a["L1_ffn_w2"]),
        "l0_b2": a["L0_ffn_b2"], "l1_b2": a["L1_ffn_b2"],
        "wqkv": np.stack([a["L0_attn_WQ"].T, a["L0_attn_WK"].T, a["L0_attn_WV"].T], axis=1),
        "l0_bg": a["L0_ffn_bg"], "l0_wg": a["L0_ffn_Wg"], "l1_wg": a["L1_ffn_gate_w"],
        "gamma": a["L1_ffn_gamma"], "beta": a["L1_ffn_beta"],
        "w_in": a["L1_attn_W_in"].T,
        "taps": np.stack([a["L1_attn_conv_w1"].T, a["L1_attn_conv_w2"].T])[None],
        "w_x": two(a["L1_attn_W_x"].T), "w_dt": a["L1_attn_W_dt"].T, "w_out": two(a["L1_attn_W_out"].T),
        "col": two(np.concatenate([rows("conv_b1"), rows("conv_b2"), rows("b_dt"), rows("D_param"), rows("A_log")], axis=1)),
        "conv_gates": a["L1_attn_conv_gates"],
    }
    nc = bacc.Bacc("TRN2", target_bir_lowering=False, num_devices=1)
    given, args = {}, []
    for name, v in arrays.items():
        v = np.ascontiguousarray(v)
        given[f"in_{name}"] = v
        args.append(nc.dram_tensor(f"in_{name}", v.shape, mybir.dt.from_np(v.dtype), kind="ExternalInput").ap())
    args.append(nc.dram_tensor("out", (TOKENS, D), F32, kind="ExternalOutput").ap())
    macaron_kernel(nc, *args)
    return run(nc, [given], core_ids=[0]).results[0]["out"].reshape(BATCH, SEQ, D)
```

```python
import concourse.bass as bass
from concourse import mybir
from contextlib import ExitStack

F32 = mybir.dt.float32
BF16 = mybir.dt.bfloat16
I32 = mybir.dt.int32
U32 = mybir.dt.uint32
ALU = mybir.AluOpType
ACT = mybir.ActivationFunctionType
AX = mybir.AxisListType

P = 128
BATCH, SEQ, D = 16, 512, 128
TOKENS = BATCH * SEQ
TILES = TOKENS // P
SEQ_TILES = SEQ // P
EXPERTS, TOPK, HIDDEN = 8, 2, 512
FT = HIDDEN // P
BLOCK = 512
CAPACITY = -(-12 * TOKENS * TOPK // (10 * EXPERTS))
NBLK = TOKENS * TOPK // BLOCK + EXPERTS
REGION = 2 * TOKENS + BLOCK
DUMP = EXPERTS * REGION
TRASH = NBLK * BLOCK
SIGN = EXPERTS
BASE = SIGN + TOPK * EXPERTS
MIDDLE = BASE + TOPK * EXPERTS
EIGHT = MIDDLE + EXPERTS
NUMBER = EIGHT + EXPERTS
SMALL = NUMBER + NBLK
PACK = HIDDEN + FT * D + FT
EPS = 1e-5
NEG = -1e30
SCALE = D ** -0.5
INNER, STATES, RANK, TAPS = 256, 16, 64, 4
DT = INNER // P
PAD = 2 * (TAPS - 1)


class Chain:

    def __init__(self, eng, sem):
        self.eng, self.sem, self.n, self.base = eng, sem, 0, None

    def turn(self, i, per, turns):
        self.base, self.start, self.per, self.turns = i * per, self.n, per, turns

    def leave(self):
        assert self.n - self.start == self.per, (self.n - self.start, self.per)
        self.n = self.start + self.per * self.turns
        self.base = None

    def __call__(self, ins):
        ins.then_inc(self.sem, 1)
        self.n += 1
        self.eng.wait_ge(self.sem, self.n if self.base is None else self.base + self.n)


class Core:
    pass


class Stage:

    def __init__(self, nc, name):
        self.nc, self.name, self.ctx, self.sems = nc, name, ExitStack(), []

    def sem(self, n):
        self.sems.append(self.nc.alloc_semaphore(f"{self.name}_{n}"))
        return self.sems[-1]

    def sb(self, n, shape, dtype=F32):
        return self.ctx.enter_context(self.nc.sbuf_tensor(f"{self.name}_{n}", shape, dtype))

    def pb(self, n, shape, dtype=F32):
        return self.ctx.enter_context(self.nc.psum_tensor(f"{self.name}_{n}", shape, dtype))

    def block(self):
        return self.ctx.enter_context(self.nc.Block())

    def __enter__(self):
        return self

    def __exit__(self, *error):
        self.ctx.__exit__(*error)
        if error[0] is None:
            self.nc.clear_and_free_semaphores(self.sems)
            self.nc.all_engine_barrier()


def rows_of(x, t, n=1):
    v = x[:, bass.ds(t, n), :]
    return v.rearrange("p a d -> p (a d)") if n == 1 else v


def sequences(eng, body, chain=None, links=0, steps=BATCH):
    turns = (steps - 4) // 2
    for s in range(3):
        body(s, s % 2, s // 2, s == 0, False)
    with eng.Fori(0, turns) as i:
        if chain is not None:
            chain.turn(i, links, turns)
        body(i * 2 + 3, 1, i + 1, False, False)
        body(i * 2 + 4, 0, i + 2, False, False)
        if chain is not None:
            chain.leave()
    body(steps - 1, 1, steps // 2 - 1, False, True)


class Norm:

    def __init__(self, st, k, name, double=False, tiles=SEQ_TILES):
        self.k, self.w, self.tiles = k, 2 if double else 1, tiles
        self.asked, self.logged, self.rooted, self.begun = (st.sem(f"{name}_{n}") for n in ("asked", "logged", "rooted", "begun"))
        self.stats = st.sb(f"{name}_stats", [P, tiles, 6])
        self.mean, self.odd, self.var = (st.sb(f"{name}_{n}", [P, tiles]) for n in ("mean", "odd", "var"))
        self.shifted, self.root, self.newton, self.rstd = (st.sb(f"{name}_{n}", [P, self.w, tiles]) for n in ("shifted", "root", "newton", "rstd"))

    def dve_stats(self, nc, chain, s):
        chain.eng.sem_inc(self.begun, 1)
        st, m, o, v = self.stats, self.mean, self.odd, self.var
        for j in range(self.tiles):
            last = nc.vector.bn_stats(st[:, j, :], rows_of(self.k.X, s * self.tiles + j))
        chain(last)
        nc.vector.tensor_tensor(m[:, :], st[:, :, 1], st[:, :, 4], ALU.add)
        nc.vector.tensor_tensor(v[:, :], st[:, :, 2], st[:, :, 5], ALU.add)
        chain(nc.vector.tensor_tensor(o[:, :], st[:, :, 1], st[:, :, 4], ALU.subtract))
        nc.vector.tensor_scalar(m[:, :], m[:, :], 0.5, None, ALU.mult)
        chain(nc.vector.scalar_tensor_tensor(out=o[:, :], in0=o[:, :], scalar=0.25, in1=o[:, :], op0=ALU.mult, op1=ALU.mult))
        chain(nc.vector.scalar_tensor_tensor(out=v[:, :], in0=v[:, :], scalar=1.0 / D, in1=o[:, :], op0=ALU.mult, op1=ALU.add))
        last = nc.vector.tensor_scalar(self.shifted[:, 0, :], v[:, :], EPS, None, ALU.add)
        if self.w == 2:
            last = nc.vector.tensor_scalar(self.shifted[:, 1, :], v[:, :], 1.0 + EPS, EPS * EPS, ALU.mult, ALU.add)
        last.then_inc(self.asked, 1)

    def act_root(self, nc, act, s):
        act.wait_ge(self.asked, s + 1)
        nc.scalar.activation(self.root[:, :, :], self.shifted[:, :, :], ACT.Ln).then_inc(self.logged, 1)
        act.wait_ge(self.logged, s + 1)
        nc.scalar.activation(self.root[:, :, :], self.root[:, :, :], ACT.Exp, scale=-0.5).then_inc(self.rooted, 1)

    def dve_finish(self, nc, dve, chain, s):
        dve.wait_ge(self.rooted, s + 1)
        chain(nc.vector.scalar_tensor_tensor(out=self.newton[:, :, :], in0=self.root[:, :, :], scalar=-0.5, in1=self.root[:, :, :], op0=ALU.mult, op1=ALU.mult))
        chain(nc.vector.tensor_tensor(self.newton[:, :, :], self.newton[:, :, :], self.shifted[:, :, :], ALU.mult))
        chain(nc.vector.scalar_tensor_tensor(out=self.rstd[:, :, :], in0=self.newton[:, :, :], scalar=1.5, in1=self.root[:, :, :], op0=ALU.add, op1=ALU.mult))

    def dve_apply(self, nc, out, s):
        for j in range(self.tiles):
            last = nc.vector.tensor_scalar(out[:, j, :], rows_of(self.k.X, s * self.tiles + j), self.mean[:, j:j + 1],
                                           self.rstd[:, self.w - 1, j:j + 1], ALU.subtract, ALU.mult)
        return last


class Router:

    def __init__(self, st, k, first, psT, psL, psP, tiles=SEQ_TILES):
        self.k, self.first, self.psT, self.psL, self.psP = k, first, psT, psL, psP
        T = self.tiles = tiles
        self.copies = TOPK * tiles
        self.norm = Norm(st, k, "r", double=not first, tiles=tiles)
        self.normed, self.flipped, self.turned, self.scored, self.centred = map(st.sem, ("r_normed", "r_flipped", "r_turned", "r_scored", "r_centred"))
        self.exped, self.chosen, self.placed, self.rowed, self.taken = map(st.sem, ("r_exped", "r_chosen", "r_placed", "r_rowed", "r_taken"))
        self.scattered = [st.sem(f"r_scattered{i}") for i in range(2 * self.copies)]
        self.zeroed, self.tabled = st.sem("r_zeroed"), st.sem("r_tabled")
        self.xn = st.sb("r_xn", [P, 2, T, D])
        self.xnT = st.sb("r_xnT", [P, T * P])
        self.L, self.prob, self.work = (st.sb(f"r_{n}", [P, T, EXPERTS]) for n in ("L", "prob", "work"))
        self.top, self.inv = st.sb("r_top", [P, T]), st.sb("r_inv", [P, T])
        self.pv = st.sb("r_pv", [P, 2, T])
        self.hot_bf = st.sb("r_hot_bf", [P, T, TOPK * EXPERTS], BF16)
        self.pos = st.sb("r_pos", [P, T, TOPK * EXPERTS])
        self.run = st.sb("r_run", [P, TOPK * EXPERTS])
        self.row = st.sb("r_row", [P, T, TOPK])
        self.idx = st.sb("r_idx", [P, 2, T * TOPK], I32)

    def four(self, s):
        return bass.ds(s * self.tiles, self.tiles)

    def dve_1(self, nc, dve, chain, s, b, turn):
        k, n = self.k, self.norm
        n.dve_finish(nc, dve, chain, s)
        if not (isinstance(turn, int) and turn == 0):
            for i in range(self.copies):
                dve.wait_ge(self.scattered[self.copies * b + i], turn * 16)
        last = n.dve_apply(nc, self.xn[:, b, :, :], s)
        last.then_inc(self.normed, 1)
        if not self.first:
            chain(nc.vector.scalar_tensor_tensor(out=n.odd[:, :], in0=n.mean[:, :], scalar=-0.5, in1=n.rstd[:, 0, :], op0=ALU.mult, op1=ALU.mult))
            chain(nc.vector.tensor_scalar(n.rstd[:, 0, :], n.rstd[:, 0, :], 0.5, 1.0, ALU.mult, ALU.add))
            for j in range(self.tiles):
                x = rows_of(k.X, s * self.tiles + j)
                last = nc.vector.tensor_scalar(x, x, n.rstd[:, 0, j:j + 1], n.odd[:, j:j + 1], ALU.mult, ALU.add)
            chain(last)

    def pe_1(self, nc, pe, s, b):
        self.pe_1a(nc, pe, s, b)
        self.pe_1b(nc, pe, s, b)

    def pe_1a(self, nc, pe, s, b):
        psT = self.psT(b)
        pe.wait_ge(self.normed, s + 1)
        for j in range(self.tiles):
            last = nc.tensor.transpose(psT[:, j * P:(j + 1) * P], self.xn[:, b, j, :], self.k.ident[:, :])
        last.then_inc(self.flipped, 1)

    def pe_1b(self, nc, pe, s, b):
        psL = self.psL(b)
        pe.wait_ge(self.turned, s + 1)
        for j in range(self.tiles):
            last = nc.tensor.matmul(psL[:, j * EXPERTS:(j + 1) * EXPERTS], self.xnT[:, j * P:(j + 1) * P], self.k.gate_w[:, 0 if self.first else 1, :], start=True, stop=True)
        last.then_inc(self.scored, 1)

    def act_1(self, nc, act, s, b):
        act.wait_ge(self.flipped, s + 1)
        if self.first:
            nc.scalar.activation(self.xnT[:, :], self.psT(b), ACT.Copy).then_inc(self.turned, 1)
        else:
            nc.scalar.activation(self.xnT[:, :], self.psT(b), ACT.Identity, scale=self.k.gamma[:, :], bias=self.k.beta[:, :]).then_inc(self.turned, 1)

    def all4(self, v):
        return v.rearrange("p (a c) -> p a c", a=1).to_broadcast([P, self.tiles, TOPK * EXPERTS])

    def wide(self, v):
        return v.rearrange("p (t a) -> p t a", a=1).to_broadcast([P, self.tiles, EXPERTS])

    def dve_2a(self, nc, dve, chain, s, b):
        L, src = self.L, self.psL(b)[:, 0:self.tiles * EXPERTS].rearrange("p (t e) -> p t e", t=self.tiles)
        dve.wait_ge(self.scored, s + 1)
        if self.first:
            chain(nc.vector.tensor_tensor(L[:, :, :], src, self.k.bg[:, :].rearrange("p (a e) -> p a e", a=1).to_broadcast([P, self.tiles, EXPERTS]), ALU.add))
            src = L[:, :, :]
        chain(nc.vector.tensor_reduce(self.top[:, :], src, AX.X, ALU.max))
        nc.vector.tensor_tensor(L[:, :, :], src, self.wide(self.top[:, :]), ALU.subtract).then_inc(self.centred, 1)

    def act_2(self, nc, act, s):
        act.wait_ge(self.centred, s + 1)
        nc.scalar.activation(self.prob[:, :, :], self.L[:, :, :], ACT.Exp).then_inc(self.exped, 1)

    def dve_2b(self, nc, dve, chain, s, b):
        k, prob, work = self.k, self.prob, self.work
        hot = k.hot[:, self.four(s), :]
        rank = k.small[:, 0:EXPERTS].rearrange("p (a e) -> p a e", a=1).to_broadcast([P, self.tiles, EXPERTS])
        dve.wait_ge(self.exped, s + 1)
        for c in range(TOPK):
            h = hot[:, :, c * EXPERTS:(c + 1) * EXPERTS]
            chain(nc.vector.tensor_reduce(self.pv[:, c, :], prob[:, :, :], AX.X, ALU.max))
            chain(nc.vector.tensor_tensor(work[:, :, :], prob[:, :, :], self.wide(self.pv[:, c, :]), ALU.is_equal))
            chain(nc.vector.tensor_tensor(work[:, :, :], work[:, :, :], rank, ALU.mult))
            chain(nc.vector.tensor_reduce(self.top[:, :], work[:, :, :], AX.X, ALU.max))
            chain(nc.vector.tensor_tensor(h, work[:, :, :], self.wide(self.top[:, :]), ALU.is_equal))
            if c == 0:
                chain(nc.vector.scalar_tensor_tensor(out=prob[:, :, :], in0=h, scalar=-4.0, in1=prob[:, :, :], op0=ALU.mult, op1=ALU.add))
        nc.vector.tensor_tensor(self.hot_bf[:, :, :], hot, self.all4(k.small[:, SIGN:SIGN + TOPK * EXPERTS]), ALU.mult).then_inc(self.chosen, 1)
        chain(nc.vector.tensor_tensor(self.inv[:, :], self.pv[:, 0, :], self.pv[:, 1, :], ALU.add))
        chain(nc.vector.reciprocal(self.inv[:, :], self.inv[:, :]))
        for c in range(TOPK):
            nc.vector.scalar_tensor_tensor(out=k.gate[:, c, self.four(s)], in0=self.pv[:, c, :], scalar=0.5, in1=self.inv[:, :], op0=ALU.mult, op1=ALU.mult)

    def pe_2(self, nc, pe, s, b):
        psP, W, T = self.psP(b), TOPK * EXPERTS, self.tiles
        pe.wait_ge(self.chosen, s + 1)
        for j in range(T + 1):
            for i in range(j):
                last = nc.tensor.matmul(psP[:, j * W:(j + 1) * W], self.k.ones[:, :], self.hot_bf[:, i, :], start=(i == 0), stop=(j == T and i == T - 1))
            if j < T:
                last = nc.tensor.matmul(psP[:, j * W:(j + 1) * W], self.k.before[:, :], self.hot_bf[:, j, :], start=(j == 0), stop=True)
        last.then_inc(self.placed, 1)

    def dve_2c(self, nc, dve, chain, s, b):
        k, W, T = self.k, TOPK * EXPERTS, self.tiles
        psP, pos = self.psP(b), self.pos
        dve.wait_ge(self.placed, s + 1)
        chain(nc.vector.tensor_tensor(pos[:, :, :], psP[:, 0:T * W].rearrange("p (t c) -> p t c", t=T), self.all4(self.run[:, :]), ALU.add))
        nc.vector.tensor_tensor(self.run[:, :], psP[:, T * W:(T + 1) * W], self.run[:, :], ALU.add)
        chain(nc.vector.tensor_tensor(pos[:, :, :], pos[:, :, :], k.hot[:, self.four(s), :], ALU.mult))
        chain(nc.vector.tensor_reduce(self.row[:, :, :], pos[:, :, :].rearrange("p t (c e) -> p t c e", c=TOPK), AX.X, ALU.add))
        nc.vector.tensor_scalar(k.row[:, self.four(s), :], self.row[:, :, :], 1.0, None, ALU.mult)
        nc.vector.tensor_copy(self.idx[:, b, :], self.row[:, :, :].rearrange("p t c -> p (t c)")).then_inc(self.rowed, 1)

    def dve_start(self, nc):
        return nc.vector.tensor_copy(self.run[:, :], self.k.small[:, BASE:BASE + TOPK * EXPERTS])

    def links(self):
        return (3, 2, 11 + 2, 3) if self.first else (3 + 3, 1, 11 + 2, 3)

    def pool_start(self, pool):
        self.last_row = pool.to_reg(DUMP - 1)

    def pool(self, pool, s, b):
        for i in range(self.copies):
            self.pool_one(pool, s, b, i)

    def pool_one(self, pool, s, b, i):
        if i == 0:
            pool.wait_ge(self.rowed, s + 1)
            pool.sem_inc(self.taken, 1)
        pool.indirect_dma_start(out=self.k.xslots[:, :], out_offset=bass.IndirectOffsetOnAxis(ap=self.idx[:, b, i:i + 1].bitcast(U32), axis=0),
                                in_=self.xn[:, b, i // 2, :], in_offset=None, bounds_check=self.last_row, oob_is_err=False).then_inc(self.scattered[self.copies * b + i], 16)

    def dve_tables(self, nc, dve, chain, st):
        k, E = self.k, EXPERTS
        names = "n1 start length nblk end before ones".split()
        n1, start, length, nblk, end, before, ones = (st.sb(f"r_{n}", [P, E]) for n in names)
        count_i = st.sb("r_count_i", [P, E], I32)
        owner, late = (st.sb(f"r_{n}", [P, NBLK, E]) for n in ("owner", "late"))
        of_block, row_f = st.sb("r_of_block", [P, NBLK]), st.sb("r_row_f", [P, NBLK])
        middle = k.small[:, MIDDLE:MIDDLE + E]
        per_block = lambda v: v.rearrange("p (a e) -> p a e", a=1).to_broadcast([P, NBLK, E])
        number = k.small[:, NUMBER:NUMBER + NBLK]
        numbers = number.rearrange("p (n a) -> p n a", a=1).to_broadcast([P, NBLK, E])
        counts = st.sb("r_counts", [P, TOPK * E])
        first_n, second_n = counts[:, 0:E], counts[:, E:2 * E]
        limit, shift = k.limit, k.shift
        chain(nc.vector.tensor_tensor(counts[:, :], self.run[:, :], k.small[:, BASE:BASE + TOPK * E], ALU.subtract))
        chain(nc.vector.tensor_tensor(counts[:, :], counts[:, :], k.small[:, SIGN:SIGN + TOPK * E], ALU.mult))
        chain(nc.vector.memset(ones[:, :], 1.0))
        chain(nc.vector.tensor_tensor(length[:, :], first_n, second_n, ALU.add))
        if self.first:
            chain(nc.vector.tensor_scalar(n1[:, :], first_n, float(CAPACITY), None, ALU.min))
            chain(nc.vector.tensor_scalar(length[:, :], length[:, :], float(CAPACITY), None, ALU.min))
            chain(nc.vector.tensor_scalar(limit[:, 0, :], middle, float(-CAPACITY), None, ALU.add))
            chain(nc.vector.tensor_tensor(limit[:, 1, :], middle, first_n, ALU.subtract))
            chain(nc.vector.tensor_scalar(limit[:, 1, :], limit[:, 1, :], float(CAPACITY), None, ALU.add))
        else:
            chain(nc.vector.tensor_copy(n1[:, :], first_n))
        chain(nc.vector.tensor_tensor(start[:, :], middle, n1[:, :], ALU.subtract))
        chain(nc.vector.tensor_tensor(nblk[:, :], start[:, :], length[:, :], ALU.add))
        nc.vector.tensor_copy(k.pad_row[:, :], nblk[:, :]).then_inc(self.tabled, 1)
        chain(nc.vector.tensor_scalar(length[:, :], length[:, :], float(BLOCK - 1), None, ALU.add))
        chain(nc.vector.tensor_copy(count_i[:, :], length[:, :]))
        chain(nc.vector.tensor_scalar(count_i[:, :], count_i[:, :], BLOCK.bit_length() - 1, None, ALU.arith_shift_right))
        chain(nc.vector.tensor_copy(nblk[:, :], count_i[:, :]))
        chain(nc.vector.tensor_tensor_scan(end[:, :], ones[:, :], nblk[:, :], 0.0, ALU.mult, ALU.add))
        chain(nc.vector.tensor_tensor(before[:, :], end[:, :], nblk[:, :], ALU.subtract))
        chain(nc.vector.scalar_tensor_tensor(out=shift[:, :], in0=before[:, :], scalar=float(BLOCK), in1=start[:, :], op0=ALU.mult, op1=ALU.subtract))
        chain(nc.vector.tensor_tensor(owner[:, :, :], per_block(before[:, :]), numbers, ALU.is_le))
        chain(nc.vector.tensor_tensor(late[:, :, :], per_block(end[:, :]), numbers, ALU.is_gt))
        chain(nc.vector.tensor_tensor(owner[:, :, :], owner[:, :, :], late[:, :, :], ALU.mult))
        chain(nc.vector.tensor_reduce(of_block[:, :], owner[:, :, :], AX.X, ALU.add))
        chain(nc.vector.tensor_scalar(before[:, :], before[:, :], float(-BLOCK), float(-DUMP), ALU.mult, ALU.add))
        chain(nc.vector.tensor_tensor(start[:, :], start[:, :], before[:, :], ALU.add))
        chain(nc.vector.tensor_tensor(late[:, :, :], owner[:, :, :], per_block(start[:, :]), ALU.mult))
        chain(nc.vector.tensor_reduce(row_f[:, :], late[:, :, :], AX.X, ALU.add))
        chain(nc.vector.tensor_tensor(of_block[:, :], of_block[:, :], number, ALU.mult))
        chain(nc.vector.tensor_scalar(of_block[:, :], of_block[:, :], float(BLOCK), float(DUMP), ALU.mult, ALU.add))
        chain(nc.vector.tensor_tensor(row_f[:, :], row_f[:, :], of_block[:, :], ALU.add))
        chain(nc.vector.tensor_copy(k.block_row[:, :], row_f[:, :]))
        chain(nc.vector.tensor_tensor(late[:, :, :], owner[:, :, :], per_block(k.small[:, EIGHT:EIGHT + E]), ALU.mult))
        chain(nc.vector.tensor_reduce(of_block[:, :], late[:, :, :], AX.X, ALU.add))
        nc.vector.tensor_copy(k.owner[:, :], of_block[:, :])

    def sp_pads(self, nc, sp, zeros, cleared):
        sp.wait_ge(self.tabled, 1)
        sp.wait_ge(cleared, 1)
        for s in range(2 * self.copies):
            sp.wait_ge(self.scattered[s], TILES // self.tiles // 2 * 16)
        for e in range(EXPERTS):
            r = sp.value_load(self.k.pad_row[0:1, e:e + 1], min_val=0, max_val=DUMP - BLOCK)
            sp.dma_start(self.k.xslots[bass.ds(r, BLOCK), :].rearrange("(p r) d -> p (r d)", p=P), zeros[:, :]).then_inc(self.zeroed, 16)
        sp.wait_ge(self.zeroed, EXPERTS * 16)


class Gather:

    def __init__(self, st, k, tiles=SEQ_TILES):
        self.k, self.tiles, self.copies = k, tiles, TOPK * tiles
        self.gathered = [st.sem(f"g_gathered{i}") for i in range(2 * self.copies)]
        self.idx_ready, self.taken = st.sem("g_idx_ready"), st.sem("g_taken")
        self.rows = st.sb("g_rows", [P, 2, self.copies, D])
        self.idx = st.sb("g_idx", [P, 2, self.copies], I32)

    def dve_ask(self, nc, s, b):
        nc.vector.tensor_scalar(self.idx[:, b, :], self.k.idx[:, bass.ds(s * self.tiles, self.tiles), :].rearrange("p t c -> p (t c)"), 1.0, None, ALU.mult).then_inc(self.idx_ready, 1)

    def dve(self, nc, dve, chain, s, b, turn):
        for c in range(TOPK):
            for j in range(self.tiles):
                x = rows_of(self.k.X, s * self.tiles + j)
                dve.wait_ge(self.gathered[self.copies * b + 2 * j + c], turn * 16 + 16)
                last = nc.vector.scalar_tensor_tensor(out=x, in0=self.rows[:, b, 2 * j + c, :], scalar=self.k.gate[:, c, bass.ds(s * self.tiles + j, 1)],
                                                      in1=x, op0=ALU.mult, op1=ALU.add)
            chain(last)
        self.dve_ask(nc, s + 2, b)

    def pool_start(self, pool):
        self.last_row = pool.to_reg(TRASH)

    def pool(self, pool, s, b):
        for i in range(self.copies):
            self.pool_one(pool, s, b, i)

    def pool_one(self, pool, s, b, i):
        if i == 0:
            pool.wait_ge(self.idx_ready, s + 1)
            pool.sem_inc(self.taken, 1)
        pool.indirect_dma_start(out=self.rows[:, b, i, :], out_offset=None, in_=self.k.yslots[:, :],
                                in_offset=bass.IndirectOffsetOnAxis(ap=self.idx[:, b, i:i + 1].bitcast(U32), axis=0),
                                bounds_check=self.last_row, oob_is_err=False).then_inc(self.gathered[self.copies * b + i], 16)


def plain_stage(nc, k, name, gather, route, out=None):
    routing = route is not None
    tiles = 2 * SEQ_TILES if routing else SEQ_TILES
    steps = TILES // tiles
    with Stage(nc, name) as st:
        G = Gather(st, k, tiles) if gather else None
        linked, cleared, added = st.sem("linked"), st.sem("cleared"), st.sem("added")
        if routing:
            psT, psL, psP = st.pb("psT", [P, tiles * P]), st.pb("psL", [P, 2, BLOCK]), st.pb("psP", [P, BLOCK])
            R = Router(st, k, route, lambda b: psT[:, :], lambda b: psL[:, b, :], lambda b: psP[:, :], tiles)
            zeros = st.sb("zeros", [P, BLOCK])
        saved = st.sem("saved")
        block = st.block()

        def order(eng, head, tail, chain=None, links=0):
            head(0, 0, 0)
            sequences(eng, lambda s, b, turn, first, last: ((None if last else head(s + 1, 1 - b, turn + b)), tail(s, b)), chain, links, steps)

        @block.vector
        def _(dve):
            chain = Chain(dve, linked)
            if routing:
                nc.vector.memset(zeros[:, :], 0.0).then_inc(cleared, 1)
                chain(R.dve_start(nc))
            if gather:
                for b in range(2):
                    G.dve_ask(nc, b, b)

            def head(s, b, turn):
                if gather:
                    G.dve(nc, dve, chain, s, b, turn)
                    if not routing:
                        dve.sem_inc(added, 1)
                if routing:
                    R.norm.dve_stats(nc, chain, s)
                    R.dve_1(nc, dve, chain, s, b, turn)

            def tail(s, b):
                if routing:
                    R.dve_2a(nc, dve, chain, s, b)
                    R.dve_2b(nc, dve, chain, s, b)
                    R.dve_2c(nc, dve, chain, s, b)

            links = (2 if gather else 0) + (sum(R.links()) + 4 if routing else 0)
            order(dve, head, tail, chain, 2 * links)
            if routing:
                R.dve_tables(nc, dve, chain, st)

        if routing:
            @block.scalar
            def _(act):
                act.preload_act_table_set("natural_log_exp_and_others")
                order(act, lambda s, b, turn: (R.norm.act_root(nc, act, s), R.act_1(nc, act, s, b)), lambda s, b: R.act_2(nc, act, s))

            @block.tensor
            def _(pe):
                order(pe, lambda s, b, turn: R.pe_1(nc, pe, s, b), lambda s, b: R.pe_2(nc, pe, s, b))

        @block.gpsimd
        def _(pool):
            if routing:
                R.pool_start(pool)
            if gather:
                G.pool_start(pool)
                G.pool(pool, 0, 0)
                G.pool(pool, 1, 1)
            sequences(pool, lambda s, b, turn, first, last: (G.pool(pool, s + 2, b) if gather and not last else None, R.pool(pool, s, b) if routing else None), steps=steps)
            if gather:
                for i in range(G.copies):
                    pool.wait_ge(G.gathered[i], (steps // 2 + 1) * 16)

        @block.sync
        def _(sp):
            if routing:
                R.sp_pads(nc, sp, zeros, cleared)
            if out is not None:
                with sp.Fori(0, BATCH) as s:
                    sp.wait_ge(added, s + 1)
                    sp.dma_start(out[bass.ds(s * SEQ, SEQ), :].rearrange("(t p) d -> p t d", p=P), k.X[:, bass.ds(s * 4, 4), :]).then_inc(saved, 16)
                sp.wait_ge(saved, BATCH * 16)


def load_stage(nc, k, x, consts, l0_bg, gate_w, gamma, beta):
    with Stage(nc, "load") as st:
        loaded, zeroed, cleared = map(st.sem, ("loaded", "zeroed", "cleared"))
        zeros = st.sb("zeros", [P, BLOCK])
        raw = st.sb("raw", [P, 35 * P])
        block = st.block()

        @block.sync
        def _(sp):
            wide = lambda v: v.rearrange("(a e) -> a e", a=1)
            for dst, src in ((raw[:, :], consts[:, P:36 * P]), (k.ident[:, :], consts[:, 0:P]), (k.small[:, :], consts[:, 36 * P:]),
                             (k.bg[:, :], wide(l0_bg).to_broadcast([P, EXPERTS])), (k.gamma[:, :], gamma.rearrange("(p a) -> p a", a=1)),
                             (k.beta[:, :], beta.rearrange("(p a) -> p a", a=1)), (k.gate_w[:, 0, :], gate_w[0]), (k.gate_w[:, 1, :], gate_w[1]),
                             (k.X[:, :, :], x.rearrange("(t p) d -> p t d", p=P))):
                sp.dma_start(dst, src).then_inc(loaded, 16)
            sp.wait_ge(loaded, 9 * 16)

        @block.scalar
        def _(act):
            act.wait_ge(cleared, 1)
            act.dma_start(k.xslots[DUMP:DUMP + BLOCK, :].rearrange("(p r) d -> p (r d)", p=P), zeros[:, :]).then_inc(zeroed, 16)
            act.dma_start(k.yslots[TRASH:TRASH + 1, :], zeros[0:1, 0:D]).then_inc(zeroed, 16)
            act.wait_ge(zeroed, 32)

        @block.vector
        def _(dve):
            nc.vector.memset(k.ones[:, :], 1.0)
            nc.vector.memset(k.idx[:, TILES:, :], TRASH)
            nc.vector.memset(zeros[:, :], 0.0).then_inc(cleared, 1)
            dve.wait_ge(loaded, 9 * 16)
            nc.vector.tensor_copy(k.before[:, :], raw[:, 0:P])
            nc.vector.tensor_copy(k.causal[:, :], raw[:, P:2 * P])
            nc.vector.tensor_copy(k.ident_bf[:, :], raw[:, 2 * P:3 * P])
            nc.vector.tensor_copy(k.pick[:, :, :].rearrange("p n m -> p (n m)"), raw[0:96, 3 * P:])


def place_rows(nc, k, st, chain, capped):
    mine, per_token, keep = st.sb("mine", [P, TILES, EXPERTS]), st.sb("per_token", [P, TILES]), st.sb("keep", [P, TILES])
    E = EXPERTS
    per_tile = lambda v: v.rearrange("p (a e) -> p a e", a=1).to_broadcast([P, TILES, E])
    for c in range(TOPK):
        hot, row = k.hot[:, :, c * E:(c + 1) * E], k.row[:, :, c]
        if capped:
            chain(nc.vector.tensor_tensor(mine[:, :, :], hot, per_tile(k.limit[:, c, :]), ALU.mult))
            chain(nc.vector.tensor_reduce(per_token[:, :], mine[:, :, :], AX.X, ALU.add))
            chain(nc.vector.tensor_tensor(keep[:, :], row, per_token[:, :], ALU.is_lt if c else ALU.is_ge))
        chain(nc.vector.tensor_tensor(mine[:, :, :], hot, per_tile(k.shift[:, :]), ALU.mult))
        chain(nc.vector.tensor_reduce(per_token[:, :], mine[:, :, :], AX.X, ALU.add))
        chain(nc.vector.tensor_tensor(row, row, per_token[:, :], ALU.add))
        if capped:
            chain(nc.vector.tensor_scalar(row, row, float(-TRASH), None, ALU.add))
            chain(nc.vector.tensor_tensor(row, row, keep[:, :], ALU.mult))
            chain(nc.vector.tensor_scalar(row, row, float(TRASH), None, ALU.add))
    chain(nc.vector.tensor_copy(k.idx[:, 0:TILES, :], k.row[:, :, :]))


def blocks_stage(nc, k, name, pack, down_bias, gelu, affine=False):
    with Stage(nc, name) as st:
        sem, sb, pb = st.sem, st.sb, st.pb
        w_ready = [sem(f"w_ready{i}") for i in range(2)]
        x_ready = [sem(f"x_ready{i}") for i in range(2)]
        stored = [sem(f"stored{i}") for i in range(2)]
        linked, x_flipped, xT_ready, h_summed, h_ready, y_summed, y_ready = map(
            sem, ("linked", "x_flipped", "xT_ready", "h_summed", "h_ready", "y_summed", "y_ready"))
        W = sb("W", [P, 2, PACK])
        b2 = sb("b2", [P, 2, 1, D])
        xs = sb("xs", [P, 2, 4, D])
        xT = sb("xT", [P, 2, BLOCK])
        H = sb("H", [P, 2, FT, BLOCK])
        yr = sb("yr", [P, 2, 4, D])
        psX = pb("psX", [P, 4, P])
        psH = pb("psH", [P, FT, BLOCK])
        psY = pb("psY", [P, 2, 4, P])
        block = st.block()

        TURNS = NBLK // 2

        def turns(eng, one):
            one(0, 0, 0, True, False)
            one(1, 1, 0, False, False)
            with eng.Fori(1, TURNS - 1) as j2:
                for b in range(2):
                    one(j2 * 2 + b, b, j2, False, False)
            one(NBLK - 2, 0, TURNS - 1, False, False)
            one(NBLK - 1, 1, TURNS - 1, False, True)

        @block.sync
        def _(sp):
            def load(j, b, waits):
                r = sp.value_load(k.block_row[0:1, bass.ds(j, 1)], min_val=0, max_val=DUMP)
                e = sp.value_load(k.owner[0:1, bass.ds(j, 1)], min_val=0, max_val=EXPERTS - 1)
                if waits:
                    sp.wait_ge(x_flipped, j - 1)
                sp.dma_start(xs[:, b, :, :], k.xslots[bass.ds(r, BLOCK), :].rearrange("(p s) d -> p s d", p=P)).then_inc(x_ready[b], 16)
                if waits:
                    sp.wait_ge(y_ready, j - 1)
                sp.dma_start(W[:, b, :], pack[bass.ds(e, 1), :, :].rearrange("a p n -> (a p) n")).then_inc(w_ready[b], 16)
                sp.dma_start(b2[:, b, 0, :], down_bias[bass.ds(e, 1), :].to_broadcast([P, D])).then_inc(w_ready[b], 16)

            def store(j, b):
                sp.wait_ge(y_ready, j + 1)
                sp.dma_start(k.yslots[bass.ds(j * BLOCK, BLOCK), :].rearrange("(p s) d -> p s d", p=P), yr[:, b, :, :]).then_inc(stored[b], 16)

            for b in range(2):
                load(b, b, False)
            with sp.Fori(1, TURNS) as j2:
                for b in range(2):
                    load(j2 * 2 + b, b, True)
                    store(j2 * 2 + b - 2, b)
            for b in range(2):
                store(NBLK - 2 + b, b)
                sp.wait_ge(stored[b], TURNS * 16)

        @block.tensor
        def _(pe):
            def flip_in(j, b, turn):
                pe.wait_ge(x_ready[b], turn * 16 + 16)
                for s in range(4):
                    last = nc.tensor.transpose(psX[:, s, :], xs[:, b, s, :], k.ident[:, :])
                last.then_inc(x_flipped, 1)

            def one(j, b, j2, first_block, last_block):
                pe.wait_ge(w_ready[b], j2 * 32 + 32)
                pe.wait_ge(xT_ready, j + 1)
                for f in range(FT):
                    nc.tensor.matmul(psH[:, f, :], W[:, b, f * P:(f + 1) * P], xT[:, b, :], start=True, stop=True).then_inc(h_summed, 1)
                if not last_block:
                    flip_in(j + 1, 1 - b, j2 + b)
                if not (isinstance(j, int) and j < 2):
                    pe.wait_ge(y_ready, j - 1)
                for f in range(FT):
                    pe.wait_ge(h_ready, j * FT + f + 1)
                    for s in range(4):
                        last = nc.tensor.matmul(psY[:, b, s, :], H[:, b, f, s * P:(s + 1) * P], W[:, b, HIDDEN + f * D:HIDDEN + (f + 1) * D],
                                                start=(f == 0 and s == 0), stop=(f == FT - 1 and s == 3))
                last.then_inc(y_summed, 1)

            flip_in(0, 0, 0)
            turns(pe, one)

        @block.scalar
        def _(act):
            with act.Fori(0, TURNS) as j2:
                for b in range(2):
                    for f in range(FT):
                        act.wait_ge(h_summed, (j2 * 2 + b) * FT + f + 1)
                        nc.scalar.activation(H[:, b, f, :], psH[:, f, :], gelu, bias=W[:, b, HIDDEN + FT * D + f:HIDDEN + FT * D + f + 1]).then_inc(h_ready, 1)

        @block.vector
        def _(dve):
            def turn_in(j, b):
                dve.wait_ge(x_flipped, j + 1)
                rows = psX[:, :, :].rearrange("p a d -> p (a d)")
                if affine:
                    nc.vector.tensor_scalar(xT[:, b, :], rows, k.gamma[:, :], k.beta[:, :], ALU.mult, ALU.add).then_inc(xT_ready, 1)
                else:
                    nc.vector.tensor_copy(xT[:, b, :], rows).then_inc(xT_ready, 1)

            def one(j, b, j2, first_block, last_block):
                if not last_block:
                    turn_in(j + 1, 1 - b)
                if first_block:
                    place_rows(nc, k, st, Chain(dve, linked), not affine)
                dve.wait_ge(y_summed, j + 1)
                if not (isinstance(j2, int) and j2 == 0):
                    dve.wait_ge(stored[b], j2 * 16)
                nc.vector.tensor_tensor(yr[:, b, :, :], psY[:, b, :, :], b2[:, b, :, :].to_broadcast([P, 4, D]), ALU.add).then_inc(y_ready, 1)

            turn_in(0, 0)
            turns(dve, one)


def attention_stage(nc, k, wqkv):
    with Stage(nc, "att") as st:
        sem, sb, pb = st.sem, st.sb, st.pb
        w_ready, linked, normed, flipped, turned, q_summed, k_summed, v_summed, qk_ready, v_ready = map(
            sem, ("w_ready", "linked", "normed", "flipped", "turned", "q_summed", "k_summed", "v_summed", "qk_ready", "v_ready"))
        scored, topped, exped, p_flipped, p_turned, summed, added, holed, cleared = map(
            sem, ("scored", "topped", "exped", "p_flipped", "p_turned", "summed", "added", "holed", "cleared"))
        W = sb("W", [P, 3, P])
        xn = sb("xn", [P, 4, D])
        xnT = sb("xnT", [P, SEQ])
        QT, KT = sb("QT", [P, 2, SEQ]), sb("KT", [P, 2, SEQ])
        V = sb("V", [P, 2, 4, D])
        hole, S, E, PT = (sb(n, [P, 2, SEQ]) for n in ("hole", "S", "E", "PT"))
        top, ntop, total, inv = (sb(n, [P, 2]) for n in ("top", "ntop", "total", "inv"))
        zeros = sb("zeros", [P, BLOCK])
        psT = pb("psT", [P, SEQ])
        psQ, psK = pb("psQ", [P, SEQ]), pb("psK", [P, SEQ])
        psS = pb("psS", [P, 2, SEQ])
        psE = pb("psE", [P, SEQ])
        psO = pb("psO", [P, D])
        psR = pb("psR", [P, SEQ])
        G = Gather(st, k)
        N = Norm(st, k, "n")
        R = Router(st, k, True, lambda b: psT[:, :], lambda b: psR[:, 0:4 * EXPERTS], lambda b: psR[:, 256:])
        block = st.block()
        ST = SEQ_TILES

        @block.sync
        def _(sp):
            sp.dma_start(W[:, :, :], wqkv).then_inc(w_ready, 16)
            R.sp_pads(nc, sp, zeros, cleared)

        @block.gpsimd
        def _(pool):
            R.pool_start(pool)
            G.pool_start(pool)
            G.pool(pool, 0, 0)
            G.pool(pool, 1, 1)

            def body(s, b, turn, first, last):
                if not last:
                    G.pool(pool, s + 2, b)
                if not first:
                    R.pool(pool, s - 1, 1 - b)
            sequences(pool, body)
            R.pool(pool, BATCH - 1, 1)
            for i in range(8):
                pool.wait_ge(G.gathered[i], (BATCH // 2 + 1) * 16)

        @block.tensor
        def _(pe):
            pe.wait_ge(w_ready, 16)

            def project(s):
                pe.wait_ge(normed, s + 1)
                for j in range(ST):
                    ins = nc.tensor.transpose(psT[:, j * P:(j + 1) * P], xn[:, j, :], k.ident[:, :])
                ins.then_inc(flipped, 1)
                pe.wait_ge(turned, s + 1)
                nc.tensor.matmul(psQ[:, :], W[:, 0, :], xnT[:, :], start=True, stop=True).then_inc(q_summed, 1)
                nc.tensor.matmul(psK[:, :], W[:, 1, :], xnT[:, :], start=True, stop=True).then_inc(k_summed, 1)
                for j in range(ST):
                    ins = nc.tensor.matmul(psT[:, j * P:(j + 1) * P], xnT[:, j * P:(j + 1) * P], W[:, 2, :], start=True, stop=True)
                ins.then_inc(v_summed, 1)

            def body(s, b, turn, first, last):
                def scores(i):
                    n = (i + 1) * P
                    if i > 0:
                        nc.tensor.matmul(psS[:, i % 2, 0:i * P], QT[:, b, i * P:n], KT[:, b, 0:i * P], start=True, stop=True)
                    nc.tensor.matmul(psS[:, i % 2, i * P:n], QT[:, b, i * P:n], KT[:, b, i * P:n], start=True, stop=False)
                    nc.tensor.matmul(psS[:, i % 2, i * P:n], k.ident_bf[:, :], k.causal[:, :], start=False, stop=True).then_inc(scored, 1)

                pe.wait_ge(qk_ready, s * 2 + 2)
                scores(0)
                for i in range(ST):
                    if i + 1 < ST:
                        scores(i + 1)
                    pe.wait_ge(exped, s * ST + i + 1)
                    for j in range(i + 1):
                        ins = nc.tensor.transpose(psE[:, j * P:(j + 1) * P], E[:, i % 2, j * P:(j + 1) * P], k.ident[:, :])
                    ins.then_inc(p_flipped, 1)
                    pe.wait_ge(p_turned, s * ST + i + 1)
                    if i == 0:
                        pe.wait_ge(v_ready, s + 1)
                    if not (i == 0 and first):
                        pe.wait_ge(added, s * ST + i)
                    for j in range(i + 1):
                        ins = nc.tensor.matmul(psO[:, :], PT[:, i % 2, j * P:(j + 1) * P], V[:, b, j, :], start=(j == 0), stop=(j == i))
                    ins.then_inc(summed, 1)
                    if i == 1 and not first:
                        R.pe_1a(nc, pe, s - 1, 1 - b)
                    if i == 2 and not first:
                        R.pe_1b(nc, pe, s - 1, 1 - b)
                    if i == 2 and not last:
                        project(s + 1)
                    if i == 3 and not first:
                        R.pe_2(nc, pe, s - 1, 1 - b)
            project(0)
            sequences(pe, body)
            R.pe_1(nc, pe, BATCH - 1, 1)
            R.pe_2(nc, pe, BATCH - 1, 1)

        @block.scalar
        def _(act):
            act.preload_act_table_set("natural_log_exp_and_others")
            def turn(s):
                act.wait_ge(flipped, s + 1)
                nc.scalar.activation(xnT[:, :], psT[:, :], ACT.Copy).then_inc(turned, 1)

            def projections(s, b):
                act.wait_ge(q_summed, s + 1)
                nc.scalar.activation(QT[:, b, :], psQ[:, :], ACT.Copy).then_inc(qk_ready, 1)
                act.wait_ge(k_summed, s + 1)
                nc.scalar.activation(KT[:, b, :], psK[:, :], ACT.Copy).then_inc(qk_ready, 1)
                act.wait_ge(v_summed, s + 1)
                nc.scalar.activation(V[:, b, :, :], psT[:, :].rearrange("p (a d) -> p a d", a=4), ACT.Copy).then_inc(v_ready, 1)

            def body(s, b, _, first, last):
                for i in range(ST):
                    n = (i + 1) * P
                    act.wait_ge(topped, s * ST + i + 1)
                    nc.scalar.activation(E[:, i % 2, 0:n], S[:, i % 2, 0:n], ACT.Exp, bias=ntop[:, i % 2:i % 2 + 1], scale=SCALE,
                                         accum_out=total[:, i % 2:i % 2 + 1]).then_inc(exped, 1)
                    if i == 3:
                        if not first:
                            R.act_2(nc, act, s - 1)
                        if not last:
                            projections(s + 1, 1 - b)
                    act.wait_ge(p_flipped, s * ST + i + 1)
                    nc.scalar.activation(PT[:, i % 2, 0:n], psE[:, 0:n], ACT.Copy).then_inc(p_turned, 1)
                    if i == 0 and not first:
                        R.norm.act_root(nc, act, s - 1)
                    if i == 1:
                        if not last:
                            N.act_root(nc, act, s + 1)
                        if not first:
                            R.act_1(nc, act, s - 1, 1 - b)
                    if i == 2 and not last:
                        turn(s + 1)
            N.act_root(nc, act, 0)
            turn(0)
            projections(0, 0)
            sequences(act, body)
            R.norm.act_root(nc, act, BATCH - 1)
            R.act_1(nc, act, BATCH - 1, 1)
            R.act_2(nc, act, BATCH - 1)

        @block.vector
        def _(dve):
            chain = Chain(dve, linked)
            nc.vector.memset(zeros[:, :], 0.0).then_inc(cleared, 1)
            chain(R.dve_start(nc))
            for b in range(2):
                G.dve_ask(nc, b, b)
            G.dve(nc, dve, chain, 0, 0, 0)
            N.dve_stats(nc, chain, 0)
            N.dve_finish(nc, dve, chain, 0)
            N.dve_apply(nc, xn, 0).then_inc(normed, 1)

            def body(s, b, turn, first, last):
                def mask(i):
                    n, h = (i + 1) * P, i % 2
                    dve.wait_ge(scored, s * ST + i + 1)
                    chain(nc.vector.tensor_scalar(hole[:, h, 0:n], psS[:, h, 0:n], 0.0, NEG, ALU.is_equal, ALU.mult))
                    dve.sem_inc(holed, 1)
                    chain(nc.vector.tensor_tensor_reduce(out=S[:, h, 0:n], in0=psS[:, h, 0:n], in1=hole[:, h, 0:n], scale=1.0, scalar=3.0 * NEG,
                                                         op0=ALU.add, op1=ALU.max, accum_out=top[:, h:h + 1]))
                    nc.vector.tensor_scalar(ntop[:, h:h + 1], top[:, h:h + 1], -SCALE, None, ALU.mult).then_inc(topped, 1)

                def finish(i):
                    t, h = s * ST + i, i % 2
                    dve.wait_ge(exped, s * ST + i + 1)
                    chain(nc.vector.reciprocal(inv[:, h:h + 1], total[:, h:h + 1]))
                    dve.wait_ge(summed, s * ST + i + 1)
                    nc.vector.scalar_tensor_tensor(out=rows_of(k.X, t), in0=psO[:, :], scalar=inv[:, h:h + 1], in1=rows_of(k.X, t),
                                                   op0=ALU.mult, op1=ALU.add).then_inc(added, 1)

                mask(0)
                if not first:
                    dve.wait_ge(added, s * ST)
                    R.norm.dve_stats(nc, chain, s - 1)
                mask(1)
                if not last:
                    G.dve(nc, dve, chain, s + 1, 1 - b, turn + b)
                    N.dve_stats(nc, chain, s + 1)
                finish(0)
                if not first:
                    R.dve_1(nc, dve, chain, s - 1, 1 - b, turn - 1 + b)
                mask(2)
                if not last:
                    N.dve_finish(nc, dve, chain, s + 1)
                    N.dve_apply(nc, xn, s + 1).then_inc(normed, 1)
                finish(1)
                if not first:
                    R.dve_2a(nc, dve, chain, s - 1, 1 - b)
                mask(3)
                finish(2)
                if not first:
                    R.dve_2b(nc, dve, chain, s - 1, 1 - b)
                finish(3)
                if not first:
                    R.dve_2c(nc, dve, chain, s - 1, 1 - b)
            sequences(dve, body, chain, 2 * (3 * ST + 2 + 4 + 3 + 4 + sum(R.links())))
            s, b = BATCH - 1, 1
            dve.wait_ge(added, BATCH * ST)
            R.norm.dve_stats(nc, chain, s)
            R.dve_1(nc, dve, chain, s, b, s // 2)
            R.dve_2a(nc, dve, chain, s, b)
            R.dve_2b(nc, dve, chain, s, b)
            R.dve_2c(nc, dve, chain, s, b)
            R.dve_tables(nc, dve, chain, st)


CONV_STEPS = {1: ((0, (0, 1)),), 2: ((0, (2, 3)),), 3: ((1, (0, 1, 2)),), 4: ((1, (3,)), (2, (0, 1))), 5: ((2, (2, 3)), (3, (0,))),
              6: ((3, (1, 2, 3)),), 7: ((4, (0,)), (5, (0,)))}
EMPTY_STEPS = {2: (0,), 4: (1,), 5: (2,), 7: (3,), 8: (4, 5)}


def scan_stage(nc, k, w):
    with Stage(nc, "ssm") as st:
        sem, sb, pb = st.sem, st.sb, st.pb
        Win = sb("Win", [P, 2 * INNER])
        Wtap = sb("Wtap", [P, 2, TAPS, INNER])
        Wx = sb("Wx", [P, DT, RANK + 3 * 32])
        Wdt = sb("Wdt", [RANK, INNER])
        Wout = sb("Wout", [P, DT, D])
        col = sb("col", [P, DT, 4 + STATES])
        gates, gmax = sb("gates", [P, 2]), sb("gmax", [P, 1])
        A = sb("A", [P, DT, STATES])
        xn = sb("xn", [P, 4, D])
        hT = sb("hT", [P, PAD + SEQ])
        pre = sb("pre", [P, 2 * DT, SEQ])
        absv, soft = pre[:, 0:DT, :], pre[:, DT:, :]
        zs, xc, delta, ux = (sb(n, [P, 2, DT, SEQ]) for n in ("zs", "xc", "delta", "ux"))
        low = sb("low", [RANK, SEQ])
        bc = sb("bc", [96, SEQ])
        bc3 = sb("bc3", [96, 2, SEQ], BF16)
        v, rest = sb("v", [P, DT, SEQ]), sb("rest", [P, DT, SEQ])
        RA, RB, RH, RC, RP = 4, 2, 4, 4, 4
        dA, dBx, H, HC = (sb(n, [P, r, DT, SEQ]) for n, r in (("dA", RA), ("dBx", RB), ("H", RH), ("HC", RP)))
        Cs = sb("Cs", [P, RC, 1, SEQ])
        zeros = dBx[:, 0, 0, :]
        tap = H[:, 0:2, :, :].rearrange("p a b t -> p (a b t)").rearrange("p (c t e) -> p c t e", c=2, t=TAPS)
        psA, psB = pb("psA", [P, 2, SEQ]), pb("psB", [P, 2, SEQ])
        psC, psR, psY = pb("psC", [P, SEQ]), pb("psR", [P, SEQ]), pb("psY", [P, DT, SEQ])
        G, N = Gather(st, k), Norm(st, k, "n")
        R = Router(st, k, False, lambda b: psR[:, :], lambda b: psR[:, 0:4 * EXPERTS], lambda b: psR[:, 256:])
        (loaded, linked, loose, exp_ready, setup, normed, flipped, turned, fronted, emptied, silu_done, mixed, projected, cut, low_ready, dt_summed, v_ready,
         abs_ready, u_ready, l_ready, delta_ready, ux_ready) = map(sem, "loaded linked loose exp_ready setup normed flipped turned fronted emptied silu_done mixed projected cut low_ready dt_summed v_ready abs_ready u_ready l_ready delta_ready ux_ready".split())
        dA_ready, B_ready, C_ready, Cs_ready, dBx_done, h_ready, hc_ready, y_summed, y_emptied, y_ready, out_summed, added, cleared, z_done = map(
            sem, "dA_ready B_ready C_ready Cs_ready dBx_done h_ready hc_ready y_summed y_emptied y_ready out_summed added cleared z_done".split())
        block = st.block()
        ST, NB = SEQ_TILES, STATES
        positive = lambda count: not isinstance(count, int) or count > 0
        there = lambda s, d: not isinstance(s, int) or 0 <= s + d < BATCH

        def run(eng, main, between, chain=None, links=0):
            turns = (BATCH - 6) // 2

            def body(s, b, turn):
                for n in range(NB):
                    main(s, b, n)
                    between(s, b, turn, n)
            for s in range(3):
                body(s, s % 2, s // 2)
            with eng.Fori(0, turns) as i:
                if chain is not None:
                    chain.turn(i, links, turns)
                body(i * 2 + 3, 1, i + 1)
                body(i * 2 + 4, 0, i + 2)
                if chain is not None:
                    chain.leave()
            for s in range(BATCH - 3, BATCH):
                body(s, s % 2, s // 2)

        @block.sync
        def _(sp):
            for dst, src in ((Win[:, :], w["in"]), (tap, w["taps"].to_broadcast([P, 2, TAPS, INNER])), (Wx[:, :, 0:RANK + 32], w["x"]),
                             (Wdt[:, :], w["dt"]), (Wout[:, :, :], w["out"]), (col[:, :, :], w["col"]),
                             (gates[:, :], w["gates"].rearrange("(a e) -> a e", a=1).to_broadcast([P, 2]))):
                sp.dma_start(dst, src).then_inc(loaded, 16)
            sp.wait_ge(loaded, 7 * 16)
            R.sp_pads(nc, sp, zeros, cleared)

        @block.tensor
        def _(pe):
            def flip(s):
                pe.wait_ge(normed, s + 1)
                if positive(s):
                    pe.wait_ge(v_ready, s)
                for j in range(ST):
                    last = nc.tensor.transpose(psA[:, 1, j * P:(j + 1) * P], xn[:, j, :], k.ident[:, :])
                last.then_inc(flipped, 1)

            def conv(s, g, taps=range(TAPS)):
                c, dt = g // 2, g % 2
                o = psA[:, g % 2, :]
                if 0 in taps:
                    if g == 0:
                        pe.wait_ge(turned, s + 1)
                    if g >= 2:
                        pe.wait_ge(emptied, s * 6 + g - 1)
                if g < 2 * DT:
                    for t in taps:
                        back = (TAPS - 1 - t) * (c + 1)
                        last = nc.tensor.matmul(o, Wtap[:, c, t, dt * P:(dt + 1) * P], hT[:, PAD - back:PAD - back + SEQ], start=(t == 0), stop=(t == TAPS - 1))
                    done = TAPS - 1 in taps
                else:
                    last = nc.tensor.matmul(o, Win[:, INNER + dt * P:INNER + (dt + 1) * P], hT[:, PAD:PAD + SEQ], start=True, stop=True)
                    done = True
                if done:
                    last.then_inc(fronted, 1)

            def project(s, b):
                pe.wait_ge(emptied, s * 6 + 6)
                pe.wait_ge(mixed, s + 1)
                for dt in range(DT):
                    nc.tensor.matmul(psA[0:RANK, 0, :], Wx[:, dt, 0:RANK], xc[:, b, dt, :], start=(dt == 0), stop=(dt == DT - 1))
                for dt in range(DT):
                    last = nc.tensor.matmul(psA[0:96, 1, :], Wx[:, dt, RANK:RANK + 96], xc[:, b, dt, :], start=(dt == 0), stop=(dt == DT - 1))
                last.then_inc(projected, 1)

            def steps(s):
                pe.wait_ge(low_ready, s + 1)
                pe.wait_ge(cut, s + 1)
                for dt in range(DT):
                    last = nc.tensor.matmul(psA[:, dt, :], Wdt[:, dt * P:(dt + 1) * P], low[:, :], start=True, stop=True)
                last.then_inc(dt_summed, 1)

            def out(s):
                pe.wait_ge(y_ready, s + 1)
                for j in range(ST):
                    for dt in range(DT):
                        last = nc.tensor.matmul(psR[:, j * P:(j + 1) * P], v[:, dt, j * P:(j + 1) * P], Wout[:, dt, :], start=(dt == 0), stop=(dt == DT - 1))
                last.then_inc(out_summed, 1)

            def spread_B(s, b, n):
                if positive(s * NB + n - 1):
                    pe.wait_ge(dBx_done, s * NB + n - 1)
                nc.tensor.matmul(psB[:, n % 2, :], k.pick[:, n, :], bc3[:, b, :], start=True, stop=True).then_inc(B_ready, 1)

            def spread_C(s, b, n):
                if positive(s * NB + n):
                    pe.wait_ge(Cs_ready, s * NB + n)
                nc.tensor.matmul(psC[:, :], k.pick[:, STATES + n, :], bc3[:, b, :], start=True, stop=True).then_inc(C_ready, 1)

            def total(s, n):
                pe.wait_ge(hc_ready, s * NB + n + 1)
                if n == 0 and positive(s):
                    pe.wait_ge(y_emptied, s)
                for dt in range(DT):
                    last = nc.tensor.matmul(psY[:, dt, :], k.ident[:, :], HC[:, n % RP, dt, :], start=(n == 0), stop=(n == NB - 1))
                last.then_inc(y_summed, 1)

            def main(s, b, n):
                if n == 0 and there(s, -1):
                    total(s - 1, NB - 2)
                    total(s - 1, NB - 1)
                if n >= 2:
                    total(s, n - 2)
                if n + 2 < NB:
                    spread_B(s, b, n + 2)
                elif there(s, 1):
                    spread_B(s + 1, 1 - b, n + 2 - NB)
                if n + 1 < NB:
                    spread_C(s, b, n + 1)
                elif there(s, 1):
                    spread_C(s + 1, 1 - b, 0)

            def between(s, b, turn, n):
                if there(s, -1):
                    if n == 2:
                        out(s - 1)
                    if n == 6:
                        R.pe_1a(nc, pe, s - 1, 1 - b)
                    if n == 8:
                        R.pe_1b(nc, pe, s - 1, 1 - b)
                    if n == 13:
                        R.pe_2(nc, pe, s - 1, 1 - b)
                if there(s, 1):
                    for g, taps in CONV_STEPS.get(n, ()):
                        conv(s + 1, g, taps)
                    if n == 10:
                        project(s + 1, 1 - b)
                    if n == 12:
                        steps(s + 1)
                if there(s, 2) and n == 15:
                    flip(s + 2)

            pe.wait_ge(setup, 1)
            flip(0)
            for g in range(6):
                conv(0, g)
            project(0, 0)
            steps(0)
            flip(1)
            spread_B(0, 0, 0)
            spread_B(0, 0, 1)
            spread_C(0, 0, 0)
            run(pe, main, between)
            for n in range(NB - 2, NB):
                total(BATCH - 1, n)
            out(BATCH - 1)
            R.pe_1a(nc, pe, BATCH - 1, 1)
            R.pe_1b(nc, pe, BATCH - 1, 1)
            R.pe_2(nc, pe, BATCH - 1, 1)

        @block.scalar
        def _(act):
            def to_hT(s):
                act.wait_ge(flipped, s + 1)
                nc.scalar.activation(hT[:, PAD:], psA[:, 1, :], ACT.Copy).then_inc(turned, 1)

            def empty(s, b, g):
                c, dt = g // 2, g % 2
                act.wait_ge(fronted, s * 6 + g + 1)
                if g < 4:
                    nc.scalar.activation(pre[:, g, :], psA[:, g % 2, :], ACT.Identity, bias=col[:, dt, c:c + 1]).then_inc(emptied, 1)
                else:
                    nc.scalar.activation(zs[:, b, dt, :], psA[:, g % 2, :], ACT.Copy).then_inc(emptied, 1)

            def silu(s, b):
                act.preload_act_table_set("silu_and_others")
                act.wait_ge(emptied, s * 6 + 6)
                nc.scalar.activation(pre[:, :, :], pre[:, :, :], ACT.Silu).then_inc(silu_done, 1)
                nc.scalar.activation(zs[:, b, :, :], zs[:, b, :, :], ACT.Silu).then_inc(z_done, 1)
                act.preload_act_table_set("natural_log_exp_and_others")

            def to_low(s):
                act.wait_ge(projected, s + 1)
                nc.scalar.activation(low[:, :], psA[0:RANK, 0, :], ACT.Copy).then_inc(low_ready, 1)

            def soften(s):
                act.wait_ge(dt_summed, s + 1)
                for dt in range(DT):
                    last = nc.scalar.activation(absv[:, dt, :], psA[:, dt, :], ACT.Abs, bias=col[:, dt, 2:3])
                last.then_inc(abs_ready, 1)
                for dt in range(DT):
                    last = nc.scalar.activation(v[:, dt, :], psA[:, dt, :], ACT.Relu, bias=col[:, dt, 2:3])
                last.then_inc(v_ready, 1)
                act.wait_ge(abs_ready, s + 1)
                nc.scalar.activation(soft, absv, ACT.Exp, scale=-1.0).then_inc(u_ready, 1)
                act.preload_act_table_set("natural_log")
                act.wait_ge(u_ready, s + 1)
                nc.scalar.activation(absv, soft, ACT.Ln, bias=1.0).then_inc(l_ready, 1)
                act.preload_act_table_set("natural_log_exp_and_others")

            def decay(s, b, n):
                if n == 0:
                    act.wait_ge(delta_ready, s + 1)
                if positive(s * NB + n - RA + 1):
                    act.wait_ge(h_ready, s * NB + n - RA + 1)
                for dt in range(DT):
                    last = nc.scalar.activation(dA[:, n % RA, dt, 1:], delta[:, b, dt, 1:], ACT.Exp, scale=A[:, dt, n:n + 1])
                last.then_inc(dA_ready, 1)

            def main(s, b, n):
                act.wait_ge(C_ready, s * NB + n + 1)
                if positive(s * NB + n - RC + 1):
                    act.wait_ge(hc_ready, s * NB + n - RC + 1)
                nc.scalar.activation(Cs[:, n % RC, 0, :], psC[:, :], ACT.Copy).then_inc(Cs_ready, 1)
                if n + 1 < NB:
                    decay(s, b, n + 1)
                elif there(s, 1):
                    decay(s + 1, 1 - b, 0)

            def between(s, b, turn, n):
                if there(s, -1):
                    if n == 4:
                        R.norm.act_root(nc, act, s - 1)
                    if n == 7:
                        R.act_1(nc, act, s - 1, 1 - b)
                    if n == 10:
                        R.act_2(nc, act, s - 1)
                if there(s, 1):
                    for g in EMPTY_STEPS.get(n, ()):
                        empty(s + 1, 1 - b, g)
                    if n == 0:
                        to_hT(s + 1)
                    if n == 8:
                        silu(s + 1, 1 - b)
                    if n == 11:
                        to_low(s + 1)
                    if n == 13:
                        soften(s + 1)
                if there(s, 2) and n == 9:
                    N.act_root(nc, act, s + 2)

            act.wait_ge(loaded, 7 * 16)
            nc.scalar.activation(A[:, :, :], col[:, :, 4:], ACT.Exp).then_inc(exp_ready, 1)
            act.wait_ge(loose, 2)
            nc.scalar.activation(gates[:, :], gates[:, :], ACT.Exp).then_inc(exp_ready, 1)
            act.wait_ge(setup, 1)
            N.act_root(nc, act, 0)
            to_hT(0)
            for g in range(6):
                empty(0, 0, g)
            silu(0, 0)
            to_low(0)
            soften(0)
            N.act_root(nc, act, 1)
            decay(0, 0, 0)
            run(act, main, between)
            R.norm.act_root(nc, act, BATCH - 1)
            R.act_1(nc, act, BATCH - 1, 1)
            R.act_2(nc, act, BATCH - 1)

        @block.gpsimd
        def _(pool):
            def main(s, b, n):
                pool.wait_ge(h_ready, s * NB + n + 1)
                pool.wait_ge(Cs_ready, s * NB + n + 1)
                if positive(s * NB + n - RP + 1):
                    pool.wait_ge(y_summed, s * NB + n - RP + 1)
                nc.gpsimd.tensor_tensor(HC[:, n % RP, :, :], H[:, n % RH, :, :], Cs[:, n % RC, :, :].to_broadcast([P, DT, SEQ]), ALU.mult).then_inc(hc_ready, 1)

            def between(s, b, turn, n):
                if n < 8 and there(s, -2):
                    R.pool_one(pool, s - 2, b, n)
                if n >= 8 and there(s, 3):
                    G.pool_one(pool, s + 3, 1 - b, n - 8)

            R.pool_start(pool)
            G.pool_start(pool)
            for s in range(3):
                G.pool(pool, s, s % 2)
            run(pool, main, between)
            R.pool(pool, BATCH - 2, 0)
            R.pool(pool, BATCH - 1, 1)

        @block.vector
        def _(dve):
            chain = Chain(dve, linked)

            def stats(s, b, turn):
                G.dve(nc, dve, chain, s, b, turn)
                N.dve_stats(nc, chain, s)

            def normalize(s):
                N.dve_finish(nc, dve, chain, s)
                N.dve_apply(nc, xn, s).then_inc(normed, 1)

            def mix(s, b):
                dve.wait_ge(silu_done, s + 1)
                chain(nc.vector.tensor_scalar(xc[:, b, :, :], pre[:, 0:2, :], gates[:, 0:1], None, ALU.mult))
                nc.vector.scalar_tensor_tensor(out=xc[:, b, :, :], in0=pre[:, 2:4, :], scalar=gates[:, 1:2], in1=xc[:, b, :, :],
                                               op0=ALU.mult, op1=ALU.add).then_inc(mixed, 1)

            def cut_rows(s, b):
                dve.wait_ge(projected, s + 1)
                c3 = bc3[:, b, :]
                chain(nc.vector.tensor_copy(c3, psA[0:96, 1, :]))
                chain(nc.vector.tensor_tensor(bc[0:64, :], psA[0:64, 1, :], bc3[0:64, b, :], ALU.subtract))
                chain(nc.vector.tensor_copy(bc3[0:64, b, :], bc[0:64, :]))
                chain(nc.vector.tensor_tensor(bc[0:32, :], bc[0:32, :], bc3[0:32, b, :], ALU.subtract))
                nc.vector.tensor_copy(bc3[0:32, b, :], bc[0:32, :]).then_inc(cut, 1)

            def step_sizes_1(s, b):
                dve.wait_ge(u_ready, s + 1)
                chain(nc.vector.tensor_scalar(rest[:, :, :], soft, 1.0, None, ALU.add))
                chain(nc.vector.scalar_tensor_tensor(out=rest[:, :, :], in0=rest[:, :, :], scalar=-1.0, in1=soft, op0=ALU.add, op1=ALU.subtract))

            def step_sizes_2(s, b):
                dve.wait_ge(l_ready, s + 1)
                chain(nc.vector.tensor_tensor(rest[:, :, :], absv, rest[:, :, :], ALU.subtract))
                nc.vector.tensor_tensor(delta[:, b, :, :], rest[:, :, :], v[:, :, :], ALU.add).then_inc(delta_ready, 1)
                dve.wait_ge(delta_ready, s + 1)
                nc.vector.tensor_tensor(ux[:, b, :, :], delta[:, b, :, :], xc[:, b, :, :], ALU.mult).then_inc(ux_ready, 1)

            def gated(s, b):
                dve.wait_ge(y_summed, s * NB + NB)
                for dt in range(DT):
                    last = nc.vector.scalar_tensor_tensor(out=v[:, dt, :], in0=xc[:, b, dt, :], scalar=col[:, dt, 3:4], in1=psY[:, dt, :], op0=ALU.mult, op1=ALU.add)
                last.then_inc(y_emptied, 1)
                dve.wait_ge(y_emptied, s + 1)
                dve.wait_ge(z_done, s + 1)
                nc.vector.tensor_tensor(v[:, :, :], v[:, :, :], zs[:, b, :, :], ALU.mult).then_inc(y_ready, 1)

            def add(s):
                dve.wait_ge(out_summed, s + 1)
                four = k.X[:, bass.ds(s * ST, ST), :]
                nc.vector.tensor_tensor(four, four, psR[:, :].rearrange("p (a d) -> p a d", a=ST), ALU.add).then_inc(added, 1)

            def main(s, b, n):
                if n == 0:
                    dve.wait_ge(ux_ready, s + 1)
                dve.wait_ge(B_ready, s * NB + n + 1)
                nc.vector.tensor_tensor(dBx[:, n % RB, :, :], ux[:, b, :, :], psB[:, n % 2:n % 2 + 1, :].to_broadcast([P, DT, SEQ]), ALU.mult).then_inc(dBx_done, 1)
                dve.wait_ge(dBx_done, s * NB + n + 1)
                dve.wait_ge(dA_ready, s * NB + n + 1)
                if positive(s * NB + n - RH + 1):
                    dve.wait_ge(hc_ready, s * NB + n - RH + 1)
                flat = lambda v, r: v[:, n % r, :, :].rearrange("p a t -> p (a t)")
                nc.vector.tensor_tensor_scan(flat(H, RH), flat(dA, RA), flat(dBx, RB), 0.0, ALU.mult, ALU.add).then_inc(h_ready, 1)

            def between(s, b, turn, n):
                if there(s, -1):
                    if n == 1:
                        gated(s - 1, 1 - b)
                    if n == 3:
                        add(s - 1)
                        dve.wait_ge(added, s)
                        R.norm.dve_stats(nc, chain, s - 1)
                    if n == 5:
                        R.dve_1(nc, dve, chain, s - 1, 1 - b, turn - 1 + b)
                    if n == 9:
                        R.dve_2a(nc, dve, chain, s - 1, 1 - b)
                    if n == 12:
                        R.dve_2b(nc, dve, chain, s - 1, 1 - b)
                    if n == 14:
                        R.dve_2c(nc, dve, chain, s - 1, 1 - b)
                if there(s, 1):
                    if n == 9:
                        mix(s + 1, 1 - b)
                    if n == 11:
                        cut_rows(s + 1, 1 - b)
                    if n == 14:
                        step_sizes_1(s + 1, 1 - b)
                    if n == 15:
                        step_sizes_2(s + 1, 1 - b)
                if there(s, 2):
                    if n == 7:
                        stats(s + 2, b, turn + 1)
                    if n == 10:
                        normalize(s + 2)

            dve.wait_ge(loaded, 7 * 16)
            nc.vector.tensor_reduce(gmax[:, :], gates[:, :], AX.X, ALU.max).then_inc(loose, 1)
            dve.wait_ge(loose, 1)
            nc.vector.tensor_scalar(gates[:, :], gates[:, :], gmax[:, :], None, ALU.subtract).then_inc(loose, 1)
            dve.wait_ge(exp_ready, 2)
            chain(nc.vector.tensor_reduce(gmax[:, :], gates[:, :], AX.X, ALU.add))
            chain(nc.vector.reciprocal(gmax[:, :], gmax[:, :]))
            chain(nc.vector.tensor_scalar(gates[:, :], gates[:, :], gmax[:, :], None, ALU.mult))
            nc.vector.tensor_scalar(A[:, :, :], A[:, :, :], -1.0, None, ALU.mult)
            for r in range(1, 3):
                chain(nc.vector.tensor_copy(Wx[:, :, RANK + 32 * r:RANK + 32 * r + 32], Wx[:, :, RANK:RANK + 32]))
            for c in range(2):
                for t in range(TAPS):
                    chain(nc.vector.tensor_tensor(Wtap[:, c, t, :], Win[:, 0:INNER], tap[:, c, t, :], ALU.mult))
            nc.vector.memset(hT[:, 0:PAD], 0.0)
            for r in range(RA):
                nc.vector.memset(dA[:, r, :, 0:1], 0.0)
            R.dve_start(nc).then_inc(setup, 1)
            dve.wait_ge(setup, 1)
            for b in range(2):
                G.dve_ask(nc, b, b)
            stats(0, 0, 0)
            normalize(0)
            mix(0, 0)
            cut_rows(0, 0)
            step_sizes_1(0, 0)
            step_sizes_2(0, 0)
            stats(1, 1, 0)
            normalize(1)
            links = (2 + 4) + 3 + 4 + sum(R.links()) + 1 + 4 + 3
            run(dve, main, between, chain, 2 * links)
            s, b = BATCH - 1, 1
            gated(s, b)
            add(s)
            dve.wait_ge(added, BATCH)
            nc.vector.memset(zeros, 0.0).then_inc(cleared, 1)
            R.norm.dve_stats(nc, chain, s)
            R.dve_1(nc, dve, chain, s, b, s // 2)
            R.dve_2a(nc, dve, chain, s, b)
            R.dve_2b(nc, dve, chain, s, b)
            R.dve_2c(nc, dve, chain, s, b)
            R.dve_tables(nc, dve, chain, st)


def macaron_kernel(nc, x, consts, l0_pack, l1_pack, l0_b2, l1_b2, wqkv, l0_bg, l0_wg, l1_wg, gamma, beta, w_in, taps, w_x, w_dt, w_out, col, conv_gates, out):
    k = Core()
    with ExitStack() as ctx:
        sb = lambda n, s, t=F32: ctx.enter_context(nc.sbuf_tensor(n, s, t))
        k.X = sb("X", [P, TILES, D])
        k.ident = sb("ident", [P, P])
        k.ident_bf = sb("ident_bf", [P, P], BF16)
        k.before = sb("before", [P, P], BF16)
        k.causal = sb("causal", [P, P], BF16)
        k.ones = sb("ones", [P, P], BF16)
        k.pick = sb("pick", [96, 2 * STATES, P], BF16)
        k.small = sb("small", [P, SMALL])
        k.bg = sb("bg", [P, EXPERTS])
        k.gate_w = sb("gate_w", [P, 2, EXPERTS])
        k.gamma, k.beta = sb("gamma", [P, 1]), sb("beta", [P, 1])
        k.gate = sb("gate", [P, TOPK, TILES])
        k.hot = sb("hot", [P, TILES, TOPK * EXPERTS])
        k.row = sb("row", [P, TILES, TOPK])
        k.idx = sb("idx", [P, TILES + 4 * SEQ_TILES, TOPK], I32)
        k.limit = sb("limit", [P, TOPK, EXPERTS])
        k.shift = sb("shift", [P, EXPERTS])
        k.pad_row = sb("pad_row", [P, EXPERTS], I32)
        k.block_row = sb("block_row", [P, NBLK], I32)
        k.owner = sb("owner", [P, NBLK], I32)
        k.xslots = nc.dram_tensor("xslots", [DUMP + BLOCK, D], F32, kind="Internal").ap()
        k.yslots = nc.dram_tensor("yslots", [TRASH + 1, D], F32, kind="Internal").ap()

        load_stage(nc, k, x, consts, l0_bg, (l0_wg, l1_wg), gamma, beta)
        plain_stage(nc, k, "to_a", False, True)
        blocks_stage(nc, k, "a", l0_pack, l0_b2, ACT.Gelu_apprx_tanh)
        attention_stage(nc, k, wqkv)
        blocks_stage(nc, k, "b", l0_pack, l0_b2, ACT.Gelu_apprx_tanh)
        plain_stage(nc, k, "to_c", True, False)
        blocks_stage(nc, k, "c", l1_pack, l1_b2, ACT.Gelu, affine=True)
        scan_stage(nc, k, {"in": w_in, "taps": taps, "x": w_x, "dt": w_dt, "out": w_out, "col": col, "gates": conv_gates})
        blocks_stage(nc, k, "d", l1_pack, l1_b2, ACT.Gelu, affine=True)
        plain_stage(nc, k, "end", True, None, out)


def kernel(**inputs):
    import numpy as np
    import concourse.bacc as bacc
    from concourse.bass_utils import run_bass_kernel_spmd as run

    a = {n: np.asarray(v) for n, v in inputs.items()}

    def pack(w1, b1, w2):
        return np.concatenate([w1, w2.reshape(EXPERTS, FT, P, D).transpose(0, 2, 1, 3).reshape(EXPERTS, P, FT * D),
                               b1.reshape(EXPERTS, FT, P).transpose(0, 2, 1)], axis=2)

    r, c = np.arange(P)[:, None], np.arange(P)[None, :]
    consts = np.zeros((P, 36 * P + SMALL), np.float32)
    consts[:, 0:P] = r == c
    consts[:, P:2 * P] = r < c
    consts[:, 2 * P:3 * P] = np.where(c > r, NEG, 0.0)
    consts[:, 3 * P:4 * P] = r == c
    for n in range(32):
        consts[:96, (4 + n) * P:(5 + n) * P] = (np.arange(96) % 32 == n)[:, None]
    e = np.arange(EXPERTS)
    middle = e * REGION + TOKENS
    consts[:, 36 * P:] = np.concatenate([EXPERTS - e, np.repeat([-1, 1], EXPERTS), middle - 1, middle, middle, e, np.arange(NBLK)])
    two = lambda v: v.reshape(DT, P, -1).transpose(1, 0, 2)
    rows = lambda n: a[f"L1_attn_{n}"].reshape(INNER, -1)
    arrays = {
        "x": a["L0_attn_x"].reshape(TOKENS, D),
        "consts": consts,
        "l0_pack": pack(a["L0_ffn_W1"], a["L0_ffn_b1"], a["L0_ffn_W2"]),
        "l1_pack": pack(a["L1_ffn_w1"], a["L1_ffn_b1"], a["L1_ffn_w2"]),
        "l0_b2": a["L0_ffn_b2"], "l1_b2": a["L1_ffn_b2"],
        "wqkv": np.stack([a["L0_attn_WQ"].T, a["L0_attn_WK"].T, a["L0_attn_WV"].T], axis=1),
        "l0_bg": a["L0_ffn_bg"], "l0_wg": a["L0_ffn_Wg"], "l1_wg": a["L1_ffn_gate_w"],
        "gamma": a["L1_ffn_gamma"], "beta": a["L1_ffn_beta"],
        "w_in": a["L1_attn_W_in"].T,
        "taps": np.stack([a["L1_attn_conv_w1"].T, a["L1_attn_conv_w2"].T])[None],
        "w_x": two(a["L1_attn_W_x"].T), "w_dt": a["L1_attn_W_dt"].T, "w_out": two(a["L1_attn_W_out"].T),
        "col": two(np.concatenate([rows("conv_b1"), rows("conv_b2"), rows("b_dt"), rows("D_param"), rows("A_log")], axis=1)),
        "conv_gates": a["L1_attn_conv_gates"],
    }
    nc = bacc.Bacc("TRN2", target_bir_lowering=False, num_devices=1)
    given, args = {}, []
    for name, v in arrays.items():
        v = np.ascontiguousarray(v)
        given[f"in_{name}"] = v
        args.append(nc.dram_tensor(f"in_{name}", v.shape, mybir.dt.from_np(v.dtype), kind="ExternalInput").ap())
    args.append(nc.dram_tensor("out", (TOKENS, D), F32, kind="ExternalOutput").ap())
    macaron_kernel(nc, *args)
    return run(nc, [given], core_ids=[0]).results[0]["out"].reshape(BATCH, SEQ, D)
```
